# Optimizing a Trainium2 kernel written in Bass

```python
import numpy as np
import jax
import jax.numpy as jnp

def _softmax(x, axis=-1):
    return jax.nn.softmax(x, axis=axis)

def _gelu(x):
    return jax.nn.gelu(x, approximate=True)

def _silu(x):
    return jax.nn.silu(x)

def _sigmoid(x):
    return jax.nn.sigmoid(x)

def _layernorm(x, axis=-1, eps=1e-05):
    m = jnp.mean(x, axis=axis, keepdims=True)
    v = jnp.var(x, axis=axis, keepdims=True)
    return (x - m) / jnp.sqrt(v + eps)

def _scatter_add(tgt, idx, src, axis=0):
    return tgt.at[idx].add(src)

def _segment_sum(src, seg, n):
    return jax.ops.segment_sum(src, seg, n)
kernel_name = 'mk_seq_preln_d1_jaxref_r8_eff347'

def setup_inputs(seed: int=0):
    np.random.seed(seed)
    _w = jnp.asarray

    def _L0_attn_setup():
        import jax, jax.numpy as jnp
        import numpy as np
        DM = 128
        NH = 16
        key = jax.random.key(seed)
        ks = jax.random.split(key, 9)
        B, S = (8, 128)
        sc = 1.0 / np.sqrt(DM)
        return {'x': jax.random.normal(ks[0], (B, S, DM), jnp.float32), 'Wq': jax.random.normal(ks[1], (DM, DM), jnp.float32) * sc, 'bq': jax.random.normal(ks[2], (DM,), jnp.float32) * 0.02, 'Wk': jax.random.normal(ks[3], (DM, DM), jnp.float32) * sc, 'bk': jax.random.normal(ks[4], (DM,), jnp.float32) * 0.02, 'Wv': jax.random.normal(ks[5], (DM, DM), jnp.float32) * sc, 'bv': jax.random.normal(ks[6], (DM,), jnp.float32) * 0.02, 'Wo': jax.random.normal(ks[7], (DM, DM), jnp.float32) * sc, 'bo': jax.random.normal(ks[8], (DM,), jnp.float32) * 0.02}
    _L0_attn_in = _L0_attn_setup()

    def _L0_ffn_setup():
        import jax, jax.numpy as jnp
        import numpy as np
        B, T, C = (4, 256, 128)
        H = 128
        E_ATT = 8
        E_MOE = 8
        I = 128
        MIN_ATT = 2
        MIN_MOE = 2
        EPS_LN = 1e-05

        def _normalize(x, axis):
            n = jnp.linalg.norm(x, axis=axis, keepdims=True)
            return x / jnp.maximum(n, 1e-12)

        def _layernorm(x, w, b):
            m = jnp.mean(x, axis=-1, keepdims=True)
            v = jnp.mean(jnp.square(x - m), axis=-1, keepdims=True)
            return (x - m) / jnp.sqrt(v + EPS_LN) * w + b

        def _gating(flat_hs, sim, gates, min_experts):
            logits = _normalize(flat_hs, -1) @ _normalize(sim, 0) - jax.nn.sigmoid(gates)
            gated = jax.nn.relu(logits)
            mask = (gated > 0).astype(gated.dtype)
            inactive = jnp.sum(mask, axis=1) == 0
            _, idx = jax.lax.top_k(logits, min_experts)
            onehot = jnp.sum(jax.nn.one_hot(idx, logits.shape[-1], dtype=gated.dtype), axis=1)
            put = inactive[:, None] & (onehot > 0)
            mask = jnp.where(put, 1.0, mask)
            masked = jnp.where(mask > 0, gated, -jnp.inf)
            return jax.nn.softmax(masked, axis=-1)
        key = jax.random.key(seed)
        ks = jax.random.split(key, 12)
        d = {}
        d['x'] = jax.random.normal(ks[0], (B, T, C), dtype=jnp.float32)
        d['ln1_w'] = jnp.ones((C,), jnp.float32)
        d['ln1_b'] = jnp.zeros((C,), jnp.float32)
        d['ln2_w'] = jnp.ones((C,), jnp.float32)
        d['ln2_b'] = jnp.zeros((C,), jnp.float32)
        d['smha_sim'] = jax.random.normal(ks[1], (C, E_ATT), dtype=jnp.float32)
        d['smha_gates'] = jnp.zeros((E_ATT,), jnp.float32)
        sq = 1.0 / np.sqrt(C + H)
        d['q_proj'] = jax.random.normal(ks[2], (E_ATT, C, H), dtype=jnp.float32) * sq
        d['k_proj'] = jax.random.normal(ks[3], (E_ATT, C, H), dtype=jnp.float32) * sq
        d['v_proj'] = jax.random.normal(ks[4], (E_ATT, C, H), dtype=jnp.float32) * sq
        d['o_proj'] = jax.random.normal(ks[5], (E_ATT, H, C), dtype=jnp.float32) * sq
        d['moe_sim'] = jax.random.normal(ks[6], (C, E_MOE), dtype=jnp.float32)
        d['moe_gates'] = jnp.zeros((E_MOE,), jnp.float32)
        d['w1'] = jax.random.normal(ks[7], (E_MOE, C, I), dtype=jnp.float32) * (1.0 / np.sqrt(C))
        d['w2'] = jax.random.normal(ks[8], (E_MOE, I, C), dtype=jnp.float32) * (1.0 / np.sqrt(I))
        return d
    _L0_ffn_in = _L0_ffn_setup()
    _d = {'L0_attn_x': _L0_attn_in['x'], 'L0_attn_Wq': _L0_attn_in['Wq'], 'L0_attn_bq': _L0_attn_in['bq'], 'L0_attn_Wk': _L0_attn_in['Wk'], 'L0_attn_bk': _L0_attn_in['bk'], 'L0_attn_Wv': _L0_attn_in['Wv'], 'L0_attn_bv': _L0_attn_in['bv'], 'L0_attn_Wo': _L0_attn_in['Wo'], 'L0_attn_bo': _L0_attn_in['bo'], 'L0_ffn_ln1_w': _L0_ffn_in['ln1_w'], 'L0_ffn_ln1_b': _L0_ffn_in['ln1_b'], 'L0_ffn_ln2_w': _L0_ffn_in['ln2_w'], 'L0_ffn_ln2_b': _L0_ffn_in['ln2_b'], 'L0_ffn_smha_sim': _L0_ffn_in['smha_sim'], 'L0_ffn_smha_gates': _L0_ffn_in['smha_gates'], 'L0_ffn_q_proj': _L0_ffn_in['q_proj'], 'L0_ffn_k_proj': _L0_ffn_in['k_proj'], 'L0_ffn_v_proj': _L0_ffn_in['v_proj'], 'L0_ffn_o_proj': _L0_ffn_in['o_proj'], 'L0_ffn_moe_sim': _L0_ffn_in['moe_sim'], 'L0_ffn_moe_gates': _L0_ffn_in['moe_gates'], 'L0_ffn_w1': _L0_ffn_in['w1'], 'L0_ffn_w2': _L0_ffn_in['w2']}
    _x0 = _d['L0_attn_x']
    _d['L0_attn_x'] = jax.random.normal(jax.random.fold_in(jax.random.key(seed), 1), (2, 1024, 128), dtype=_x0.dtype)
    del _x0
    return _d

def reference(L0_attn_x, L0_attn_Wq, L0_attn_bq, L0_attn_Wk, L0_attn_bk, L0_attn_Wv, L0_attn_bv, L0_attn_Wo, L0_attn_bo, L0_ffn_ln1_w, L0_ffn_ln1_b, L0_ffn_ln2_w, L0_ffn_ln2_b, L0_ffn_smha_sim, L0_ffn_smha_gates, L0_ffn_q_proj, L0_ffn_k_proj, L0_ffn_v_proj, L0_ffn_o_proj, L0_ffn_moe_sim, L0_ffn_moe_gates, L0_ffn_w1, L0_ffn_w2):

    def _L0_attn_ref(x, Wq, bq, Wk, bk, Wv, bv, Wo, bo):
        import jax, jax.numpy as jnp
        import numpy as np
        DM = 128
        NH = 16
        B, S, dm = x.shape
        H = NH
        dk = dm // H
        Q = (x @ Wq.T + bq).reshape(B, S, H, dk)
        K = (x @ Wk.T + bk).reshape(B, S, H, dk)
        V = (x @ Wv.T + bv).reshape(B, S, H, dk)
        scores = jnp.einsum('bqhd,bkhd->hbqk', Q, K)
        attn = jax.nn.softmax(scores, axis=1)
        heads = jnp.einsum('hbqk,bkhd->bqhd', attn, V).reshape(B, S, dm)
        return heads @ Wo.T + bo

    def _L0_ffn_ref(x, ln1_w, ln1_b, ln2_w, ln2_b, smha_sim, smha_gates, q_proj, k_proj, v_proj, o_proj, moe_sim, moe_gates, w1, w2):
        import jax, jax.numpy as jnp
        import numpy as np
        B, T, C = (4, 256, 128)
        H = 128
        E_ATT = 8
        E_MOE = 8
        I = 128
        MIN_ATT = 2
        MIN_MOE = 2
        EPS_LN = 1e-05

        def _normalize(x, axis):
            n = jnp.linalg.norm(x, axis=axis, keepdims=True)
            return x / jnp.maximum(n, 1e-12)

        def _layernorm(x, w, b):
            m = jnp.mean(x, axis=-1, keepdims=True)
            v = jnp.mean(jnp.square(x - m), axis=-1, keepdims=True)
            return (x - m) / jnp.sqrt(v + EPS_LN) * w + b

        def _gating(flat_hs, sim, gates, min_experts):
            logits = _normalize(flat_hs, -1) @ _normalize(sim, 0) - jax.nn.sigmoid(gates)
            gated = jax.nn.relu(logits)
            mask = (gated > 0).astype(gated.dtype)
            inactive = jnp.sum(mask, axis=1) == 0
            _, idx = jax.lax.top_k(logits, min_experts)
            onehot = jnp.sum(jax.nn.one_hot(idx, logits.shape[-1], dtype=gated.dtype), axis=1)
            put = inactive[:, None] & (onehot > 0)
            mask = jnp.where(put, 1.0, mask)
            masked = jnp.where(mask > 0, gated, -jnp.inf)
            return jax.nn.softmax(masked, axis=-1)
        b, t, c = x.shape
        n1 = _layernorm(x, ln1_w, ln1_b)
        rw = _gating(n1.reshape(b * t, c), smha_sim, smha_gates, MIN_ATT).reshape(b, t, -1)
        q = jnp.einsum('btc,ech,bte->bth', n1, q_proj, rw)
        k = jnp.einsum('btc,ech,bte->bth', n1, k_proj, rw)
        v = jnp.einsum('btc,ech,bte->bth', n1, v_proj, rw)
        scale = 1.0 / jnp.sqrt(jnp.asarray(q.shape[-1], q.dtype))
        scores = jnp.einsum('bth,bsh->bts', q, k) * scale
        causal = jnp.tril(jnp.ones((t, t), dtype=bool))
        scores = jnp.where(causal, scores, -jnp.inf)
        attn = jnp.einsum('bts,bsh->bth', jax.nn.softmax(scores, axis=-1), v)
        attn_out = jnp.einsum('bth,ehc,bte->btc', attn, o_proj, rw)
        hs = x + attn_out
        n2 = _layernorm(hs, ln2_w, ln2_b)
        rw2 = _gating(n2.reshape(b * t, c), moe_sim, moe_gates, MIN_MOE).reshape(b, t, -1)
        inter = jax.nn.gelu(jnp.einsum('btc,eci->btei', n2, w1), approximate=False)
        moe_out = jnp.einsum('btei,eic,bte->btc', inter, w2, rw2)
        return hs + moe_out
    x = L0_attn_x
    x = x + _L0_attn_ref(_layernorm(x, axis=-1), L0_attn_Wq, L0_attn_bq, L0_attn_Wk, L0_attn_bk, L0_attn_Wv, L0_attn_bv, L0_attn_Wo, L0_attn_bo)
    x = x + _L0_ffn_ref(_layernorm(x, axis=-1), L0_ffn_ln1_w, L0_ffn_ln1_b, L0_ffn_ln2_w, L0_ffn_ln2_b, L0_ffn_smha_sim, L0_ffn_smha_gates, L0_ffn_q_proj, L0_ffn_k_proj, L0_ffn_v_proj, L0_ffn_o_proj, L0_ffn_moe_sim, L0_ffn_moe_gates, L0_ffn_w1, L0_ffn_w2)
    return x

_drawn_inputs = setup_inputs


def setup_inputs(seed=0):
    import zlib

    import numpy as np

    out = dict(_drawn_inputs(seed))
    spreads = {'L0_ffn_ln1_w': (1.0, 0.6),
     'L0_ffn_ln1_b': (0.0, 0.8),
     'L0_ffn_ln2_w': (1.0, 0.6),
     'L0_ffn_ln2_b': (0.0, 0.8),
     'L0_ffn_smha_gates': (0.0, 0.8),
     'L0_ffn_moe_gates': (0.0, 0.8)}
    factors = {'L0_attn_bq': 3.344,
     'L0_attn_bk': 5.106,
     'L0_attn_bo': 8.0,
     'L0_ffn_smha_sim': 8.0,
     'L0_ffn_q_proj': 8.0,
     'L0_ffn_k_proj': 8.0,
     'L0_ffn_v_proj': 8.0,
     'L0_ffn_o_proj': 8.0,
     'L0_ffn_moe_sim': 4.267,
     'L0_ffn_w1': 4.416,
     'L0_ffn_w2': 3.7}
    for name, (base, spread) in spreads.items():
        noise = np.random.default_rng([zlib.crc32(name.encode()), seed]).standard_normal(out[name].shape)
        drawn = base * np.exp(spread * noise) if base else spread * noise
        out[name] = jnp.asarray(drawn.astype(out[name].dtype))
    for name, factor in factors.items():
        out[name] = (out[name] * factor).astype(out[name].dtype)
    return out
```

```python
from contextlib import ExitStack

import concourse.bass as bass
from concourse import mybir

ALU = mybir.AluOpType
ACT = mybir.ActivationFunctionType
AX = mybir.AxisListType
F32 = mybir.dt.float32
F32R = mybir.dt.float32r
BF16 = mybir.dt.bfloat16

P = 128
EPS = 1e-5
MASKED = -3.0e38


def preln_layer(nc, x, Wq, bq, Wk, bk, Wv, bv, Wo, bo, ln1_w, ln1_b, ln2_w, ln2_b,
                smha_sim, smha_gates, q_proj, k_proj, v_proj, o_proj, moe_sim, moe_gates, w1, w2, out):
    NB, S, C = x.shape
    NH = 16
    D = C // NH
    NE = q_proj.shape[0]
    NT = S // P
    HALF = 512
    NHF = S // HALF
    TPH = HALF // P
    assert C == P and NB == 2 and NE * C == 1024 and NT == 8
    GH = 4
    NG = NH // GH
    R = NB * D
    SMAX_SCALE = float(C) ** -0.5
    Q_, K_ = 0, 1
    BLOCKS = [3, 3, 2]
    OP_DMAS = 2 * len(BLOCKS)
    NW = 6
    WQ, WK, WV, WO, W1, W2 = range(NW)

    JOBS = [("wT", 0, 0, "act"), ("xT", 0, 0, "dve"), ("xT", 0, 1, "act")]
    JOBS += [(w, 0, h, "act") for w in "qk" for h in range(NHF)]
    JOBS += [("xT", 1, 0, "dve"), ("xT", 1, 1, "act")]
    JOBS += [(w, 1, h, "act") for w in "qk" for h in range(NHF)]
    JOBS += [("v", b, h, "dve") for b in range(NB) for h in range(NHF)]
    JOBS += [("sums", 0, 0, "dve"), ("rows", 0, 0, "dve")]
    JOB = {j[:3]: n for n, j in enumerate(JOBS)}
    NJ = len(JOBS)

    def emptied(n):
        e = JOBS[n][3]
        return e, sum(1 for j in JOBS[:n + 1] if j[3] == e)

    qk_parts = nc.dram_tensor("qk_parts", [2, 3, P, NB, S], BF16, kind="Internal").ap()

    with ExitStack() as ctx:
        def tensor(name, shape, dt, stack=ctx):
            return stack.enter_context(nc.sbuf_tensor(name, shape, dt))

        def sem(name):
            return ctx.enter_context(nc.semaphore(name))

        ps = ctx.enter_context(nc.psum_tensor("ps", [P, 8, 512], F32))
        psf = ps[:, :, :].rearrange("p a b -> p (a b)")

        ident = tensor("ident", [P, P], F32)
        identb = tensor("identb", [P, P], BF16)
        maskb = tensor("maskb", [P, P], BF16)
        spread = tensor("spread", [P, NE, P], BF16)
        before = tensor("before", [P, NE, NE], F32)
        ones = tensor("ones", [P, P], F32)
        minus_half = tensor("minus_half", [P, 16], F32)
        warm = tensor("warm", [P, 2], F32)
        start = tensor("start", [P, 2], F32)
        bcol = tensor("bcol", [P, 4], F32)
        lncol = tensor("lncol", [P, 4], F32)
        bv_row = tensor("bv_row", [P, P], F32)
        bo_row = tensor("bo_row", [P, P], F32)
        gates = tensor("gates", [P, 2, NE], F32)
        sims = tensor("sims", [P, 2, NE], F32)
        simsq = tensor("simsq", [P, 2 * NE], F32)
        simn2 = tensor("simn2", [P, 2 * NE], F32)
        simrn = tensor("simrn", [P, 2 * NE], F32)
        wnat = tensor("wnat", [P, 4, P], F32)
        wT = tensor("wT", [P, 4, P], F32)
        X = tensor("X", [P, NB * NT, P], F32)
        U = tensor("U", [P, NB * NT, P], F32)
        nT = tensor("nT", [P, NB * S], F32)
        stats = tensor("stats", [P, NB * NT, 6], F32)
        mv = tensor("mv", [P, NB * NT, 2], F32)
        powin = tensor("powin", [P, NB, 2, NT], F32)
        powout = tensor("powout", [P, NB, 2, NT], F32)
        tmp8 = tensor("tmp8", [P, 3, NT], F32)
        sumx = tensor("sumx", [P, NB], F32)
        cvec = tensor("cvec", [P, NB], F32)
        cvecb = tensor("cvecb", [P, NB, P], F32)
        row_add = tensor("row_add", [P, NB, P], F32)
        whi = tensor("whi", [P, NW, NE * C], F32R)
        wlo = tensor("wlo", [P, NW, NE * C], F32R)
        HT = tensor("HT", [P, NB, S], F32)

        early = ExitStack()
        wraw = tensor("wraw", [P, 2, NE * C], F32, early)
        parts = tensor("parts", [P, 2, 3, NB, S], BF16, early)
        q32 = tensor("q32", [P, 2, HALF], F32, early)
        rest = tensor("rest", [P, HALF], F32, early)
        ops = tensor("ops", [P, 2, 2, GH, S], BF16, early)
        VP = tensor("VP", [P, NT, NH, R], F32, early)
        vst = tensor("vst", [P, 2, NT, GH, 32], F32, early)
        tanhs = tensor("tanhs", [P, 4, 2, HALF], F32, early)
        hout = tensor("hout", [P, 2, S], F32, early)
        early.close()
        RP = tensor("RP", [P, NB, NT, 3 * NE], BF16)
        RPT = tensor("RPT", [P, NB, S], BF16)
        SQ = tensor("SQ", [P, NB * S], F32)
        rw = tensor("rw", [P, NB, NT, NE], F32)
        gt = tensor("gt", [P, 6, NT, NE], F32)
        cmp_ = tensor("cmp_", [P, 2, NT, NE, NE], F32)
        g1 = tensor("g1", [P, 6, NT], F32)
        HS = tensor("HS", [P, NB * NT, P], F32)
        sring = tensor("sring", [P, 3, HALF], F32)
        shi = tensor("shi", [P, 3, HALF], F32R)
        slo = tensor("slo", [P, 3, HALF], F32R)
        qT = tensor("qT", [P, NB, S], F32)
        kT = tensor("kT", [P, NB, S], F32)
        vT = tensor("vT", [P, 2, HALF], F32)
        V = tensor("V", [P, NB * NT, P], F32)
        prob = tensor("prob", [P, 2, S], F32)
        probT = tensor("probT", [P, 2, NT, P], F32)
        mx = tensor("mx", [P, 2, NB * NT], F32)
        rowsum = tensor("rowsum", [P, NB * NT], F32)
        rwn = tensor("rwn", [P, NB, NT, NE], F32)
        ahi = tensor("ahi", [P, NB * S], F32R)
        alo = tensor("alo", [P, NB * S], F32R)
        gel = tensor("gel", [P, 2, HALF], F32)
        moeT = vT
        fin = tensor("fin", [P, 2, HALF], F32)

        s_x = [sem(f"x_loaded{b}") for b in range(NB)]
        s_wnat = sem("wnat_loaded")
        s_small = sem("small_loaded")
        s_const = sem("consts_made")
        s_id = sem("ident_made")
        s_pool = sem("pool_step")
        s_dve = sem("dve_step")
        s_powin = sem("pow_inputs")
        s_pow = sem("pow_results")
        s_xn = sem("xn_ready")
        s_job = sem("job_products")
        s_jact = sem("job_emptied_by_act")
        s_jdve = sem("job_emptied_by_dve")
        s_rest = sem("qk_rest_taken")
        s_split = sem("qk_split")
        s_sums = sem("sums_inputs")
        s_cvec = sem("cvec_ready")
        s_gtan = sem("gates_tanh")
        s_qd = sem("parts_in_dram")
        s_ops = [sem(f"ops_loaded{u}") for u in range(2)]
        s_vst = sem("v_staged")
        s_score = sem("scores_ready")
        s_tanh = sem("tanh_done")
        s_pair = sem("tanh_pairs_used")
        s_head = sem("heads_emptied")
        s_ht = [sem(f"heads_moved{u}") for u in range(2)]
        s_wraw = [sem(f"wraw_loaded{u}") for u in range(2)]
        s_wsplit = sem("weights_split")
        s_o1 = sem("out_proj_ready")
        s_x1 = sem("x1_ready")
        s_y = sem("y_ready")
        s_u = sem("u_ready")
        s_uT = sem("uT_ready")
        s_nT = sem("nT_ready")
        s_sq = sem("sq_ready")
        s_log = sem("logits_ready")
        s_gex = sem("gate_exp_in")
        s_gexo = sem("gate_exp_out")
        s_rp = sem("rw_parts")
        s_rpT = sem("rw_partsT")
        s_rpt = sem("rpt_ready")
        s_bc = sem("bcast_ready")
        s_s = sem("scaled_ready")
        s_shi = sem("scaled_hi")
        s_slo = sem("scaled_lo")
        s_mm = sem("qkv_steps")
        s_qk = sem("qk_copied")
        s_vT = sem("vT_copied")
        s_vtr = sem("v_turned")
        s_v = sem("v_copied")
        s_S = sem("S_ready")
        s_nb = sem("negmax_ready")
        s_exp = sem("exp_done")
        s_ptm = sem("probT_made")
        s_pt = sem("probT_copied")
        s_av = sem("av_done")
        s_ahi = sem("attn_hi")
        s_alo = sem("attn_lo")
        s_op = sem("oproj_ready")
        s_acc = sem("oproj_added")
        s_hs = sem("hs_ready")
        s_xh = sem("xh_ready")
        s_n2hi = sem("n2_hi")
        s_n2lo = sem("n2_lo")
        s_int = sem("inter_ready")
        s_gel = sem("gelu_done")
        s_w2 = sem("w2_steps")
        s_moe = sem("moe_copied")
        s_mtr = sem("moe_turned")
        s_fin = sem("fin_ready")
        s_out = [sem(f"out_stored{u}") for u in range(2)]

        SCORES = 3 + NG * NHF * NT * 2
        ring_jobs = []
        for m in range(NB * NHF):
            for e in range(NE):
                ring_jobs.append(("bc", m, e))
                if e == 3 and m:
                    ring_jobs.append(("v", m - 1, 0))
        ring_jobs.append(("v", NB * NHF - 1, 0))
        RING = {j: n for n, j in enumerate(ring_jobs)}

        def scaled_before(n):
            return sum(1 for j in ring_jobs[:n] if j[0] == "bc")

        def v_before(n):
            return n - scaled_before(n)

        ptjobs = []
        for T in range(NB * NT):
            i = T % NT
            for k0 in range(0, i + 1, 4):
                ptjobs.append((T, k0, min(4, i + 1 - k0)))

        def pt_until(T):
            return sum(1 for j in ptjobs if j[0] <= T)

        def toks(b, hf):
            return slice(b * S + hf * HALF, b * S + (hf + 1) * HALF)

        block = ctx.enter_context(nc.Block())

        @block.sync
        def _(sp):
            xv = x.rearrange("b (i p) c -> b p i c", p=P)
            for b in range(NB):
                sp.dma_start(X[:, b * NT:b * NT + NT // 2, :], xv[b, :, 0:NT // 2]).then_inc(s_x[b], 16)
                sp.dma_start(X[:, b * NT + NT // 2:(b + 1) * NT, :], xv[b, :, NT // 2:]).then_inc(s_x[b], 16)
                if b == 0:
                    for n, w in enumerate((Wq, Wk, Wv, Wo)):
                        sp.dma_start(wnat[:, n, :], w).then_inc(s_wnat, 16)

            def load_weight(n):
                if n >= 2:
                    sp.wait_ge(s_wsplit, n - 1)
                src = (q_proj, k_proj, v_proj, o_proj, w1, w2)[n]
                sp.dma_start(wraw[:, n % 2, :].rearrange("p (e n) -> p e n", e=NE),
                             src.rearrange("e c n -> c e n")).then_inc(s_wraw[n % 2], 16)

            load_weight(0)
            load_weight(1)
            sp.wait_ge(s_split, 4 * NB)
            for g in range(NG):
                rows = slice(32 * g, 32 * g + 32)
                for t in (Q_, K_):
                    sp.dma_start(qk_parts[t, :, rows].rearrange("a r b s -> r a (b s)"),
                                 parts[rows, t].rearrange("r a b s -> r a (b s)")).then_inc(s_qd, 16)

            def load_group(g):
                u = g % 2
                if g >= 2:
                    sp.wait_ge(s_score, 32 * (g - 1))
                for i, nj in enumerate(BLOCKS):
                    r0 = sum(BLOCKS[:i]) * R
                    own = qk_parts[:, :, 32 * g:32 * g + 32].rearrange("t a (h d) b s -> t a h (d b) s", d=D)
                    for t in (Q_, K_):
                        for j in range(nj):
                            src = own[t, i if t == Q_ else j].rearrange("h r s -> r h s")
                            dst = ops[r0 + j * R:r0 + (j + 1) * R, u, t, :, :]
                            sp.dma_start(dst, src).then_inc(s_ops[u], 16)

            sp.wait_ge(s_qd, 2 * 16 * NG)
            load_group(0)
            load_group(1)
            for n in range(2, NW):
                load_weight(n)
            for g in range(NG):
                if g + 2 < NG:
                    load_group(g + 2)
                sp.wait_ge(s_head, 2 + NHF * (g + 1))
                for j in range(GH):
                    for b in range(NB):
                        h = g * GH + j
                        sp.dma_start(HT[D * h:D * h + D, b, :],
                                     hout[32 * j + D * b:32 * j + D * b + D, g % 2, :]).then_inc(s_ht[g % 2], 16)
            ov = out.rearrange("b (i p) c -> b p i c", p=P)
            for m in range(NB * NHF):
                b, hf = divmod(m, NHF)
                sp.wait_ge(s_fin, m + 1)
                sp.dma_start(ov[b, :, hf * TPH:(hf + 1) * TPH, :],
                             fin[:, m % 2, :].rearrange("p (i c) -> p i c", i=TPH)).then_inc(s_out[m % 2], 16)
            for u in range(2):
                sp.wait_ge(s_out[u], 16 * NB * NHF // 2)

        @block.gpsimd
        def _(pool):
            pool.memset(ident[:, :], 0.0).then_inc(s_pool, 1)
            pool.memset(warm[:, :], 0.0).then_inc(s_const, 1)
            pool.memset(minus_half[:, :], -0.5).then_inc(s_pool, 1)
            pool.wait_ge(s_pool, 2)
            pool.affine_select(out=ident[:, :], in_=ident[:, :], compare_op=ALU.not_equal, fill=1.0,
                               base=0, pattern=[[-1, P]], channel_multiplier=1).then_inc(s_id, 1)
            pool.memset(ones[:, :], 1.0).then_inc(s_const, 1)
            pool.memset(start[:, 0:1], 0.0).then_inc(s_pair, 2)
            pool.memset(start[:, 1:2], 0.0).then_inc(s_head, 2)
            pool.memset(before[:, :, :], 1.0).then_inc(s_pool, 1)
            pool.memset(maskb[:, :], 0.0).then_inc(s_pool, 1)
            pool.memset(spread[:, :, :], 0.0).then_inc(s_pool, 1)
            pool.memset(identb[:, :], 0.0).then_inc(s_pool, 1)
            pool.memset(vst[:, 0, :, :, :], 0.0).then_inc(s_const, 1)
            pool.memset(vst[:, 1, :, :, :], 0.0).then_inc(s_const, 1)

            def power(n, o, i):
                pool.wait_ge(s_powin, n)
                pool.tensor_tensor(o, i, minus_half[:, 0:i.shape[1]], ALU.pow).then_inc(s_pow, 1)

            def flat(t, b):
                return t[:, b].rearrange("p a i -> p (a i)")

            for b in range(NB):
                power(b + 1, powout[:, b, 0, :], powin[:, b, 0, :])
            pool.wait_ge(s_pool, 6)
            pool.affine_select(out=identb[:, :], in_=identb[:, :], compare_op=ALU.not_equal, fill=1.0,
                               base=0, pattern=[[-1, P]], channel_multiplier=1).then_inc(s_const, 1)
            pool.affine_select(out=maskb[:, :], in_=maskb[:, :], compare_op=ALU.is_ge, fill=MASKED,
                               base=0, pattern=[[-1, P]], channel_multiplier=1).then_inc(s_const, 1)
            pool.affine_select(out=before[:, :, :], in_=before[:, :, :], compare_op=ALU.is_gt, fill=0.0,
                               base=0, pattern=[[1, NE], [-1, NE]], channel_multiplier=0).then_inc(s_const, 1)
            for a in range(3):
                if a:
                    pool.wait_ge(s_pool, 6 + a)
                pool.affine_select(out=spread[:, :, :], in_=spread[:, :, :], compare_op=ALU.not_equal, fill=1.0,
                                   base=-NE * a, pattern=[[-1, NE], [0, P]], channel_multiplier=1)\
                    .then_inc(s_pool if a < 2 else s_const, 1)
            power(3, simrn[:, :], simn2[:, :])

            for part in range(2):
                for b in range(NB):
                    if part == 0:
                        power(4 + b, flat(powout, b), flat(powin, b))
                    else:
                        power(8 + b, powout[:, b, 0, :], powin[:, b, 0, :])
                    if part == 0:
                        pool.wait_ge(s_y, b + 1)
                        for i in range(NT):
                            ins = pool.tensor_scalar(HS[:, b * NT + i, :], X[:, b * NT + i, :],
                                                     powout[:, b, 0, i:i + 1], powin[:, b, 1, i:i + 1],
                                                     ALU.mult, ALU.add)
                        ins.then_inc(s_hs, 1)
                for b in range(NB):
                    n = (6 if part == 0 else 10) + b
                    power(n, g1[:, 1, :] if b == 0 else g1[:, 3, :], g1[:, 0, :] if b == 0 else g1[:, 2, :])

        @block.scalar
        def _(act):
            act.dma_start(bcol[:, 0:1], bq.rearrange("(p a) -> p a", a=1)).then_inc(s_small, 16)
            act.dma_start(bcol[:, 1:2], bk.rearrange("(p a) -> p a", a=1)).then_inc(s_small, 16)
            act.dma_start(bcol[:, 2:3], bv.rearrange("(p a) -> p a", a=1)).then_inc(s_small, 16)
            for n, a in enumerate((ln1_w, ln1_b, ln2_w, ln2_b)):
                act.dma_start(lncol[:, n:n + 1], a.rearrange("(p a) -> p a", a=1)).then_inc(s_small, 16)
            for t, a in ((bv_row, bv), (bo_row, bo)):
                act.dma_start(t[:, :], a.rearrange("(a c) -> a c", a=1).to_broadcast([P, P])).then_inc(s_small, 16)
            for n, a in enumerate((smha_gates, moe_gates)):
                act.dma_start(gates[:, n, :], a.rearrange("(a c) -> a c", a=1).to_broadcast([P, NE]))\
                    .then_inc(s_small, 16)
            for n, a in enumerate((smha_sim, moe_sim)):
                act.dma_start(sims[:, n, :], a).then_inc(s_small, 16)
            act.wait_ge(s_const, 1)
            act.activation(warm[:, 1:2], warm[:, 0:1], ACT.Tanh).then_inc(s_tanh, 3)

            nq = 0
            for n, (what, b, h, e) in enumerate(JOBS):
                if e != "act":
                    continue
                act.wait_ge(s_job, n + 1)
                src = ps[:, n % 8, :]
                if what == "wT":
                    act.activation(wT[:, :, :].rearrange("p a b -> p (a b)"), src, ACT.Copy).then_inc(s_jact, 1)
                elif what == "xT":
                    act.activation(nT[:, toks(b, h)], src, ACT.Copy).then_inc(s_jact, 1)
                else:
                    t = Q_ if what == "q" else K_
                    sign = -1.0 if (t == K_ and b == 1) else 1.0
                    bias = bcol[:, 3:4] if sign < 0 else bcol[:, t:t + 1]
                    if nq == 0:
                        act.wait_ge(s_small, 16 * 13)
                    if nq >= 2:
                        act.wait_ge(s_rest, nq - 1)
                    if sign < 0 and h == 0:
                        act.wait_ge(s_sums, 1)
                    act.activation(q32[:, nq % 2, :], src, ACT.Identity, bias=bias, scale=sign)
                    act.activation(parts[:, t, 0, b, h * HALF:(h + 1) * HALF], src, ACT.Identity,
                                   bias=bias, scale=sign).then_inc(s_jact, 1)
                    nq += 1
            act.activation(gates[:, :, :].rearrange("p a b -> p (a b)"),
                           gates[:, :, :].rearrange("p a b -> p (a b)"), ACT.Tanh, scale=0.5).then_inc(s_gtan, 1)

            with act.Fori(0, NG // 2) as gg:
                for i in range(64):
                    act.wait_ge(s_score, 64 * gg + (i + 1))
                    if i % 2 == 0:
                        act.wait_ge(s_pair, 32 * gg + (i // 2 + 1))
                    act.activation(tanhs[:, i % 4, :, :].rearrange("p a b -> p (a b)"),
                                   psf[:, (i % 3) * 1024:(i % 3) * 1024 + 1024],
                                   ACT.Tanh, scale=0.5).then_inc(s_tanh, 1)

            def normed(part, b):
                act.wait_ge(s_uT, 2 * part + b + 1)
                k = 4 + 2 * b
                dst = nT[:, b * S:(b + 1) * S]
                act.activation(dst, psf[:, k * 512:k * 512 + S], ACT.Identity, bias=lncol[:, 2 * part + 1:2 * part + 2],
                               scale=lncol[:, 2 * part:2 * part + 1]).then_inc(s_nT, 1)
                act.wait_ge(s_nT, 2 * part + b + 1)
                act.activation(SQ[:, b * S:(b + 1) * S], dst, ACT.Square).then_inc(s_sq, 1)

            def gate_exp(n, b):
                act.wait_ge(s_gex, n)
                act.activation(gt[:, 3 * b + 2, :, :], gt[:, 3 * b + 2, :, :], ACT.Exp).then_inc(s_gexo, 1)

            for b in range(NB):
                normed(0, b)
            gate_exp(1, 0)

            for m in range(NB * NHF):
                b, hf = divmod(m, NHF)
                for e in range(NE):
                    n = m * NE + e
                    act.wait_ge(s_s, n + 1)
                    if n >= 3:
                        act.wait_ge(s_mm, n - 2)
                    act.activation(shi[:, n % 3, :], sring[:, n % 3, :], ACT.Copy).then_inc(s_shi, 1)
                    if n == 1:
                        gate_exp(2, 1)
                act.wait_ge(s_mm, (m + 1) * NE)
                k = 3 * (m % 2)
                act.activation(qT[:, b, hf * HALF:(hf + 1) * HALF], ps[:, k, :], ACT.Copy)
                act.activation(kT[:, b, hf * HALF:(hf + 1) * HALF], ps[:, k + 1, :], ACT.Copy).then_inc(s_qk, 1)

            def exps(T):
                i = T % NT
                act.wait_ge(s_nb, T + 1)
                if T >= 2:
                    act.wait_ge(s_ptm, pt_until(T - 2))
                act.activation(prob[:, T % 2, 0:(i + 1) * P], psf[:, (T % 2) * 1024:(T % 2) * 1024 + (i + 1) * P],
                               ACT.Exp, bias=mx[:, 1, T:T + 1], scale=SMAX_SCALE,
                               accum_out=rowsum[:, T:T + 1]).then_inc(s_exp, 1)

            def copies(T):
                for n, (T_, k0, nk) in enumerate(ptjobs):
                    if T_ != T:
                        continue
                    act.wait_ge(s_ptm, n + 1)
                    if T >= 2 and k0 == 0:
                        act.wait_ge(s_av, T - 1)
                    act.activation(probT[:, T % 2, k0:k0 + nk, :].rearrange("p a b -> p (a b)"),
                                   ps[:, 4 + n % 2, 0:nk * P], ACT.Copy).then_inc(s_pt, 1)

            def attn_hi(q):
                act.wait_ge(s_av, 4 * q + 4)
                act.activation(ahi[:, q * HALF:(q + 1) * HALF], ps[:, 6 + q % 2, :], ACT.Copy).then_inc(s_ahi, 1)

            exps(0)
            for T in range(NB * NT):
                if T + 1 < NB * NT:
                    exps(T + 1)
                copies(T)
                if T % 4 == 0 and T:
                    attn_hi(T // 4 - 1)
            attn_hi(3)

            for b in range(NB):
                normed(1, b)
                act.activation(ahi[:, b * S:(b + 1) * S], nT[:, b * S:(b + 1) * S], ACT.Copy).then_inc(s_n2hi, 1)
            gate_exp(3, 0)
            gate_exp(4, 1)

            def gelu(n):
                act.wait_ge(s_int, n + 1)
                if n >= 2:
                    act.wait_ge(s_s, 32 + n - 1)
                act.activation(gel[:, n % 2, :], ps[:, n % 2, :], ACT.Gelu).then_inc(s_gel, 1)

            def high(n):
                act.wait_ge(s_s, 32 + n + 1)
                if n >= 3:
                    act.wait_ge(s_w2, n - 2)
                act.activation(shi[:, (32 + n) % 3, :], sring[:, (32 + n) % 3, :], ACT.Copy).then_inc(s_shi, 1)

            NM = NB * NHF * NE
            gelu(0)
            for n in range(NM):
                if n + 1 < NM:
                    gelu(n + 1)
                high(n)

        @block.vector
        def _(dve):
            steps = [0]

            def link(ins):
                steps[0] += 1
                ins.then_inc(s_dve, 1)
                dve.wait_ge(s_dve, steps[0])

            def statistics(src, b):
                for i in range(NT):
                    last = dve.bn_stats(stats[:, b * NT + i, :], src[:, b * NT + i, :])
                link(last)
                for i in range(NT):
                    last = dve.bn_aggr(mv[:, b * NT + i, :], stats[:, b * NT + i, :])
                link(last)
                return mv[:, b * NT:(b + 1) * NT, 0], mv[:, b * NT:(b + 1) * NT, 1]

            for b in range(NB):
                dve.wait_ge(s_x[b], 32)
                m_, v_ = statistics(X, b)
                dve.tensor_scalar(powin[:, b, 0, :], v_, EPS, None, ALU.add).then_inc(s_powin, 1)

            def normalise(b, r, sem_):
                for i in range(NT):
                    last = dve.tensor_scalar(U[:, b * NT + i, :], X[:, b * NT + i, :], mv[:, b * NT + i, 0:1],
                                             r[:, i:i + 1], ALU.subtract, ALU.mult)
                last.then_inc(sem_, 1)

            def empty(n, fn):
                dve.wait_ge(s_job, n + 1)
                fn(ps[:, n % 8, :]).then_inc(s_jdve, 1)

            def split_rest(nq, t, b, h):
                dst = parts[:, t, :, b, h * HALF:(h + 1) * HALF]
                n = JOB[("qk"[t], b, h)]
                dve.wait_ge(s_jact, emptied(n)[1])
                if nq:
                    dve.wait_ge(s_split, nq)
                ins = dve.tensor_tensor(rest[:, :], q32[:, nq % 2, :], dst[:, 0, :], ALU.subtract)
                ins.then_inc(s_rest, 1)
                dve.wait_ge(s_rest, nq + 1)
                link(dve.tensor_copy(dst[:, 1, :], rest[:, :]))
                dve.tensor_tensor(dst[:, 2, :], rest[:, :], dst[:, 1, :], ALU.subtract).then_inc(s_split, 1)

            dve.wait_ge(s_pow, 1)
            normalise(0, powout[:, 0, 0, :], s_xn)
            empty(JOB[("xT", 0, 0)], lambda src: dve.tensor_copy(nT[:, toks(0, 0)], src))
            dve.wait_ge(s_pow, 2)
            normalise(1, powout[:, 1, 0, :], s_xn)
            dve.wait_ge(s_small, 16 * 13)
            dve.tensor_scalar(bcol[:, 3:4], bcol[:, 1:2], -1.0, None, ALU.mult).then_inc(s_sums, 1)
            split_rest(0, Q_, 0, 0)
            split_rest(1, Q_, 0, 1)
            empty(JOB[("xT", 1, 0)], lambda src: dve.tensor_copy(nT[:, toks(1, 0)], src))
            split_rest(2, K_, 0, 0)
            split_rest(3, K_, 0, 1)
            for n, (t, h) in enumerate(((Q_, 0), (Q_, 1), (K_, 0), (K_, 1))):
                split_rest(4 + n, t, 1, h)

            link(dve.tensor_scalar(cvecb[:, 0, :], bv_row[:, :], 0.5, None, ALU.mult))
            link(dve.tensor_scalar(cvecb[:, 1, :], bv_row[:, :], -0.5, None, ALU.mult))
            for b in range(NB):
                for h in range(NHF):
                    n = JOB[("v", b, h)]
                    dve.wait_ge(s_job, n + 1)
                    for k in range(TPH):
                        last = dve.scalar_tensor_tensor(
                            out=VP[:, h * TPH + k, :, b * D:(b + 1) * D],
                            in0=ps[:, n % 8, k * P:(k + 1) * P].rearrange("p (h d) -> p h d", d=D),
                            scalar=0.5 if b == 0 else -0.5,
                            in1=cvecb[:, b, :].rearrange("p (h d) -> p h d", d=D), op0=ALU.mult, op1=ALU.add)
                    last.then_inc(s_jdve, 1)
            jd = emptied(JOB[("v", 1, 1)])[1]
            dve.wait_ge(s_jdve, jd)
            dve.wait_ge(s_const, 4)
            def stage_v(g):
                if g >= 2:
                    dve.wait_ge(s_pair, 2 + NHF * NT * (g - 1))
                dve.tensor_copy(vst[:, g % 2, :, :, 0:R], VP[:, :, g * GH:(g + 1) * GH, :]).then_inc(s_vst, 1)

            stage_v(0)
            stage_v(1)

            link(dve.tensor_tensor(simsq[:, :], sims[:, :, :].rearrange("p a b -> p (a b)"),
                                   sims[:, :, :].rearrange("p a b -> p (a b)"), ALU.mult))
            dve.wait_ge(s_jact, emptied(JOB[("xT", 1, 1)])[1])
            dve.tensor_reduce(sumx[:, :], nT[:, :].rearrange("p (b s) -> p b s", b=NB), AX.X,
                              ALU.add).then_inc(s_sums, 1)
            n = JOB[("sums", 0, 0)]
            dve.wait_ge(s_job, n + 1)
            dve.tensor_scalar(simn2[:, :], ps[:, n % 8, 0:2 * NE], 1e-24, None, ALU.max).then_inc(s_powin, 1)
            dve.tensor_scalar(cvec[:, :], ps[:, n % 8, 2 * NE:2 * NE + NB], 0.5, None, ALU.mult).then_inc(s_jdve, 1)
            dve.wait_ge(s_jdve, emptied(n)[1])
            link(dve.tensor_scalar(tmp8[:, 0, 0:1], bcol[:, 2:3], 0.5 * S, None, ALU.mult))
            link(dve.tensor_tensor(cvec[:, :], cvec[:, :], tmp8[:, 0, 0:1].to_broadcast([P, NB]), ALU.add))
            for b in range(NB):
                last = dve.tensor_scalar(cvecb[:, b, :], ones[:, :], cvec[:, b:b + 1], None, ALU.mult)
            last.then_inc(s_cvec, 1)
            n = JOB[("rows", 0, 0)]
            dve.wait_ge(s_job, n + 1)
            for b in range(NB):
                last = dve.tensor_tensor(row_add[:, b, :], ps[:, n % 8, b * P:(b + 1) * P], bo_row[:, :], ALU.add)
            last.then_inc(s_jdve, 1)
            dve.wait_ge(s_jdve, emptied(n)[1])
            for b in range(NB):
                xb = X[:, b * NT:(b + 1) * NT, :]
                last = dve.tensor_tensor(xb, xb, row_add[:, b:b + 1, :].to_broadcast([P, NT, P]), ALU.add)
            link(last)
            dve.wait_ge(s_gtan, 1)
            link(dve.tensor_scalar(gates[:, :, :], gates[:, :, :], 0.5, 0.5, ALU.mult, ALU.add))
            dve.wait_ge(s_pow, 3)
            link(dve.tensor_tensor(sims[:, :, :].rearrange("p a b -> p (a b)"),
                                   sims[:, :, :].rearrange("p a b -> p (a b)"), simrn[:, :], ALU.mult))

            def split_weight(n):
                dve.wait_ge(s_wraw[n % 2], 16 * (n // 2 + 1))
                link(dve.tensor_copy(whi[:, n, :], wraw[:, n % 2, :]))
                dve.tensor_tensor(wlo[:, n, :], wraw[:, n % 2, :], whi[:, n, :].bitcast(F32),
                                  ALU.subtract).then_inc(s_wsplit, 1)

            for n in range(NW):
                split_weight(n)
            for g in range(NG):
                if g >= 2:
                    dve.wait_ge(s_ht[g % 2], 16 * GH * NB * (g // 2))
                for qc in range(NHF):
                    dve.wait_ge(s_pair, 2 + NT * (NHF * g + qc + 1))
                    dve.tensor_copy(hout[:, g % 2, qc * HALF:(qc + 1) * HALF], ps[:, 6 + qc, :]).then_inc(s_head, 1)
                if g + 2 < NG:
                    stage_v(g + 2)

            def x1_and_norms(b):
                dve.wait_ge(s_o1, b + 1)
                xb = X[:, b * NT:(b + 1) * NT, :].rearrange("p a b -> p (a b)")
                ins = dve.tensor_tensor(xb, psf[:, b * 1024:b * 1024 + 1024], xb, ALU.add)
                ins.then_inc(s_x1, 1)
                dve.wait_ge(s_x1, b + 1)
                m_, v_ = statistics(X, b)
                link(dve.tensor_scalar(powin[:, b, 0, :], v_, EPS, None, ALU.add))
                link(dve.reciprocal(tmp8[:, 0, :], powin[:, b, 0, :]))
                link(dve.tensor_tensor(tmp8[:, 1, :], tmp8[:, 0, :], v_, ALU.mult))
                dve.tensor_scalar(powin[:, b, 1, :], tmp8[:, 1, :], EPS, None, ALU.add).then_inc(s_powin, 1)
                dve.wait_ge(s_pow, 4 + b)
                link(dve.tensor_tensor(tmp8[:, 2, :], powout[:, b, 0, :], powout[:, b, 1, :], ALU.mult))
                dve.scalar_tensor_tensor(out=powin[:, b, 1, :], in0=m_, scalar=-1.0, in1=powout[:, b, 0, :],
                                         op0=ALU.mult, op1=ALU.mult).then_inc(s_y, 1)
                normalise(b, tmp8[:, 2, :], s_u)

            def gating(part, b, bank):
                n = 2 * part + b
                lg, gr, ex = gt[:, 3 * b, :, :], gt[:, 3 * b + 1, :, :], gt[:, 3 * b + 2, :, :]
                norm2, rn = g1[:, 2 * b, :], g1[:, 2 * b + 1, :]
                top, ss = g1[:, 4, :], g1[:, 5, :]
                L = ps[:, bank, 0:NT * NE].rearrange("p (i e) -> p i e", e=NE)
                full = [P, NT, NE]

                def wide(t):
                    return t.unsqueeze(2).to_broadcast(full)

                dve.wait_ge(s_log, n + 1)
                dve.tensor_scalar(norm2, ps[:, bank, 64:64 + NT], 1e-24, None, ALU.max).then_inc(s_powin, 1)
                dve.wait_ge(s_pow, (6 if part == 0 else 10) + b)
                link(dve.tensor_tensor(lg, L, wide(rn), ALU.mult))
                link(dve.tensor_tensor(lg, lg, gates[:, part:part + 1, :].to_broadcast(full), ALU.subtract))
                link(dve.tensor_scalar(gr, lg, 0.0, None, ALU.max))
                link(dve.tensor_reduce(top, gr, AX.X, ALU.max))
                dve.tensor_tensor(ex, gr, wide(top), ALU.subtract).then_inc(s_gex, 1)
                others = lg.unsqueeze(2).to_broadcast([P, NT, NE, NE])
                own = lg.unsqueeze(3).to_broadcast([P, NT, NE, NE])
                dve.tensor_tensor(cmp_[:, 0], others, own, ALU.is_gt)
                link(dve.tensor_tensor(cmp_[:, 1], others, own, ALU.is_equal))
                link(dve.tensor_tensor(cmp_[:, 1], cmp_[:, 1],
                                       before[:, :, :].unsqueeze(1).to_broadcast([P, NT, NE, NE]), ALU.mult))
                link(dve.tensor_tensor(cmp_[:, 0], cmp_[:, 0], cmp_[:, 1], ALU.add))
                link(dve.tensor_reduce(lg, cmp_[:, 0], AX.X, ALU.add))
                link(dve.tensor_scalar(ss, top, 0.0, None, ALU.is_le))
                link(dve.scalar_tensor_tensor(out=lg, in0=lg, scalar=2.0, in1=wide(ss), op0=ALU.is_lt, op1=ALU.mult))
                link(dve.scalar_tensor_tensor(out=lg, in0=gr, scalar=0.0, in1=lg, op0=ALU.is_gt, op1=ALU.max))
                dve.wait_ge(s_gexo, n + 1)
                link(dve.tensor_tensor(ex, ex, lg, ALU.mult))
                link(dve.tensor_reduce(ss, ex, AX.X, ALU.add))
                link(dve.reciprocal(ss, ss))
                r = rw[:, b, :, :]
                link(dve.tensor_tensor(r, ex, wide(ss), ALU.mult))
                rp = RP[:, b, :, :]
                link(dve.tensor_copy(rp[:, :, 0:NE], r))
                link(dve.tensor_tensor(lg, r, rp[:, :, 0:NE], ALU.subtract))
                link(dve.tensor_copy(rp[:, :, NE:2 * NE], lg))
                dve.tensor_tensor(rp[:, :, 2 * NE:3 * NE], lg, rp[:, :, NE:2 * NE], ALU.subtract).then_inc(s_rp, 1)

            def rpt_copy(n, b, bank):
                dve.wait_ge(s_rpT, n)
                dve.tensor_copy(RPT[0:3 * NE, b, :], ps[0:3 * NE, bank, :].bitcast(BF16)).then_inc(s_rpt, 1)

            x1_and_norms(0)
            link(dve.memset(RPT[:, :, :], 0.0))
            x1_and_norms(1)
            gating(0, 0, 0)
            rpt_copy(1, 0, 1)

            def low(n):
                dve.wait_ge(s_shi, n + 1)
                dve.tensor_tensor(slo[:, n % 3, :], sring[:, n % 3, :], shi[:, n % 3, :].bitcast(F32),
                                  ALU.subtract).then_inc(s_slo, 1)

            pending = None
            for r, (kind, m, e) in enumerate(ring_jobs):
                if kind == "bc":
                    n = m * NE + e
                    b, hf = divmod(m, NHF)
                    dve.wait_ge(s_bc, n + 1)
                    dve.tensor_tensor(sring[:, n % 3, :], ps[:, 6 + r % 2, :], nT[:, toks(b, hf)],
                                      ALU.mult).then_inc(s_s, 1)
                    if n:
                        if n - 1 >= 3:
                            dve.wait_ge(s_mm, n - 3)
                        low(n - 1)
                    if n == 1:
                        gating(0, 1, 3)
                    if n == NE - 1:
                        rpt_copy(2, 1, 4)
                    if e == 1 and m:
                        dve.wait_ge(s_mm, m * NE)
                        dve.tensor_copy(vT[:, (m - 1) % 2, :], ps[:, 3 * ((m - 1) % 2) + 2, :]).then_inc(s_vT, 1)
                    if n == NB * NHF * NE - 1:
                        dve.wait_ge(s_mm, n - 2)
                        low(n)
                        dve.wait_ge(s_mm, n + 1)
                        dve.tensor_copy(vT[:, m % 2, :], ps[:, 3 * (m % 2) + 2, :]).then_inc(s_vT, 1)
                else:
                    dve.wait_ge(s_vtr, m + 1)
                    dve.tensor_copy(V[:, m * TPH:(m + 1) * TPH, :].rearrange("p a b -> p (a b)"),
                                    ps[:, 6 + r % 2, :]).then_inc(s_v, 1)

            def attn_low(q):
                dve.wait_ge(s_ahi, q + 1)
                sl = slice(q * HALF, (q + 1) * HALF)
                dve.tensor_tensor(alo[:, sl], ps[:, 6 + q % 2, :], ahi[:, sl].bitcast(F32),
                                  ALU.subtract).then_inc(s_alo, 1)

            for T in range(NB * NT):
                i = T % NT
                dve.wait_ge(s_S, T + 1)
                link(dve.tensor_reduce(mx[:, 0, T:T + 1], psf[:, (T % 2) * 1024:(T % 2) * 1024 + (i + 1) * P],
                                       AX.X, ALU.max))
                dve.tensor_scalar(mx[:, 1, T:T + 1], mx[:, 0, T:T + 1], -SMAX_SCALE, None,
                                  ALU.mult).then_inc(s_nb, 1)
                if T % 4 == 3 and T > 3:
                    attn_low(T // 4 - 1)
            attn_low(3)

            dve.wait_ge(s_exp, NB * NT)
            link(dve.reciprocal(rowsum[:, :], rowsum[:, :]))
            for b in range(NB):
                last = dve.tensor_tensor(rwn[:, b], rw[:, b],
                                         rowsum[:, b * NT:(b + 1) * NT].unsqueeze(2).to_broadcast([P, NT, NE]),
                                         ALU.mult)
            link(last)
            dve.wait_ge(s_hs, 2)
            def add_experts(b):
                for i in range(NT):
                    T = b * NT + i
                    dve.wait_ge(s_op, T + 1)
                    for e in range(NE):
                        col = (T % 3) * 1024 + e * P
                        ins = dve.scalar_tensor_tensor(out=HS[:, T, :], in0=psf[:, col:col + P],
                                                       scalar=rwn[:, b, i, e:e + 1], in1=HS[:, T, :],
                                                       op0=ALU.mult, op1=ALU.add)
                        if e < NE - 1:
                            link(ins)
                    ins.then_inc(s_acc, 1)
                dve.wait_ge(s_acc, (b + 1) * NT)

            def second_norm(b):
                m_, v_ = statistics(HS, b)
                dve.tensor_scalar(powin[:, b, 0, :], v_, EPS, None, ALU.add).then_inc(s_powin, 1)
                dve.tensor_tensor(X[:, b * NT:(b + 1) * NT, :], X[:, b * NT:(b + 1) * NT, :],
                                  HS[:, b * NT:(b + 1) * NT, :], ALU.add).then_inc(s_xh, 1)
                dve.wait_ge(s_pow, 8 + b)
                for i in range(NT):
                    last = dve.tensor_scalar(U[:, b * NT + i, :], HS[:, b * NT + i, :], mv[:, b * NT + i, 0:1],
                                             powout[:, b, 0, i:i + 1], ALU.subtract, ALU.mult)
                last.then_inc(s_u, 1)

            def n2_low(b):
                dve.wait_ge(s_n2hi, b + 1)
                sl = slice(b * S, (b + 1) * S)
                dve.tensor_tensor(alo[:, sl], nT[:, sl], ahi[:, sl].bitcast(F32), ALU.subtract).then_inc(s_n2lo, 1)

            add_experts(0)
            second_norm(0)
            add_experts(1)
            second_norm(1)
            n2_low(0)
            gating(1, 0, 4)
            rpt_copy(3, 0, 5)
            n2_low(1)
            gating(1, 1, 6)

            NM = NB * NHF * NE

            def moe_low(n):
                dve.wait_ge(s_shi, 32 + n + 1)
                if n >= 3:
                    dve.wait_ge(s_w2, n - 2)
                k = (32 + n) % 3
                dve.tensor_tensor(slo[:, k, :], sring[:, k, :], shi[:, k, :].bitcast(F32),
                                  ALU.subtract).then_inc(s_slo, 1)

            def moe_end(m):
                dve.wait_ge(s_w2, (m + 1) * NE)
                dve.tensor_copy(moeT[:, m % 2, :], ps[:, 4 + m % 2, :]).then_inc(s_moe, 1)

            def moe_out(m):
                dve.wait_ge(s_mtr, m + 1)
                if m >= 2:
                    dve.wait_ge(s_out[m % 2], 16 * (m // 2))
                dve.tensor_tensor(fin[:, m % 2, :], ps[:, 4 + m % 2, :],
                                  X[:, m * TPH:(m + 1) * TPH, :].rearrange("p a b -> p (a b)"),
                                  ALU.add).then_inc(s_fin, 1)

            for n in range(NM):
                m, e = divmod(n, NE)
                if n == NE:
                    rpt_copy(4, 1, 7)
                dve.wait_ge(s_bc, 32 + n + 1)
                dve.wait_ge(s_gel, n + 1)
                dve.tensor_tensor(sring[:, (32 + n) % 3, :], ps[:, 2 + n % 2, :], gel[:, n % 2, :],
                                  ALU.mult).then_inc(s_s, 1)
                if n:
                    moe_low(n - 1)
                if e == 2 and m:
                    moe_end(m - 1)
                if e == 4 and m:
                    moe_out(m - 1)
            moe_low(NM - 1)
            moe_end(NB * NHF - 1)
            moe_out(NB * NHF - 1)

        @block.tensor
        def _(pe):
            def three_pass(o, wh, wl, xh, xl, start, stop):
                pe.matmul(o, wh, xh, start=start, stop=False)
                pe.matmul(o, wl, xh, start=False, stop=False)
                return pe.matmul(o, wh, xl, start=False, stop=stop)

            pe.wait_ge(s_id, 1)
            for n, (what, b, h, e) in enumerate(JOBS):
                if n >= 8:
                    eng, cnt = emptied(n - 8)
                    pe.wait_ge(s_jact if eng == "act" else s_jdve, cnt)
                bank = ps[:, n % 8, :]
                if what == "wT":
                    pe.wait_ge(s_wnat, 64)
                    for k in range(4):
                        last = pe.transpose(bank[:, k * P:(k + 1) * P], wnat[:, k, :], ident[:, :])
                elif what == "xT":
                    pe.wait_ge(s_xn, b + 1)
                    for k in range(TPH):
                        last = pe.transpose(bank[:, k * P:(k + 1) * P], U[:, b * NT + h * TPH + k, :], ident[:, :])
                elif what in "qk":
                    if h == 0 and what == "q":
                        pe.wait_ge(s_jact, emptied(JOB[("xT", b, 1)])[1])
                        pe.wait_ge(s_jdve, emptied(JOB[("xT", b, 0)])[1])
                    last = pe.matmul(bank, wT[:, "qk".index(what), :], nT[:, toks(b, h)], start=True, stop=True)
                elif what == "v":
                    for k in range(TPH):
                        t0 = b * S + h * HALF + k * P
                        last = pe.matmul(bank[:, k * P:(k + 1) * P], nT[:, t0:t0 + P], wT[:, 2, :],
                                         start=True, stop=True)
                elif what == "sums":
                    pe.wait_ge(s_sums, 2)
                    pe.wait_ge(s_const, 2)
                    pe.matmul(bank[:, 0:2 * NE], ones[:, :], simsq[:, :], start=True, stop=True)
                    last = pe.matmul(bank[:, 2 * NE:2 * NE + NB], wT[:, 2, :], sumx[:, :], start=True, stop=True)
                else:
                    pe.wait_ge(s_cvec, 1)
                    for k in range(NB):
                        last = pe.matmul(bank[:, k * P:(k + 1) * P], cvecb[:, k, :], wT[:, 3, :],
                                         start=True, stop=True)
                last.then_inc(s_job, 1)
            pe.wait_ge(s_jact, sum(1 for j in JOBS if j[3] == "act"))
            pe.wait_ge(s_jdve, sum(1 for j in JOBS if j[3] == "dve"))

            with pe.Fori(0, NG // 2) as gg:
                def scores(i):
                    u, k = divmod(i, 32)
                    qc, kc, pair = k // 16, (k // 2) % 8, k % 2
                    if i == 0:
                        pe.wait_ge(s_tanh, 64 * gg + 3)
                    elif i >= 3:
                        pe.wait_ge(s_tanh, 64 * gg + (i + 1))
                    for j in range(2):
                        h = 2 * pair + j
                        col = (i % 3) * 1024 + j * 512
                        last = pe.matmul(psf[:, col:col + 512], ops[:, u, K_, h, kc * P:(kc + 1) * P],
                                         ops[:, u, Q_, h, qc * HALF:(qc + 1) * HALF], start=True, stop=True)
                    last.then_inc(s_score, 1)

                def heads(k):
                    u, qc, kc = k // 16, (k // 8) % 2, k % 8
                    if kc == 0:
                        pe.wait_ge(s_head, 4 * gg + (2 * u + qc + 1))
                    pe.wait_ge(s_tanh, 64 * gg + (3 + 2 * k + 2))
                    for j in range(GH):
                        last = pe.matmul(ps[32 * j:32 * j + 32, 6 + qc, :], vst[:, u, kc, j, :],
                                         tanhs[:, (2 * k + j // 2) % 4, j % 2, :], start=(kc == 0), stop=(kc == 7))
                    last.then_inc(s_pair, 1)

                for k in range(32):
                    if k % 16 == 0:
                        u = k // 16
                        pe.wait_ge(s_ops[u], 16 * 16 * gg + 16 * 16)
                    scores(2 * k)
                    scores(2 * k + 1)
                    if k % 16 == 1:
                        pe.wait_ge(s_vst, 2 * gg + (k // 16 + 1))
                    if k:
                        heads(k - 1)
                heads(31)

            pe.wait_ge(s_tanh, SCORES)
            for u in range(2):
                pe.wait_ge(s_ht[u], 16 * NH * NB // 2)
            for b in range(NB):
                for i in range(NT):
                    last = pe.matmul(psf[:, b * 1024 + i * P:b * 1024 + (i + 1) * P],
                                     HT[:, b, i * P:(i + 1) * P], wT[:, 3, :], start=True, stop=True)
                last.then_inc(s_o1, 1)

            def turn_u(part, b):
                pe.wait_ge(s_u, 2 * part + b + 1)
                for i in range(NT):
                    col = (4 + 2 * b) * 512 + i * P
                    last = pe.transpose(psf[:, col:col + P], U[:, b * NT + i, :], ident[:, :])
                last.then_inc(s_uT, 1)

            def logits(part, b, bank):
                pe.wait_ge(s_sq, 2 * part + b + 1)
                for i in range(NT):
                    t0 = b * S + i * P
                    pe.matmul(ps[:, bank, i * NE:(i + 1) * NE], nT[:, t0:t0 + P], sims[:, part, :],
                              start=True, stop=True)
                    last = pe.matmul(ps[:, bank, 64 + i:65 + i], SQ[:, t0:t0 + P], ones[:, 0:1],
                                     start=True, stop=True)
                last.then_inc(s_log, 1)

            def turn_rw(n, b, bank):
                pe.wait_ge(s_rp, n)
                for i in range(NT):
                    last = pe.transpose(ps[0:3 * NE, bank, :].bitcast(BF16)[:, i * P:(i + 1) * P],
                                        RP[:, b, i, :], identb[:, :])
                last.then_inc(s_rpT, 1)

            pe.wait_ge(s_head, 2 + NG * NHF)
            turn_u(0, 0)
            logits(0, 0, 0)
            turn_u(0, 1)
            pe.wait_ge(s_x1, 2)
            logits(0, 1, 3)
            pe.wait_ge(s_const, 8)
            turn_rw(1, 0, 1)

            def broadcast(n, b, hf, e, bank):
                last = pe.matmul(ps[:, bank, :], spread[:, e, :], RPT[:, b, hf * HALF:(hf + 1) * HALF],
                                 start=True, stop=True)
                last.then_inc(s_bc, 1)

            pe.wait_ge(s_rpt, 1)
            pe.wait_ge(s_nT, 2)
            pe.wait_ge(s_wsplit, NW)

            def ring_job(r):
                kind, m, e = ring_jobs[r]
                if r >= 2:
                    k, m2, e2 = ring_jobs[r - 2]
                    if k == "bc":
                        pe.wait_ge(s_s, m2 * NE + e2 + 1)
                    else:
                        pe.wait_ge(s_v, m2 + 1)
                if kind == "bc":
                    b, hf = divmod(m, NHF)
                    broadcast(m * NE + e, b, hf, e, 6 + r % 2)
                else:
                    pe.wait_ge(s_vT, m + 1)
                    for k in range(TPH):
                        last = pe.transpose(ps[:, 6 + r % 2, k * P:(k + 1) * P], vT[:, m % 2, k * P:(k + 1) * P],
                                            ident[:, :])
                    last.then_inc(s_vtr, 1)

            issued = 0
            for n in range(NB * NHF * NE):
                m, e = divmod(n, NE)
                ahead = min(n + 2, NB * NHF * NE - 1)
                while issued <= RING[("bc", *divmod(ahead, NE))]:
                    if ring_jobs[issued] == ("bc", 1, 0):
                        turn_rw(2, 1, 4)
                        pe.wait_ge(s_rpt, 2)
                    ring_job(issued)
                    issued += 1
                if e == 0 and m >= 2:
                    pe.wait_ge(s_qk, m - 1)
                    pe.wait_ge(s_vT, m - 1)
                pe.wait_ge(s_slo, n + 1)
                for k, w in enumerate((WQ, WK, WV)):
                    sl = slice(e * C, (e + 1) * C)
                    last = three_pass(ps[:, 3 * (m % 2) + k, :], whi[:, w, sl], wlo[:, w, sl],
                                      shi[:, n % 3, :], slo[:, n % 3, :], e == 0, e == NE - 1)
                last.then_inc(s_mm, 1)
            ring_job(len(ring_jobs) - 1)

            pe.wait_ge(s_qk, 4)
            pe.wait_ge(s_v, 4)

            def qk(T):
                b, i = divmod(T, NT)
                if T >= 2:
                    pe.wait_ge(s_exp, T - 1)
                base, nk = (T % 2) * 1024, (i + 1) * P
                for k0 in range(0, nk, HALF):
                    w = min(HALF, nk - k0)
                    pe.matmul(psf[:, base + k0:base + k0 + w], qT[:, b, i * P:(i + 1) * P], kT[:, b, k0:k0 + w],
                              start=True, stop=True)
                pe.matmul(psf[:, base + nk - P:base + nk], identb[:, :], maskb[:, :], start=False, stop=True,
                          skip_group_check=True).then_inc(s_S, 1)

            def turn_prob(T):
                pe.wait_ge(s_exp, T + 1)
                for n, (T_, k0, nk) in enumerate(ptjobs):
                    if T_ != T:
                        continue
                    if n >= 2:
                        pe.wait_ge(s_pt, n - 1)
                    for k in range(nk):
                        last = pe.transpose(ps[:, 4 + n % 2, k * P:(k + 1) * P],
                                            prob[:, T % 2, (k0 + k) * P:(k0 + k + 1) * P], ident[:, :])
                    last.then_inc(s_ptm, 1)

            def attend(T):
                b, i = divmod(T, NT)
                q = T // 4
                pe.wait_ge(s_pt, pt_until(T))
                if q >= 2 and T % 4 == 0:
                    pe.wait_ge(s_alo, q - 1)
                for j in range(i + 1):
                    last = pe.matmul(ps[:, 6 + q % 2, (T % 4) * P:(T % 4 + 1) * P], V[:, b * NT + j, :],
                                     probT[:, T % 2, j, :], start=(j == 0), stop=(j == i))
                last.then_inc(s_av, 1)

            qk(0)
            for T in range(NB * NT):
                if T + 1 < NB * NT:
                    qk(T + 1)
                turn_prob(T)
                if T:
                    attend(T - 1)
            attend(NB * NT - 1)

            pe.wait_ge(s_alo, 4)
            pe.wait_ge(s_exp, NB * NT)
            pe.wait_ge(s_pt, len(ptjobs))

            def oproj(T):
                if T >= 3:
                    pe.wait_ge(s_acc, T - 2)
                t0 = T * P
                for k in range(2):
                    base = (T % 3) * 1024 + k * 512
                    sl = slice(k * 512, (k + 1) * 512)
                    o = psf[:, base:base + 512]
                    pe.matmul(o, ahi[:, t0:t0 + P], whi[:, WO, sl], start=True, stop=False)
                    pe.matmul(o, ahi[:, t0:t0 + P], wlo[:, WO, sl], start=False, stop=False)
                    last = pe.matmul(o, alo[:, t0:t0 + P], whi[:, WO, sl], start=False, stop=True)
                last.then_inc(s_op, 1)

            for T in range(NB * NT):
                oproj(T)
            pe.wait_ge(s_acc, NB * NT)
            turn_u(1, 0)
            pe.wait_ge(s_nT, 3)
            logits(1, 0, 4)
            turn_u(1, 1)
            pe.wait_ge(s_nT, 4)
            logits(1, 1, 6)

            def first_layer(n):
                m, e = divmod(n, NE)
                b, hf = divmod(m, NHF)
                if n >= 2:
                    pe.wait_ge(s_gel, n - 1)
                if e == 0:
                    pe.wait_ge(s_n2lo, b + 1)
                sl = slice(e * C, (e + 1) * C)
                three_pass(ps[:, n % 2, :], whi[:, W1, sl], wlo[:, W1, sl], ahi[:, toks(b, hf)],
                           alo[:, toks(b, hf)], True, True).then_inc(s_int, 1)

            def gate(n):
                m, e = divmod(n, NE)
                b, hf = divmod(m, NHF)
                if n == 0:
                    turn_rw(3, 0, 5)
                    pe.wait_ge(s_rpt, 3)
                if n == NE:
                    turn_rw(4, 1, 7)
                    pe.wait_ge(s_rpt, 4)
                if n >= 2:
                    pe.wait_ge(s_s, 32 + n - 1)
                broadcast(32 + n, b, hf, e, 2 + n % 2)

            def second_layer(n):
                m, e = divmod(n, NE)
                pe.wait_ge(s_slo, 32 + n + 1)
                if e == 0 and m >= 2:
                    pe.wait_ge(s_fin, m - 1)
                k = (32 + n) % 3
                sl = slice(e * C, (e + 1) * C)
                three_pass(ps[:, 4 + m % 2, :], whi[:, W2, sl], wlo[:, W2, sl], shi[:, k, :], slo[:, k, :],
                           e == 0, e == NE - 1).then_inc(s_w2, 1)

            def turn_moe(m):
                pe.wait_ge(s_moe, m + 1)
                for k in range(TPH):
                    last = pe.transpose(ps[:, 4 + m % 2, k * P:(k + 1) * P], moeT[:, m % 2, k * P:(k + 1) * P],
                                        ident[:, :])
                last.then_inc(s_mtr, 1)

            NM = NB * NHF * NE
            for n in range(NM + 2):
                if n < NM:
                    first_layer(n)
                    gate(n)
                if n >= 2:
                    second_layer(n - 2)
                    m, e = divmod(n - 2, NE)
                    if e == 3 and m:
                        turn_moe(m - 1)
            turn_moe(NB * NHF - 1)


_INS = ['L0_attn_x', 'L0_attn_Wq', 'L0_attn_bq', 'L0_attn_Wk', 'L0_attn_bk', 'L0_attn_Wv', 'L0_attn_bv',
        'L0_attn_Wo', 'L0_attn_bo', 'L0_ffn_ln1_w', 'L0_ffn_ln1_b', 'L0_ffn_ln2_w', 'L0_ffn_ln2_b',
        'L0_ffn_smha_sim', 'L0_ffn_smha_gates', 'L0_ffn_q_proj', 'L0_ffn_k_proj', 'L0_ffn_v_proj',
        'L0_ffn_o_proj', 'L0_ffn_moe_sim', 'L0_ffn_moe_gates', 'L0_ffn_w1', 'L0_ffn_w2']
_OUTS = [((2, 1024, 128), 'float32')]


def kernel(**inputs):
    import numpy as _np
    import concourse.bacc as _bacc
    from concourse import mybir as _mybir
    from concourse.bass_utils import run_bass_kernel_spmd as _run

    nc = _bacc.Bacc("TRN2", target_bir_lowering=False, num_devices=1)
    arrays, args = {}, []
    for name in _INS:
        a = _np.ascontiguousarray(inputs[name])
        arrays[f"in_{name}_dram"] = a
        args.append(nc.dram_tensor(f"in_{name}_dram", a.shape, _mybir.dt.from_np(a.dtype), kind="ExternalInput").ap())
    for i, (shape, dtype) in enumerate(_OUTS):
        dt = _mybir.dt.from_np(_np.dtype(dtype))
        args.append(nc.dram_tensor(f"out_{i}_dram", shape, dt, kind="ExternalOutput").ap())
    preln_layer(nc, *args)
    r = _run(nc, [arrays], core_ids=[0])
    got = tuple(r.results[0][f"out_{i}_dram"] for i in range(len(_OUTS)))
    return got[0]
```

```python
from contextlib import ExitStack

import concourse.bass as bass
from concourse import mybir

ALU = mybir.AluOpType
ACT = mybir.ActivationFunctionType
AX = mybir.AxisListType
F32 = mybir.dt.float32
F32R = mybir.dt.float32r
BF16 = mybir.dt.bfloat16

P = 128
EPS = 1e-5
MASKED = -3.0e38


def preln_layer(nc, x, Wq, bq, Wk, bk, Wv, bv, Wo, bo, ln1_w, ln1_b, ln2_w, ln2_b,
                smha_sim, smha_gates, q_proj, k_proj, v_proj, o_proj, moe_sim, moe_gates, w1, w2, out):
    NB, S, C = x.shape
    NH = 16
    D = C // NH
    NE = q_proj.shape[0]
    NT = S // P
    HALF = 512
    NHF = S // HALF
    TPH = HALF // P
    PT = NB * TPH
    assert C == P and NB == 2 and NE * C == 1024 and NT == 8
    GH = 4
    NG = NH // GH
    R = NB * D
    SMAX_SCALE = float(C) ** -0.5
    Q_, K_ = 0, 1
    PAIRS = [(0, 0), (0, 1), (0, 2), (1, 0), (1, 1), (1, 2), (2, 0), (2, 1)]
    OP_DMAS = 2 * len(PAIRS)
    NW = 6
    WQ, WK, WV, WO, W1, W2 = range(NW)

    JOBS = [("wT", 0, 0, "act"), ("xT", 0, 0, "act"), ("xT", 0, 1, "act")]
    JOBS += [(w, 0, b, "act") for w in "qk" for b in range(NB)]
    JOBS += [("xT", 1, 0, "dve"), ("xT", 1, 1, "dve")]
    JOBS += [(w, 1, b, "act") for w in "kq" for b in range(NB)]
    JOBS += [("v", c, b, "dve") for c in range(NHF) for b in range(NB)]
    JOB = {j[:3]: n for n, j in enumerate(JOBS)}
    NJ = len(JOBS)

    def emptied(n):
        e = JOBS[n][3]
        return e, sum(1 for j in JOBS[:n + 1] if j[3] == e)

    SPLITS = [(Q_, 0, 0), (Q_, 0, 1), (K_, 0, 0), (K_, 0, 1), (K_, 1, 0), (K_, 1, 1), (Q_, 1, 0), (Q_, 1, 1)]

    qk_parts = nc.dram_tensor("qk_parts", [2, 3, P, NB, S], BF16, kind="Internal").ap()

    with ExitStack() as ctx:
        def tensor(name, shape, dt, stack=ctx):
            return stack.enter_context(nc.sbuf_tensor(name, shape, dt))

        def sem(name):
            return ctx.enter_context(nc.semaphore(name))

        ps = ctx.enter_context(nc.psum_tensor("ps", [P, 8, 512], F32))
        psf = ps[:, :, :].rearrange("p a b -> p (a b)")

        ident = tensor("ident", [P, P], F32)
        identb = tensor("identb", [P, P], BF16)
        maskb = tensor("maskb", [P, P], BF16)
        spread = tensor("spread", [P, NE, P], BF16)
        before = tensor("before", [P, NE, NE], BF16)
        ones = tensor("ones", [P, P], F32)
        minus_half = tensor("minus_half", [P, 16], F32)
        warm = tensor("warm", [P, 2], F32)
        start = tensor("start", [P, 2], F32)
        bcol = tensor("bcol", [P, 4], F32)
        lncol = tensor("lncol", [P, 4], F32)
        bv_row = tensor("bv_row", [P, P], F32)
        bo_row = tensor("bo_row", [P, P], F32)
        gates = tensor("gates", [P, 2, NE], F32)
        sims = tensor("sims", [P, 4, NE], F32)
        simsq = tensor("simsq", [P, 2 * NE], F32)
        simn2 = tensor("simn2", [P, 2 * NE], F32)
        simrn = tensor("simrn", [P, 2 * NE], F32)
        wnat = tensor("wnat", [P, 4, P], F32)
        wT = tensor("wT", [P, 4, P], F32)
        X = tensor("X", [P, NB * NT, P], F32)
        U = tensor("U", [P, NB * NT, P], F32)
        nT = tensor("nT", [P, NB * S], F32)
        stats = tensor("stats", [P, NB * NT, 6], F32)
        mv = tensor("mv", [P, NB * NT, 2], F32)
        powin = tensor("powin", [P, NB, 2, NT], F32)
        powout = tensor("powout", [P, NB, 2, NT], F32)
        tmp8 = tensor("tmp8", [P, 4, NT], F32)
        sumq = tensor("sumq", [P, NB * NHF], F32)
        sumx = tensor("sumx", [P, NB], F32)
        cvec = tensor("cvec", [P, NB], F32)
        cvecb = tensor("cvecb", [P, NB, P], F32)
        row_add = tensor("row_add", [P, NB, P], F32)
        whi = tensor("whi", [P, NW, NE * C], F32R)
        wlo = tensor("wlo", [P, NW, NE * C], F32R)
        HT = tensor("HT", [P, NB * S], F32)
        wraw = tensor("wraw", [P, 2, NE * C], F32)
        SQ = wraw[:, 0, :]
        RP = tensor("RP", [P, NHF, PT, 3 * NE], BF16)
        RPT = tensor("RPT", [P, NHF, S], BF16)
        rw = tensor("rw", [P, NHF, PT, NE], F32)
        gt = tensor("gt", [P, NHF, 3, PT, NE], F32)
        cmp_ = wraw[:, 1, :].bitcast(BF16)[:, 0:2 * PT * NE * NE].rearrange("p (t i j e) -> p t i j e", t=2, i=PT, j=NE)
        g1 = tensor("g1", [P, 6, PT], F32)

        early = ExitStack()
        parts = tensor("parts", [P, 2, 3, NB, S], BF16, early)
        q32 = tensor("q32", [P, 2, HALF], F32, early)
        rest = tensor("rest", [P, 2, HALF], F32, early)
        ops_k = tensor("ops_k", [P, 2, GH, S], BF16, early)
        ops_q = tensor("ops_q", [P, 2, GH, HALF], BF16, early)
        VP = tensor("VP", [P, NT, NH, R], F32, early)
        vst = tensor("vst", [P, 2, NT, GH, 32], F32, early)
        tanhs = tensor("tanhs", [P, 4, 2, HALF], F32, early)
        hout = tensor("hout", [P, 2, HALF], F32, early)
        early.close()
        HS = tensor("HS", [P, NB * NT, P], F32)
        sring = tensor("sring", [P, 3, HALF], F32)
        shi = tensor("shi", [P, 3, HALF], F32R)
        slo = tensor("slo", [P, 3, HALF], F32R)
        qT = tensor("qT", [P, NB * NHF, HALF], F32)
        kT = tensor("kT", [P, NB * NHF, HALF], F32)
        vT = tensor("vT", [P, 2, HALF], F32)
        V = tensor("V", [P, NB * NT, P], F32)
        prob = tensor("prob", [P, 2, S], F32)
        probT = tensor("probT", [P, 2, NT, 2, P], F32)
        mx = tensor("mx", [P, 2, NB * NT], F32)
        rowsum = tensor("rowsum", [P, NB * NT], F32)
        rwn = tensor("rwn", [P, NHF, PT, NE], F32)
        ahi = tensor("ahi", [P, NB * S], F32R)
        alo = tensor("alo", [P, NB * S], F32R)
        gel = tensor("gel", [P, 2, HALF], F32)
        eterms = [t.rearrange("p t (e c) -> p t e c", c=P) for t in (gel[:, :, :], qT[:, 0:2, :])]

        def eterm(T):
            return eterms[T // PT][:, T % 2]

        moeT = vT
        fin = HS

        s_x = [sem(f"x_loaded{b}") for b in range(NB)]
        s_wnat = sem("wnat_loaded")
        s_small = sem("biases_loaded")
        s_rows_in = sem("small_loaded")
        s_const = sem("consts_made")
        s_id = sem("ident_made")
        s_pool = sem("pool_step")
        s_dve = sem("dve_step")
        s_powin = sem("pow_inputs")
        s_pow = sem("pow_results")
        s_xn = sem("xn_ready")
        s_job = sem("job_products")
        s_jact = sem("job_emptied_by_act")
        s_jdve = sem("job_emptied_by_dve")
        s_rest = sem("qk_rest_taken")
        s_mid = sem("qk_middle_taken")
        s_split = sem("qk_split")
        s_sums = sem("sums_inputs")
        s_cvec = sem("cvec_ready")
        s_gtan = sem("gates_tanh")
        s_kd = sem("k_parts_in_dram")
        s_qd = [sem(f"q_parts{c}_in_dram") for c in range(NHF)]
        s_ops = [sem(f"ops_loaded{u}") for u in range(2)]
        s_vst = sem("v_staged")
        s_score = sem("scores_ready")
        s_tanh = sem("tanh_done")
        s_pair = sem("tanh_pairs_used")
        s_head = sem("heads_emptied")
        s_ht = [sem(f"heads_moved{u}") for u in range(2)]
        s_wraw = [sem(f"wraw_loaded{u}") for u in range(2)]
        s_wsplit = sem("weights_split")
        s_o1 = sem("out_proj_ready")
        s_x1 = sem("x1_ready")
        s_y = sem("y_ready")
        s_u = sem("u_ready")
        s_uT = sem("uT_ready")
        s_nT = sem("nT_ready")
        s_sq = sem("sq_ready")
        s_log = sem("logits_ready")
        s_gex = sem("gate_tanh_in")
        s_gexo = sem("gate_tanh_out")
        s_rp = sem("rw_parts")
        s_rpT = sem("rw_partsT")
        s_rpt = sem("rpt_ready")
        s_bc = sem("bcast_ready")
        s_s = sem("scaled_ready")
        s_shi = sem("scaled_hi")
        s_slo = sem("scaled_lo")
        s_mm = sem("steps_done")
        s_qksum = sem("qk_sums")
        s_rptz = sem("rpt_cleared")
        s_added = sem("experts_added")
        s_sumd = sem("batch_sums_ready")
        s_cvt = sem("batch_sums_taken")
        s_addrow = sem("added_rows_ready")
        s_rowadd = sem("added_rows_taken")
        s_simz = sem("sims_cleared")
        s_nTe = sem("part0_n1_ready")
        s_sqe = sem("part0_sq_ready")
        s_rows = sem("logit_rows_ready")
        s_rowsc = sem("logit_rows_copied")
        s_rwn = sem("gates_over_rowsum")
        s_op2 = sem("oproj_second_ready")
        s_esc = sem("experts_scaled")
        s_pool2 = sem("pool_sums")
        s_qk = sem("qk_copied")
        s_vT = sem("vT_copied")
        s_vtr = sem("v_turned")
        s_v = sem("v_copied")
        s_S = sem("S_ready")
        s_nb = sem("negmax_ready")
        s_exp = sem("exp_done")
        s_ptm = sem("probT_made")
        s_pt = sem("probT_copied")
        s_av = sem("av_done")
        s_ahi = sem("attn_hi")
        s_alo = sem("attn_lo")
        s_op = sem("oproj_ready")
        s_acc = sem("oproj_added")
        s_hs = sem("hs_ready")
        s_xh = sem("xh_ready")
        s_n2hi = sem("n2_hi")
        s_n2lo = sem("n2_lo")
        s_int = sem("inter_ready")
        s_gel = sem("gelu_done")
        s_moe = sem("moe_copied")
        s_mtr = sem("moe_turned")
        s_fin = sem("fin_ready")
        s_out = [sem(f"out_stored{u}") for u in range(2)]

        SCORES = 3 + NHF * NG * NT * 2
        NS = NB * NHF * NE
        LAG = 3
        MOE_SUM = (4, 4, 5, 4)
        MOE_OUT = (19, 24, 30)
        OPROJ_AT = {8: (0, 2), 9: (4,), 10: (6,)}
        AH = dict(sums=1, add=3, out=(5, 8), turn=(14, 16), rows=(18, 19), tokens=22, exp=26, rw=29)
        CH = dict(out=1, x1=4, stats=6, power=8, norms=10, turn=9, normed=11, squares=11, rows=12, copy=13,
                  tokens=13, norm=14, direction=14, logits=15, exp=14, weights=15, rw=15, rpt=15, residual=24)
        MH = dict(norms=3, turn=5, normed=4, squares=5, rows=6, copy=7, tokens=8, norm=8, direction=6,
                  logits=9, exp=9, ranks=10, weights=12, rw=14, rpt=14)
        ring_jobs = []
        for m in range(NB * NHF):
            for e in range(NE):
                ring_jobs.append(("bc", m, e))
                if e == 3 and m:
                    ring_jobs.append(("v", m - 1, 0))
        RING = {j: n for n, j in enumerate(ring_jobs)}
        RING0, SCORE0, HEADS = 3, 5, 7
        OUT1 = ((7, 7), (5, 6))
        TURNED = (((7, 7), (5, 6)), ((0, 1), (5, 6)))
        LOGITS_T = (((7, 7), (5, 6)), ((0, 1), (5, 6)))
        LOGITS = ((7, 7), (2, 7))
        RW_TURNED = (7, 7, 2, 7)

        def op_bank(T, k):
            if T < PT:
                return 2 if k else T % 2
            return (4, 7)[T % 2] if k else 5 + T % 2


        ATT = {0: 14, 1: 15, 2: 18, 3: 19, 4: 21, 5: 23, 6: 26, 7: 27}
        T_IN = len(ATT)

        def place(T):
            m = T // TPH
            return m % NB, m // NB * TPH + T % TPH

        def tile_of(b, i):
            return (i // TPH * NB + b) * TPH + i % TPH

        def score_bank(T):
            if T < PT:
                return SCORE0 + T % 2
            return RING0 if T % 2 else SCORE0

        ptjobs = []
        for T in range(NB * NT):
            i = place(T)[1]
            for k0 in range(0, i + 1, 4):
                ptjobs.append((T, k0, min(4, i + 1 - k0)))

        def pt_until(T):
            return sum(1 for j in ptjobs if j[0] <= T)

        GR = 4 * NE

        def rows_of(c):
            return U[0:2 * GR, c * PT:(c + 1) * PT, :].rearrange("p i c -> p (i c)")

        def toks(c, b):
            return slice(c * S + b * HALF, c * S + (b + 1) * HALF)

        block = ctx.enter_context(nc.Block())

        @block.sync
        def _(sp):
            xv = x.rearrange("b (i p) c -> b p i c", p=P)
            for c in range(NHF):
                for b in range(NB):
                    m = c * NB + b
                    sp.dma_start(X[:, m * TPH:(m + 1) * TPH, :], xv[b, :, c * TPH:(c + 1) * TPH]).then_inc(s_x[c], 16)
                if c == 0:
                    for n, w in enumerate((Wq, Wk, Wv, Wo)):
                        sp.dma_start(wnat[:, n, :], w).then_inc(s_wnat, 16)

            for n, a in enumerate((ln1_w, ln1_b, ln2_w, ln2_b)):
                sp.dma_start(lncol[:, n:n + 1], a.rearrange("(p a) -> p a", a=1)).then_inc(s_rows_in, 16)
            for t, a in ((bv_row, bv), (bo_row, bo)):
                sp.dma_start(t[:, :], a.rearrange("(a c) -> a c", a=1).to_broadcast([P, P])).then_inc(s_rows_in, 16)
            for n, a in enumerate((smha_gates, moe_gates)):
                sp.dma_start(gates[:, n, :], a.rearrange("(a c) -> a c", a=1).to_broadcast([P, NE]))\
                    .then_inc(s_rows_in, 16)
            for n, a in enumerate((smha_sim, moe_sim)):
                sp.dma_start(sims[:, n, :], a).then_inc(s_rows_in, 16)

            def load_weight(n):
                if n >= 2:
                    sp.wait_ge(s_wsplit, n - 1)
                src = (q_proj, k_proj, v_proj, o_proj, w1, w2)[n]
                sp.dma_start(wraw[:, n % 2, :].rearrange("p (e n) -> p e n", e=NE),
                             src.rearrange("e c n -> c e n")).then_inc(s_wraw[n % 2], 16)

            load_weight(0)
            load_weight(1)
            def write_parts(n):
                t, c, b = SPLITS[n]
                sl = slice(c * HALF, (c + 1) * HALF)
                sp.wait_ge(s_split, n + 1)
                sp.dma_start(qk_parts[t, :, :, b, sl].rearrange("a r s -> r a s"), parts[:, t, :, b, sl])\
                    .then_inc(s_kd if t == K_ else s_qd[c], 16)

            def load_group(G, queries=range(len(PAIRS)), keys=range(len(PAIRS))):
                half, g = divmod(G, NG)
                if G >= 2:
                    sp.wait_ge(s_score, 16 * (G - 1))
                own = qk_parts[:, :, 32 * g:32 * g + 32].rearrange("t a (h d) b s -> t a (d b) h s", d=D)

                def load(ops, t, which, sl):
                    for r in which:
                        sp.dma_start(ops[r * R:(r + 1) * R, G % 2, :, :], own[t, PAIRS[r][t], :, :, sl])\
                            .then_inc(s_ops[G % 2], 16)

                load(ops_q, Q_, queries, slice(half * HALF, (half + 1) * HALF))
                load(ops_k, K_, keys, slice(0, S))

            for n in range(4):
                write_parts(n)
            sp.wait_ge(s_qd[0], 16 * 2)
            load_group(0, queries=range(0, 3), keys=())
            write_parts(4)
            load_group(0, queries=range(3, 6), keys=())
            write_parts(5)
            load_group(0, queries=range(6, 8), keys=())
            sp.wait_ge(s_kd, 16 * 4)
            load_group(0, queries=())
            load_group(1)
            for n in range(2, NW):
                load_weight(n)
            write_parts(6)
            write_parts(7)
            sp.wait_ge(s_qd[1], 16 * 2)
            for G in range(NHF * NG):
                if G + 2 < NHF * NG:
                    load_group(G + 2)
                sp.wait_ge(s_head, 2 + G + 1)
                half, g = divmod(G, NG)
                for j in range(GH):
                    for b in range(NB):
                        h = g * GH + j
                        sp.dma_start(HT[D * h:D * h + D, toks(half, b)],
                                     hout[32 * j + D * b:32 * j + D * b + D, G % 2, :]).then_inc(s_ht[G % 2], 16)
            ov = out.rearrange("b (i p) c -> b p i c", p=P)
            for m in range(NB * NHF):
                c, b = divmod(m, NB)
                sp.wait_ge(s_fin, m + 1)
                sp.dma_start(ov[b, :, c * TPH:(c + 1) * TPH, :],
                             fin[:, m * TPH:(m + 1) * TPH, :]).then_inc(s_out[m % 2], 16)
            for u in range(2):
                sp.wait_ge(s_out[u], 16 * NB * NHF // 2)

        @block.gpsimd
        def _(pool):
            pool.memset(ident[:, :], 0.0).then_inc(s_pool, 1)
            pool.memset(warm[:, :], 0.0).then_inc(s_const, 1)
            pool.memset(minus_half[:, :], -0.5).then_inc(s_pool, 1)
            pool.wait_ge(s_pool, 2)
            pool.affine_select(out=ident[:, :], in_=ident[:, :], compare_op=ALU.not_equal, fill=1.0,
                               base=0, pattern=[[-1, P]], channel_multiplier=1).then_inc(s_id, 1)
            pool.memset(ones[:, :], 1.0).then_inc(s_const, 1)
            pool.memset(start[:, 0:1], 0.0).then_inc(s_pair, 2)
            pool.memset(start[:, 1:2], 0.0).then_inc(s_head, 2)
            pool.memset(sims[:, 2:4, :], 0.0).then_inc(s_simz, 1)
            pool.memset(RPT[:, :, :], 0.0).then_inc(s_rptz, 1)
            pool.memset(before[:, :, :], 1.0).then_inc(s_pool, 1)
            pool.memset(maskb[:, :], 0.0).then_inc(s_pool, 1)
            pool.memset(spread[:, :, :], 0.0).then_inc(s_pool, 1)
            pool.memset(identb[:, :], 0.0).then_inc(s_pool, 1)
            pool.memset(vst[:, 0, :, :, :], 0.0).then_inc(s_const, 1)
            pool.memset(vst[:, 1, :, :, :], 0.0).then_inc(s_const, 1)

            def power(n, o, i):
                pool.wait_ge(s_powin, n)
                pool.tensor_tensor(o, i, minus_half[:, 0:i.shape[1]], ALU.pow).then_inc(s_pow, 1)

            def flat(t, b):
                return t[:, b].rearrange("p a i -> p (a i)")

            for b in range(NB):
                power(b + 1, powout[:, b, 0, :], powin[:, b, 0, :])
            def low_part(nq):
                t, c, b = SPLITS[nq]
                dst = parts[:, t, :, b, c * HALF:(c + 1) * HALF]
                pool.wait_ge(s_mid, nq + 1)
                pool.tensor_tensor(dst[:, 2, :], rest[:, nq % 2, :], dst[:, 1, :], ALU.subtract).then_inc(s_split, 1)

            for n in range(len(SPLITS)):
                low_part(n)
            pool.wait_ge(s_pool, 6)
            pool.affine_select(out=identb[:, :], in_=identb[:, :], compare_op=ALU.not_equal, fill=1.0,
                               base=0, pattern=[[-1, P]], channel_multiplier=1).then_inc(s_const, 1)
            pool.affine_select(out=maskb[:, :], in_=maskb[:, :], compare_op=ALU.is_ge, fill=MASKED,
                               base=0, pattern=[[-1, P]], channel_multiplier=1).then_inc(s_const, 1)
            pool.affine_select(out=before[:, :, :], in_=before[:, :, :], compare_op=ALU.is_gt, fill=0.0,
                               base=0, pattern=[[1, NE], [-1, NE]], channel_multiplier=0).then_inc(s_const, 1)
            for a in range(3):
                if a:
                    pool.wait_ge(s_pool, 6 + a)
                pool.affine_select(out=spread[:, :, :], in_=spread[:, :, :], compare_op=ALU.not_equal, fill=1.0,
                                   base=-NE * a, pattern=[[-1, NE], [0, P]], channel_multiplier=1)\
                    .then_inc(s_pool if a < 2 else s_const, 1)
            power(3, simrn[:, :], simn2[:, :])

            def residual(b):
                pool.wait_ge(s_y, b + 1)
                pool.wait_ge(s_o1, 4)
                for i in range(NT):
                    ins = pool.tensor_scalar(HS[:, b * NT + i, :], X[:, b * NT + i, :],
                                             powout[:, b, 0, i:i + 1], powin[:, b, 1, i:i + 1],
                                             ALU.mult, ALU.add)
                ins.then_inc(s_hs, 1)

            def direction(b, n):
                power(n, g1[:, 2 * b + 1, :], g1[:, 2 * b, :])

            def low(n):
                pool.wait_ge(s_shi, n + 1)
                if n >= 3:
                    pool.wait_ge(s_mm, n - 2)
                pool.tensor_tensor(slo[:, n % 3, :], sring[:, n % 3, :], shi[:, n % 3, :].bitcast(F32),
                                   ALU.subtract).then_inc(s_slo, 1)

            def add_scaled(T):
                pool.wait_ge(s_esc, T + 1)
                t = eterm(T)
                pool.tensor_tensor(t[:, 0:2, :], t[:, 0:2, :], t[:, 2:4, :], ALU.add).then_inc(s_pool2, 1)
                pool.wait_ge(s_pool2, 2 * T + 1)
                pool.tensor_tensor(t[:, 0, :], t[:, 0, :], t[:, 1, :], ALU.add).then_inc(s_pool2, 1)
                pool.wait_ge(s_pool2, 2 * T + 2)
                pool.wait_ge(s_acc, T + 1)
                pool.tensor_tensor(HS[:, T, :], HS[:, T, :], t[:, 0, :], ALU.add).then_inc(s_added, 1)

            def sum_residuals(b):
                pool.wait_ge(s_added, (b + 1) * NT)
                xb = X[:, b * NT:(b + 1) * NT, :]
                pool.tensor_tensor(xb, xb, HS[:, b * NT:(b + 1) * NT, :], ALU.add).then_inc(s_xh, 1)

            def n2_low():
                pool.wait_ge(s_n2hi, 1)
                sl = slice(0, S)
                pool.tensor_tensor(alo[:, sl], nT[:, sl], ahi[:, sl].bitcast(F32), ALU.subtract).then_inc(s_n2lo, 1)

            power(4, flat(powout, 0), flat(powin, 0))
            direction(0, 5)
            for n in range(NS):
                low(n)
                if n == CH["power"]:
                    power(6, flat(powout, 1), flat(powin, 1))
                if n == CH["direction"]:
                    direction(1, 7)
                if n == CH["residual"]:
                    residual(0)
                if n == CH["residual"] + 3:
                    residual(1)
            for T in range(PT):
                add_scaled(T)
            power(8, powout[:, 0, 0, :], powin[:, 0, 0, :])
            n2_low()
            direction(0, 9)
            for T in range(PT, NB * NT - 2):
                add_scaled(T)
            for n in range(NS):
                low(NS + n)
                if n == 0:
                    add_scaled(14)
                    add_scaled(15)
                if n == 1:
                    power(10, powout[:, 1, 0, :], powin[:, 1, 0, :])
                if n == MH["direction"]:
                    direction(1, 11)
                if n == 17:
                    sum_residuals(0)
                if n == 22:
                    sum_residuals(1)

        @block.scalar
        def _(act):
            act.dma_start(bcol[:, 0:1], bq.rearrange("(p a) -> p a", a=1)).then_inc(s_small, 16)
            act.dma_start(bcol[:, 1:2], bk.rearrange("(p a) -> p a", a=1)).then_inc(s_small, 16)
            act.dma_start(bcol[:, 2:3], bv.rearrange("(p a) -> p a", a=1)).then_inc(s_small, 16)
            act.wait_ge(s_const, 1)
            act.activation(warm[:, 1:2], warm[:, 0:1], ACT.Tanh).then_inc(s_tanh, 3)

            nq = 0
            for n, (what, b, h, e) in enumerate(JOBS):
                if e != "act":
                    continue
                act.wait_ge(s_job, n + 1)
                src = ps[:, n % 8, :]
                if what == "wT":
                    act.activation(wT[:, :, :].rearrange("p a b -> p (a b)"), src, ACT.Copy).then_inc(s_jact, 1)
                elif what == "xT":
                    act.activation(nT[:, toks(b, h)], src, ACT.Copy).then_inc(s_jact, 1)
                else:
                    t = Q_ if what == "q" else K_
                    c, b = b, h
                    sign = -1.0 if (t == K_ and b == 1) else 1.0
                    bias = bcol[:, 3:4] if sign < 0 else bcol[:, t:t + 1]
                    if nq == 0:
                        act.wait_ge(s_small, 16 * 3)
                    if nq >= 2:
                        act.wait_ge(s_rest, nq - 1)
                    if sign < 0 and c == 0:
                        act.wait_ge(s_sums, 1)
                    act.activation(q32[:, nq % 2, :], src, ACT.Identity, bias=bias, scale=sign)
                    act.activation(parts[:, t, 0, b, c * HALF:(c + 1) * HALF], src, ACT.Identity,
                                   bias=bias, scale=sign).then_inc(s_jact, 1)
                    nq += 1
            act.wait_ge(s_rows_in, 16 * 10)
            act.activation(gates[:, :, :].rearrange("p a b -> p (a b)"),
                           gates[:, :, :].rearrange("p a b -> p (a b)"), ACT.Tanh, scale=0.5).then_inc(s_gtan, 1)

            def tanh(i, scored, free):
                act.wait_ge(s_score, scored)
                if i % 2 == 0:
                    act.wait_ge(s_pair, free)
                act.activation(tanhs[:, i % 4, :, :].rearrange("p a b -> p (a b)"),
                               psf[:, (i % 3) * 1024:(i % 3) * 1024 + 1024],
                               ACT.Tanh, scale=0.5).then_inc(s_tanh, 1)

            def gate_tanh(part, c):
                act.wait_ge(s_gex, 2 * part + c + 1)
                act.activation(gt[:, c, 2, :, :], gt[:, c, 2, :, :], ACT.Tanh, scale=0.5).then_inc(s_gexo, 1)

            with act.Fori(0, NG // 2) as gg:
                for i in range(32):
                    tanh(i, 32 * gg + (i + 1), 16 * gg + (i // 2 + 1))
            for i in range(64):
                tanh(i, 64 + i + 1, 32 + i // 2 + 1)
                if i == 2 * AH["exp"]:
                    gate_tanh(0, 0)

            def normed(part, b):
                act.wait_ge(s_uT, 2 * (2 * part + b) + 2)
                k = TURNED[part][b][0]
                act.activation(nT[:, b * S:(b + 1) * S], psf[:, k * 512:k * 512 + S], ACT.Identity,
                               bias=lncol[:, 2 * part + 1:2 * part + 2],
                               scale=lncol[:, 2 * part:2 * part + 1]).then_inc(s_nT, 1)

            def squares(part, b):
                act.wait_ge(s_nT, 2 * part + b)
                act.activation(SQ[:, 0:S], nT[:, b * S:(b + 1) * S], ACT.Square).then_inc(s_sq, 1)

            def n2_high(b):
                act.activation(ahi[:, b * S:(b + 1) * S], nT[:, b * S:(b + 1) * S], ACT.Copy).then_inc(s_n2hi, 1)

            def high(n):
                act.wait_ge(s_s, n + 1)
                if n >= 3:
                    act.wait_ge(s_mm, n - 2)
                act.activation(shi[:, n % 3, :], sring[:, n % 3, :], ACT.Copy).then_inc(s_shi, 1)

            def exps(T):
                i = place(T)[1]
                act.wait_ge(s_nb, T + 1)
                if T >= 2:
                    act.wait_ge(s_ptm, pt_until(T - 2))
                col = score_bank(T) * 512
                act.activation(prob[:, T % 2, 0:(i + 1) * P], psf[:, col:col + (i + 1) * P],
                               ACT.Exp, bias=mx[:, 1, T:T + 1], scale=SMAX_SCALE,
                               accum_out=rowsum[:, T:T + 1]).then_inc(s_exp, 1)

            def copies(T):
                for n, (T_, k0, nk) in enumerate(ptjobs):
                    if T_ != T:
                        continue
                    act.wait_ge(s_ptm, n + 1)
                    if T >= 4 and k0 == 0:
                        act.wait_ge(s_av, T // 2 - 1)
                    act.activation(probT[:, T // 2 % 2, k0:k0 + nk, T % 2, :],
                                   ps[:, score_bank(T) + k0 // 4, 0:nk * P].rearrange("p (a b) -> p a b", b=P),
                                   ACT.Copy).then_inc(s_pt, 1)

            def attn_hi(q):
                act.wait_ge(s_av, 2 * q + 2)
                act.activation(ahi[:, q * HALF:(q + 1) * HALF], ps[:, HEADS, :], ACT.Copy).then_inc(s_ahi, 1)

            def take_qk(m):
                for k, t in enumerate((qT, kT)):
                    act.wait_ge(s_qksum, 2 * m + k + 1)
                    act.activation(t[:, m, :], ps[:, k, :], ACT.Copy).then_inc(s_qk, 1)

            for n in range(NS):
                m, e = divmod(n, NE)
                high(n)
                if e == 0 and m:
                    take_qk(m - 1)
                if n == CH["normed"]:
                    normed(0, 1)
                if n == CH["squares"]:
                    squares(0, 1)
                if n == CH["exp"]:
                    gate_tanh(0, 1)
                for T in range(T_IN):
                    if n == ATT[T] + 4:
                        copies(T)
                    if n == ATT[T] + 2:
                        exps(T)
                if n == ATT[3] + 6:
                    attn_hi(0)
            take_qk(NB * NHF - 1)

            def scale_experts(T):
                b, i = divmod(T, NT)
                act.wait_ge(s_rwn, b + 1)
                act.wait_ge(s_op2, T + 1)
                if T >= 2:
                    act.wait_ge(s_added, T - 1)
                for e in range(NE // 2):
                    ins = act.activation(eterm(T)[:, e, :], ps[:, op_bank(T, 1), e * P:(e + 1) * P], ACT.Copy,
                                         scale=rwn[:, b, i, NE // 2 + e:NE // 2 + e + 1])
                ins.then_inc(s_esc, 1)

            exps(T_IN)
            for T in range(T_IN, NB * NT):
                if T + 1 < NB * NT:
                    exps(T + 1)
                copies(T)
                if T % 4 == 0:
                    attn_hi(T // 4 - 1)
                for t in OPROJ_AT.get(T, ()):
                    scale_experts(t)
                    scale_experts(t + 1)
                if T == 13:
                    normed(1, 0)
                    squares(1, 0)
                if T == 14:
                    n2_high(0)
            attn_hi(3)
            scale_experts(8)
            scale_experts(9)
            gate_tanh(1, 0)
            scale_experts(10)
            scale_experts(11)

            def gelu(n):
                act.wait_ge(s_int, n + 1)
                if n >= 2:
                    act.wait_ge(s_s, NS + n - 1)
                act.activation(gel[:, n % 2, :], ps[:, n % 2, :], ACT.Gelu).then_inc(s_gel, 1)

            act.wait_ge(s_added, PT)
            gelu(0)
            scale_experts(12)
            scale_experts(13)
            for n in range(NS):
                if n + 1 < NS:
                    gelu(n + 1)
                high(NS + n)
                if n == 0:
                    scale_experts(14)
                    scale_experts(15)
                if n == MH["normed"]:
                    normed(1, 1)
                if n == MH["squares"]:
                    squares(1, 1)
                    n2_high(1)
                if n == MH["exp"]:
                    gate_tanh(1, 1)

        @block.vector
        def _(dve):
            steps = [0]

            def link(ins):
                steps[0] += 1
                ins.then_inc(s_dve, 1)
                dve.wait_ge(s_dve, steps[0])

            def statistics(src, b):
                for i in range(NT):
                    last = dve.bn_stats(stats[:, b * NT + i, :], src[:, b * NT + i, :])
                link(last)
                for i in range(NT):
                    last = dve.bn_aggr(mv[:, b * NT + i, :], stats[:, b * NT + i, :])
                link(last)
                return mv[:, b * NT:(b + 1) * NT, 0], mv[:, b * NT:(b + 1) * NT, 1]

            def first_statistics(b):
                dve.wait_ge(s_x[b], 32)
                m_, v_ = statistics(X, b)
                dve.tensor_scalar(powin[:, b, 0, :], v_, EPS, None, ALU.add).then_inc(s_powin, 1)

            def normalise(b, r, sem_, only=None):
                for i in range(PT) if only is None else range(only * TPH, (only + 1) * TPH):
                    last = dve.tensor_scalar(U[:, b * NT + i, :], X[:, b * NT + i, :], mv[:, b * NT + i, 0:1],
                                             r[:, i:i + 1], ALU.subtract, ALU.mult)
                last.then_inc(sem_, 1)

            def empty(n, fn):
                dve.wait_ge(s_job, n + 1)
                fn(ps[:, n % 8, :]).then_inc(s_jdve, 1)

            def split_rest(nq):
                t, c, b = SPLITS[nq]
                dst = parts[:, t, :, b, c * HALF:(c + 1) * HALF]
                n = JOB[("qk"[t], c, b)]
                dve.wait_ge(s_jact, emptied(n)[1])
                if nq >= 2:
                    dve.wait_ge(s_split, nq - 1)
                ins = dve.tensor_tensor(rest[:, nq % 2, :], q32[:, nq % 2, :], dst[:, 0, :], ALU.subtract)
                ins.then_inc(s_rest, 1)
                dve.wait_ge(s_rest, nq + 1)
                dve.tensor_copy(dst[:, 1, :], rest[:, nq % 2, :]).then_inc(s_mid, 1)

            first_statistics(0)
            dve.wait_ge(s_pow, 1)
            for b in range(NB):
                normalise(0, powout[:, 0, 0, :], s_xn, b)
            first_statistics(1)
            dve.wait_ge(s_small, 16 * 3)
            dve.tensor_scalar(bcol[:, 3:4], bcol[:, 1:2], -1.0, None, ALU.mult).then_inc(s_sums, 1)
            split_rest(0)
            dve.wait_ge(s_pow, 2)
            for b in range(NB):
                normalise(1, powout[:, 1, 0, :], s_xn, b)
            split_rest(1)
            empty(JOB[("xT", 1, 0)], lambda src: dve.tensor_copy(nT[:, toks(1, 0)], src))
            empty(JOB[("xT", 1, 1)], lambda src: dve.tensor_copy(nT[:, toks(1, 1)], src))
            for n in range(2, 6):
                split_rest(n)

            dve.wait_ge(s_rows_in, 16 * 10)
            link(dve.tensor_scalar(cvecb[:, 0, :], bv_row[:, :], 0.5, None, ALU.mult))
            link(dve.tensor_scalar(cvecb[:, 1, :], bv_row[:, :], -0.5, None, ALU.mult))
            for c in range(NHF):
                for b in range(NB):
                    n = JOB[("v", c, b)]
                    dve.wait_ge(s_job, n + 1)
                    for k in range(TPH):
                        last = dve.scalar_tensor_tensor(
                            out=VP[:, c * TPH + k, :, b * D:(b + 1) * D],
                            in0=ps[:, n % 8, k * P:(k + 1) * P].rearrange("p (h d) -> p h d", d=D),
                            scalar=0.5 if b == 0 else -0.5,
                            in1=cvecb[:, b, :].rearrange("p (h d) -> p h d", d=D), op0=ALU.mult, op1=ALU.add)
                    last.then_inc(s_jdve, 1)
            jd = emptied(JOB[("v", 1, 1)])[1]
            dve.wait_ge(s_jdve, jd)
            dve.wait_ge(s_const, 4)
            def stage_v(G):
                if G >= 2:
                    dve.wait_ge(s_pair, 2 + NT * (G - 1))
                g = G % NG
                dve.tensor_copy(vst[:, G % 2, :, :, 0:R], VP[:, :, g * GH:(g + 1) * GH, :]).then_inc(s_vst, 1)

            stage_v(0)
            stage_v(1)
            split_rest(6)
            split_rest(7)

            link(dve.tensor_tensor(simsq[:, :], sims[:, 0:2, :].rearrange("p a b -> p (a b)"),
                                   sims[:, 0:2, :].rearrange("p a b -> p (a b)"), ALU.mult))
            dve.wait_ge(s_jact, emptied(JOB[("xT", 0, 1)])[1])
            link(dve.tensor_reduce(sumq[:, :], nT[:, :].rearrange("p (m s) -> p m s", s=HALF), AX.X, ALU.add))
            dve.tensor_tensor(sumx[:, :], sumq[:, 0:NB], sumq[:, NB:2 * NB], ALU.add).then_inc(s_sums, 1)
            def batch_sums():
                dve.wait_ge(s_sumd, 1)
                dve.tensor_scalar(simn2[:, :], ps[:, 7, 0:2 * NE], 1e-24, None, ALU.max).then_inc(s_powin, 1)
                link(dve.tensor_scalar(cvec[:, :], ps[:, 7, 2 * NE:2 * NE + NB], 0.5, None, ALU.mult))
                link(dve.tensor_scalar(tmp8[:, 0, 0:1], bcol[:, 2:3], 0.5 * S, None, ALU.mult))
                link(dve.tensor_tensor(cvec[:, :], cvec[:, :], tmp8[:, 0, 0:1].to_broadcast([P, NB]), ALU.add))
                for b in range(NB):
                    last = dve.tensor_scalar(cvecb[:, b, :], ones[:, :], cvec[:, b:b + 1], None, ALU.mult)
                last.then_inc(s_cvec, 1)

            def add_rows():
                dve.wait_ge(s_addrow, 1)
                for b in range(NB):
                    last = dve.tensor_tensor(row_add[:, b, :], ps[:, 7, b * P:(b + 1) * P], bo_row[:, :], ALU.add)
                last.then_inc(s_rowadd, 1)
                dve.wait_ge(s_rowadd, 1)
                for m in range(NB * NHF):
                    b = m % NB
                    xb = X[:, m * TPH:(m + 1) * TPH, :]
                    last = dve.tensor_tensor(xb, xb, row_add[:, b:b + 1, :].to_broadcast([P, TPH, P]), ALU.add)
                link(last)
                dve.wait_ge(s_pow, 3)
                link(dve.tensor_tensor(sims[:, 0:2, :].rearrange("p a b -> p (a b)"),
                                       sims[:, 0:2, :].rearrange("p a b -> p (a b)"), simrn[:, :], ALU.mult))

            dve.wait_ge(s_gtan, 1)
            link(dve.tensor_scalar(gates[:, :, :], gates[:, :, :], 0.5, 0.5, ALU.mult, ALU.add))

            def split_weight(n):
                dve.wait_ge(s_wraw[n % 2], 16 * (n // 2 + 1))
                link(dve.tensor_copy(whi[:, n, :], wraw[:, n % 2, :]))
                dve.tensor_tensor(wlo[:, n, :], wraw[:, n % 2, :], whi[:, n, :].bitcast(F32),
                                  ALU.subtract).then_inc(s_wsplit, 1)

            for n in range(NW):
                split_weight(n)
            def take_heads(G):
                if G >= 2:
                    dve.wait_ge(s_ht[G % 2], 16 * GH * NB * (G // 2))
                dve.wait_ge(s_pair, 2 + NT * (G + 1))
                dve.tensor_copy(hout[:, G % 2, :], ps[:, 6 + (G % 2 if G < NG else 0), :]).then_inc(s_head, 1)
                if G + 2 < NHF * NG:
                    stage_v(G + 2)

            def add_x1(c):
                for b in range(NB):
                    m = c * NB + b
                    dve.wait_ge(s_o1, m + 1)
                    xb = X[:, m * TPH:(m + 1) * TPH, :].rearrange("p a b -> p (a b)")
                    dve.tensor_tensor(xb, ps[:, OUT1[c][b], :], xb, ALU.add).then_inc(s_x1, 1)

            def x1_statistics(b):
                dve.wait_ge(s_x1, NB * (b + 1))
                m_, v_ = statistics(X, b)
                link(dve.tensor_scalar(powin[:, b, 0, :], v_, EPS, None, ALU.add))
                link(dve.reciprocal(tmp8[:, 0, :], powin[:, b, 0, :]))
                link(dve.tensor_tensor(tmp8[:, 1, :], tmp8[:, 0, :], v_, ALU.mult))
                dve.tensor_scalar(powin[:, b, 1, :], tmp8[:, 1, :], EPS, None, ALU.add).then_inc(s_powin, 1)

            def x1_norms(b):
                dve.wait_ge(s_pow, 4 + 2 * b)
                link(dve.tensor_tensor(tmp8[:, 2 + b, :], powout[:, b, 0, :], powout[:, b, 1, :], ALU.mult))
                dve.scalar_tensor_tensor(out=powin[:, b, 1, :], in0=mv[:, b * NT:(b + 1) * NT, 0], scalar=-1.0,
                                         in1=powout[:, b, 0, :], op0=ALU.mult, op1=ALU.mult).then_inc(s_y, 1)
                normalise(b, tmp8[:, 2 + b, :], s_u)

            def normed_early(b):
                dve.wait_ge(s_uT, b + 1)
                dve.tensor_scalar(nT[:, toks(0, b)], ps[:, 7, :], lncol[:, 0:1], lncol[:, 1:2],
                                  ALU.mult, ALU.add).then_inc(s_nTe, 1)
                dve.wait_ge(s_nTe, b + 1)
                sl = toks(0, b)
                dve.tensor_tensor(SQ[:, sl], nT[:, sl], nT[:, sl], ALU.mult).then_inc(s_sqe, 1)

            full = [P, NT, NE]

            def wide(t):
                return t.unsqueeze(2).to_broadcast(full)

            def copy_rows(part, c, b):
                k = 2 * (2 * part + c) + b
                dve.wait_ge(s_rows, k + 1)
                dve.tensor_copy(rows_of(c)[:, b * HALF:(b + 1) * HALF],
                                ps[0:2 * GR, LOGITS_T[part][c][b], :]).then_inc(s_rowsc, 1)

            def gate_norm(part, b):
                dve.wait_ge(s_log, 2 * part + b + 1)
                L = ps[:, LOGITS[part][b], :].rearrange("p (i e) -> p i e", e=2 * GR)
                dve.tensor_scalar(g1[:, 2 * b, :], L[:, :, GR], 1e-24, None, ALU.max).then_inc(s_powin, 1)

            def gate_logits(part, b, npow):
                lg, gr, ex = gt[:, b, 0, :, :], gt[:, b, 1, :, :], gt[:, b, 2, :, :]
                L = ps[:, LOGITS[part][b], :].rearrange("p (i e) -> p i e", e=2 * GR)[:, :, part * NE:(part + 1) * NE]
                dve.wait_ge(s_pow, npow)
                link(dve.tensor_tensor(lg, L, wide(g1[:, 2 * b + 1, :]), ALU.mult))
                link(dve.tensor_tensor(lg, lg, gates[:, part:part + 1, :].to_broadcast(full), ALU.subtract))
                link(dve.tensor_scalar(gr, lg, 0.0, None, ALU.max))
                link(dve.tensor_reduce(g1[:, 4, :], gr, AX.X, ALU.max))
                dve.tensor_tensor(ex, gr, wide(g1[:, 4, :]), ALU.subtract).then_inc(s_gex, 1)
                others = lg.unsqueeze(2).to_broadcast([P, NT, NE, NE])
                own = lg.unsqueeze(3).to_broadcast([P, NT, NE, NE])
                dve.tensor_tensor(cmp_[:, 0], others, own, ALU.is_gt)
                link(dve.tensor_tensor(cmp_[:, 1], others, own, ALU.is_equal))

            def gate_ranks(b):
                lg, gr, ss = gt[:, b, 0, :, :], gt[:, b, 1, :, :], g1[:, 5, :]
                link(dve.tensor_tensor(cmp_[:, 1], cmp_[:, 1],
                                       before[:, :, :].unsqueeze(1).to_broadcast([P, NT, NE, NE]), ALU.mult))
                link(dve.tensor_tensor(cmp_[:, 0], cmp_[:, 0], cmp_[:, 1], ALU.add))
                link(dve.tensor_reduce(lg, cmp_[:, 0], AX.X, ALU.add))
                link(dve.tensor_scalar(ss, g1[:, 4, :], 0.0, None, ALU.is_le))
                link(dve.scalar_tensor_tensor(out=lg, in0=lg, scalar=2.0, in1=wide(ss), op0=ALU.is_lt, op1=ALU.mult))
                link(dve.scalar_tensor_tensor(out=lg, in0=gr, scalar=0.0, in1=lg, op0=ALU.is_gt, op1=ALU.max))

            def gate_weights(part, b):
                lg, ex, ss = gt[:, b, 0, :, :], gt[:, b, 2, :, :], g1[:, 5, :]
                dve.wait_ge(s_gexo, 2 * part + b + 1)
                om = gt[:, b, 1, :, :]
                link(dve.tensor_scalar(om, ex, -1.0, 1.0, ALU.mult, ALU.add))
                link(dve.reciprocal(om, om))
                link(dve.scalar_tensor_tensor(out=ex, in0=ex, scalar=1.0, in1=om, op0=ALU.add, op1=ALU.mult))
                link(dve.tensor_tensor(ex, ex, lg, ALU.mult))
                link(dve.tensor_reduce(ss, ex, AX.X, ALU.add))
                link(dve.reciprocal(ss, ss))
                r = rw[:, b, :, :]
                link(dve.tensor_tensor(r, ex, wide(ss), ALU.mult))
                rp = RP[:, b, :, :]
                link(dve.tensor_copy(rp[:, :, 0:NE], r))
                link(dve.tensor_tensor(lg, r, rp[:, :, 0:NE], ALU.subtract))
                link(dve.tensor_copy(rp[:, :, NE:2 * NE], lg))
                dve.tensor_tensor(rp[:, :, 2 * NE:3 * NE], lg, rp[:, :, NE:2 * NE], ALU.subtract).then_inc(s_rp, 1)

            def rpt_copy(n, b):
                dve.wait_ge(s_rpT, n)
                dve.tensor_copy(RPT[0:3 * NE, b, :], ps[0:3 * NE, RW_TURNED[n - 1], :].bitcast(BF16))\
                    .then_inc(s_rpt, 1)

            for G in range(NG):
                take_heads(G)
            batch_sums()
            add_rows()
            add_x1(0)
            take_heads(4)
            x1_statistics(0)
            x1_norms(0)
            for b in range(NB):
                normed_early(b)
            take_heads(5)
            for b in range(NB):
                copy_rows(0, 0, b)
            gate_norm(0, 0)
            take_heads(6)
            gate_logits(0, 0, 5)
            gate_ranks(0)
            gate_weights(0, 0)
            dve.wait_ge(s_rptz, 1)
            rpt_copy(1, 0)
            take_heads(7)

            def maxima(T):
                i = place(T)[1]
                col = score_bank(T) * 512
                dve.wait_ge(s_S, T + 1)
                link(dve.tensor_reduce(mx[:, 0, T:T + 1], psf[:, col:col + (i + 1) * P], AX.X, ALU.max))
                dve.tensor_scalar(mx[:, 1, T:T + 1], mx[:, 0, T:T + 1], -SMAX_SCALE, None,
                                  ALU.mult).then_inc(s_nb, 1)

            def attn_low(q):
                dve.wait_ge(s_ahi, q + 1)
                sl = slice(q * HALF, (q + 1) * HALF)
                dve.tensor_tensor(alo[:, sl], ps[:, HEADS, :], ahi[:, sl].bitcast(F32),
                                  ALU.subtract).then_inc(s_alo, 1)

            def take_v(m):
                dve.wait_ge(s_mm, (m + 1) * NE)
                if m >= 2:
                    dve.wait_ge(s_vtr, m - 1)
                dve.tensor_copy(vT[:, m % 2, :], ps[:, 2, :]).then_inc(s_vT, 1)

            for r, (kind, m, e) in enumerate(ring_jobs):
                if kind == "v":
                    dve.wait_ge(s_vtr, m + 1)
                    dve.tensor_copy(V[:, m * TPH:(m + 1) * TPH, :].rearrange("p a b -> p (a b)"),
                                    ps[:, RING0 + r % 2, :]).then_inc(s_v, 1)
                    continue
                n = m * NE + e
                b, hf = divmod(m, NHF)
                dve.wait_ge(s_bc, n + 1)
                if n >= 3:
                    dve.wait_ge(s_slo, n - 2)
                dve.tensor_tensor(sring[:, n % 3, :], ps[:, RING0 + r % 2, :], nT[:, toks(b, hf)],
                                  ALU.mult).then_inc(s_s, 1)
                if e == 1 and m:
                    take_v(m - 1)
                if n == CH["x1"]:
                    add_x1(1)
                if n == CH["stats"]:
                    x1_statistics(1)
                if n == CH["norms"]:
                    x1_norms(1)
                if n == CH["copy"]:
                    for k in range(NB):
                        copy_rows(0, 1, k)
                if n == CH["norm"]:
                    gate_norm(0, 1)
                if n == CH["logits"]:
                    gate_logits(0, 1, 7)
                    gate_ranks(1)
                    gate_weights(0, 1)
                    rpt_copy(2, 1)
                for T in range(T_IN):
                    if n == ATT[T] + 2:
                        maxima(T)
                if n == ATT[3] + 7:
                    attn_low(0)
            m = NB * NHF - 1
            take_v(m)
            dve.wait_ge(s_vtr, m + 1)
            dve.tensor_copy(V[:, m * TPH:(m + 1) * TPH, :].rearrange("p a b -> p (a b)"), ps[:, 2, :]).then_inc(s_v, 1)

            def gates_over_rowsum(b):
                dve.wait_ge(s_exp, (b + 1) * NT)
                own = rowsum[:, b * NT:(b + 1) * NT]
                link(dve.reciprocal(own, own))
                dve.tensor_tensor(rwn[:, b], rw[:, b], own.unsqueeze(2).to_broadcast([P, NT, NE]),
                                  ALU.mult).then_inc(s_rwn, 1)
                dve.wait_ge(s_rwn, b + 1)

            def add_experts(T):
                dve.wait_ge(s_op, T + 2)
                for e in range(NE // 2):
                    for t in (T, T + 1):
                        if e:
                            dve.wait_ge(s_dve, steps[0] - (0 if t > T and e == NE // 2 - 1 else 1))
                        b, i = divmod(t, NT)
                        ins = dve.scalar_tensor_tensor(out=HS[:, t, :], in0=ps[:, op_bank(t, 0), e * P:(e + 1) * P],
                                                       scalar=rwn[:, b, i, e:e + 1], in1=HS[:, t, :],
                                                       op0=ALU.mult, op1=ALU.add)
                        if e < NE // 2 - 1:
                            ins.then_inc(s_dve, 1)
                            steps[0] += 1
                        else:
                            ins.then_inc(s_acc, 1)

            def second_statistics(b):
                dve.wait_ge(s_added, (b + 1) * NT)
                m_, v_ = statistics(HS, b)
                dve.tensor_scalar(powin[:, b, 0, :], v_, EPS, None, ALU.add).then_inc(s_powin, 1)

            def second_norm(b, npow):
                dve.wait_ge(s_pow, npow)
                for i in range(NT):
                    last = dve.tensor_scalar(U[:, b * NT + i, :], HS[:, b * NT + i, :], mv[:, b * NT + i, 0:1],
                                             powout[:, b, 0, i:i + 1], ALU.subtract, ALU.mult)
                last.then_inc(s_u, 1)

            dve.wait_ge(s_hs, 2)
            for T in range(T_IN, NB * NT):
                maxima(T)
                if T == 8:
                    gates_over_rowsum(0)
                if T == 13:
                    second_norm(0, 8)
                if T % 4 == 1:
                    attn_low(T // 4 - 1)
                for t in OPROJ_AT.get(T - 1, ()):
                    add_experts(t)
                if T == 12:
                    second_statistics(0)
                if T == 15:
                    for b in range(NB):
                        copy_rows(1, 0, b)
            gate_norm(1, 0)
            attn_low(3)
            gates_over_rowsum(1)
            gate_logits(1, 0, 9)
            add_experts(8)
            gate_ranks(0)
            gate_weights(1, 0)
            add_experts(10)
            rpt_copy(3, 0)
            add_experts(12)

            def moe_end(m):
                dve.wait_ge(s_mm, NS + (m + 1) * NE)
                dve.tensor_copy(moeT[:, m % 2, :], ps[:, MOE_SUM[m], :]).then_inc(s_moe, 1)

            def moe_out(m):
                dve.wait_ge(s_mtr, m + 1)
                dve.wait_ge(s_xh, m // NHF + 1)
                dve.tensor_tensor(fin[:, m * TPH:(m + 1) * TPH, :].rearrange("p a b -> p (a b)"), ps[:, 7, :],
                                  X[:, m * TPH:(m + 1) * TPH, :].rearrange("p a b -> p (a b)"),
                                  ALU.add).then_inc(s_fin, 1)

            for n in range(NS):
                m, e = divmod(n, NE)
                dve.wait_ge(s_bc, NS + n + 1)
                dve.wait_ge(s_gel, n + 1)
                if n >= 3:
                    dve.wait_ge(s_slo, NS + n - 2)
                dve.tensor_tensor(sring[:, (NS + n) % 3, :], ps[:, 2 + n % 2, :], gel[:, n % 2, :],
                                  ALU.mult).then_inc(s_s, 1)
                if n == 0:
                    add_experts(14)
                if n == 1:
                    second_statistics(1)
                if n == MH["norms"]:
                    second_norm(1, 10)
                if n == MH["copy"]:
                    for k in range(NB):
                        copy_rows(1, 1, k)
                if n == MH["norm"]:
                    gate_norm(1, 1)
                    dve.wait_ge(s_n2hi, 2)
                    sl = slice(S, 2 * S)
                    dve.tensor_tensor(alo[:, sl], nT[:, sl], ahi[:, sl].bitcast(F32), ALU.subtract).then_inc(s_n2lo, 1)
                if n == MH["logits"]:
                    gate_logits(1, 1, 11)
                if n == MH["ranks"]:
                    gate_ranks(1)
                if n == MH["weights"]:
                    gate_weights(1, 1)
                if n == MH["rpt"]:
                    rpt_copy(4, 1)
                if e == LAG and m:
                    moe_end(m - 1)
                if n in MOE_OUT:
                    moe_out(MOE_OUT.index(n))
            moe_end(NB * NHF - 1)
            moe_out(NB * NHF - 1)

        @block.tensor
        def _(pe):
            def three_pass(o, wh, wl, xh, xl, start, stop):
                pe.matmul(o, wh, xh, start=start, stop=False)
                pe.matmul(o, wl, xh, start=False, stop=False)
                return pe.matmul(o, wh, xl, start=False, stop=stop)

            pe.wait_ge(s_id, 1)
            for n, (what, b, h, e) in enumerate(JOBS):
                if n >= 8:
                    eng, cnt = emptied(n - 8)
                    pe.wait_ge(s_jact if eng == "act" else s_jdve, cnt)
                bank = ps[:, n % 8, :]
                if what == "wT":
                    pe.wait_ge(s_wnat, 64)
                    for k in range(4):
                        last = pe.transpose(bank[:, k * P:(k + 1) * P], wnat[:, k, :], ident[:, :])
                elif what == "xT":
                    pe.wait_ge(s_xn, 2 * b + h + 1)
                    for k in range(TPH):
                        last = pe.transpose(bank[:, k * P:(k + 1) * P], U[:, b * NT + h * TPH + k, :], ident[:, :])
                elif what in "qk":
                    eng, cnt = emptied(JOB[("xT", b, h)])
                    pe.wait_ge(s_jact if eng == "act" else s_jdve, cnt)
                    last = pe.matmul(bank, wT[:, "qk".index(what), :], nT[:, toks(b, h)], start=True, stop=True)
                elif what == "v":
                    for k in range(TPH):
                        t0 = (b * NB + h) * HALF + k * P
                        last = pe.matmul(bank[:, k * P:(k + 1) * P], nT[:, t0:t0 + P], wT[:, 2, :],
                                         start=True, stop=True)
                last.then_inc(s_job, 1)
            pe.wait_ge(s_jact, sum(1 for j in JOBS if j[3] == "act"))
            pe.wait_ge(s_jdve, sum(1 for j in JOBS if j[3] == "dve"))

            def scores(i, slot, kc, pair):
                for j in range(2):
                    h = 2 * pair + j
                    col = (i % 3) * 1024 + j * 512
                    last = pe.matmul(psf[:, col:col + 512], ops_k[:, slot, h, kc * P:(kc + 1) * P],
                                     ops_q[:, slot, h, :], start=True, stop=True)
                last.then_inc(s_score, 1)

            def heads(k, slot, bank):
                kc = k % NT
                for j in range(GH):
                    last = pe.matmul(ps[32 * j:32 * j + 32, bank, :], vst[:, slot, kc, j, :],
                                     tanhs[:, (2 * k + j // 2) % 4, j % 2, :], start=(kc == 0), stop=(kc == NT - 1))
                last.then_inc(s_pair, 1)

            with pe.Fori(0, NG // 2) as gg:
                def loop_heads(k):
                    u = k // NT
                    if k % NT == 0:
                        pe.wait_ge(s_head, 2 * gg + (u + 1))
                    pe.wait_ge(s_tanh, 32 * gg + (3 + 2 * k + 2))
                    heads(k, u, 6 + u)

                for k in range(2 * NT):
                    u = k // NT
                    if k % NT == 0:
                        pe.wait_ge(s_ops[u], 16 * OP_DMAS * gg + 16 * OP_DMAS)
                    for i in (2 * k, 2 * k + 1):
                        if i == 0:
                            pe.wait_ge(s_tanh, 32 * gg + 3)
                        elif i >= 3:
                            pe.wait_ge(s_tanh, 32 * gg + (i + 1))
                        scores(i, u, k % NT, i % 2)
                    if k % NT == 1:
                        pe.wait_ge(s_vst, 2 * gg + (u + 1))
                    if k:
                        loop_heads(k - 1)
                loop_heads(2 * NT - 1)

            def out_one(c, b):
                for i in range(TPH):
                    t0 = (c * NB + b) * HALF + i * P
                    last = pe.matmul(ps[:, OUT1[c][b], i * P:(i + 1) * P], HT[:, t0:t0 + P], wT[:, 3, :],
                                     start=True, stop=True)
                last.then_inc(s_o1, 1)

            def turn_u(part, c, b):
                pe.wait_ge(s_u, 2 * part + c + 1)
                for i in range(TPH):
                    last = pe.transpose(ps[:, TURNED[part][c][b], i * P:(i + 1) * P],
                                        U[:, c * PT + b * TPH + i, :], ident[:, :])
                last.then_inc(s_uT, 1)

            def logit_rows(part, c, b):
                bank = LOGITS_T[part][c][b]
                pe.matmul(ps[0:GR, bank, :], sims[:, :, :].rearrange("p a b -> p (a b)"), nT[:, toks(c, b)],
                          start=True, stop=True)
                pe.matmul(ps[GR:2 * GR, bank, :], ones[:, 0:GR], SQ[:, b * HALF:(b + 1) * HALF],
                          start=True, stop=True).then_inc(s_rows, 1)

            def logits(part, c):
                pe.wait_ge(s_rowsc, 2 * (2 * part + c) + 2)
                for i in range(PT):
                    last = pe.transpose(ps[:, LOGITS[part][c], i * 2 * GR:(i + 1) * 2 * GR],
                                        rows_of(c)[:, i * P:(i + 1) * P], ident[0:2 * GR, 0:2 * GR])
                last.then_inc(s_log, 1)

            def turn_rw(n, c):
                pe.wait_ge(s_rp, n)
                for i in range(PT):
                    last = pe.transpose(ps[0:3 * NE, RW_TURNED[n - 1], :].bitcast(BF16)[:, i * P:(i + 1) * P],
                                        RP[:, c, i, :], identb[:, :])
                last.then_inc(s_rpT, 1)

            def late_heads(k):
                if k == 0:
                    pe.wait_ge(s_head, 2 + NG - 1)
                elif k % NT == 0:
                    pe.wait_ge(s_head, 2 + NG + k // NT)
                pe.wait_ge(s_tanh, 64 + 3 + 2 * k + 2)
                heads(k, k // NT % 2, 6)

            for k in range(NG * NT):
                G = NG + k // NT
                if k % NT == 0:
                    pe.wait_ge(s_ops[G % 2], 16 * OP_DMAS * (G // 2 + 1))
                for i in (2 * k, 2 * k + 1):
                    if i == 0:
                        pe.wait_ge(s_tanh, 64 + 3)
                    elif i >= 3:
                        pe.wait_ge(s_tanh, 64 + i + 1)
                    scores(i, G % 2, k % NT, i % 2)
                if k % NT == 1:
                    pe.wait_ge(s_vst, G + 1)
                if k:
                    late_heads(k - 1)
                if k == AH["sums"]:
                    pe.wait_ge(s_head, 2 + NG)
                    pe.wait_ge(s_sums, 2)
                    pe.wait_ge(s_const, 2)
                    pe.matmul(ps[:, 7, 0:2 * NE], ones[:, :], simsq[:, :], start=True, stop=True)
                    pe.matmul(ps[:, 7, 2 * NE:2 * NE + NB], wT[:, 2, :], sumx[:, :],
                              start=True, stop=True).then_inc(s_sumd, 1)
                if k == AH["add"]:
                    pe.wait_ge(s_cvec, 1)
                    for b in range(NB):
                        last = pe.matmul(ps[:, 7, b * P:(b + 1) * P], cvecb[:, b, :], wT[:, 3, :],
                                         start=True, stop=True)
                    last.then_inc(s_addrow, 1)
                if k == AH["out"][0]:
                    pe.wait_ge(s_rowadd, 1)
                    for u in range(2):
                        pe.wait_ge(s_ht[u], 16 * GH * NB * 2)
                    out_one(0, 0)
                if k == AH["out"][1]:
                    pe.wait_ge(s_x1, 1)
                    out_one(0, 1)
                if k == AH["turn"][0]:
                    turn_u(0, 0, 0)
                if k == AH["turn"][1]:
                    pe.wait_ge(s_nTe, 1)
                    turn_u(0, 0, 1)
                if k == AH["rows"][0]:
                    pe.wait_ge(s_nTe, 2)
                    pe.wait_ge(s_sqe, 2)
                    logit_rows(0, 0, 0)
                if k == AH["rows"][1]:
                    pe.wait_ge(s_rowsc, 1)
                    logit_rows(0, 0, 1)
                if k == AH["tokens"]:
                    logits(0, 0)
                if k == AH["rw"]:
                    pe.wait_ge(s_const, 8)
                    turn_rw(1, 0)
            late_heads(NG * NT - 1)
            pe.wait_ge(s_tanh, SCORES)

            def broadcast(n, b, hf, e, bank):
                last = pe.matmul(ps[:, bank, :], spread[:, e, :], RPT[:, b, hf * HALF:(hf + 1) * HALF],
                                 start=True, stop=True)
                last.then_inc(s_bc, 1)

            def qk(T):
                b, i = place(T)
                pe.wait_ge(s_qk, 2 * (T // 4 + 1))
                if T in (2, 3, 4, 5, 6, 7):
                    pe.wait_ge(s_pt, pt_until(T - 2))
                elif T == PT:
                    pe.wait_ge(s_pt, pt_until(T - 1))
                elif T == PT + 1:
                    pe.wait_ge(s_s, NS)
                elif T > PT:
                    pe.wait_ge(s_pt, pt_until(T - 2))
                base, nk = score_bank(T) * 512, (i + 1) * P
                for k0 in range(0, nk, HALF):
                    w = min(HALF, nk - k0)
                    pe.matmul(psf[:, base + k0:base + k0 + w], qT[:, T // TPH, T % TPH * P:(T % TPH + 1) * P],
                              kT[:, k0 // HALF * NB + b, 0:w],
                              start=True, stop=True)
                pe.matmul(psf[:, base + nk - P:base + nk], identb[:, :], maskb[:, :], start=False, stop=True,
                          skip_group_check=True).then_inc(s_S, 1)

            def turn_prob(T):
                pe.wait_ge(s_exp, T + 1)
                for n, (T_, k0, nk) in enumerate(ptjobs):
                    if T_ != T:
                        continue
                    for k in range(nk):
                        last = pe.transpose(ps[:, score_bank(T) + k0 // 4, k * P:(k + 1) * P],
                                            prob[:, T % 2, (k0 + k) * P:(k0 + k + 1) * P], ident[:, :])
                    last.then_inc(s_ptm, 1)

            def attend(T):
                b, i = place(T)
                pe.wait_ge(s_pt, pt_until(T))
                pe.wait_ge(s_v, T // 4 + 1)
                if T == 1:
                    pe.wait_ge(s_rpt, 2)
                elif T % 4 == 1:
                    pe.wait_ge(s_alo, T // 4)
                col = (T % 4) * P
                for j in range(i):
                    pe.matmul(ps[:, HEADS, col - P:col + P], V[:, tile_of(b, j), :],
                              probT[:, T // 2 % 2, j, :, :].rearrange("p a b -> p (a b)"),
                              start=(j == 0), stop=(j == i - 1))
                pe.matmul(ps[:, HEADS, col:col + P], V[:, tile_of(b, i), :], probT[:, T // 2 % 2, i, 1, :],
                          start=False, stop=True, skip_group_check=True).then_inc(s_av, 1)

            pe.wait_ge(s_rpt, 1)
            pe.wait_ge(s_wsplit, NW)

            def turn_v(m, bank):
                pe.wait_ge(s_vT, m + 1)
                for k in range(TPH):
                    last = pe.transpose(ps[:, bank, k * P:(k + 1) * P], vT[:, m % 2, k * P:(k + 1) * P],
                                        ident[:, :])
                last.then_inc(s_vtr, 1)

            def ring_job(r):
                kind, m, e = ring_jobs[r]
                if r >= 2:
                    k, m2, e2 = ring_jobs[r - 2]
                    if k == "bc":
                        pe.wait_ge(s_s, m2 * NE + e2 + 1)
                    else:
                        pe.wait_ge(s_v, m2 + 1)
                if kind == "bc":
                    b, hf = divmod(m, NHF)
                    broadcast(m * NE + e, b, hf, e, RING0 + r % 2)
                else:
                    turn_v(m, RING0 + r % 2)

            issued = 0
            for n in range(NS):
                m, e = divmod(n, NE)
                ahead = min(n + 2, NS // 2 - 1 if n < NS // 2 else NS - 1)
                while issued <= RING[("bc", *divmod(ahead, NE))]:
                    if ring_jobs[issued] == ("bc", NHF, 0):
                        pe.wait_ge(s_rpt, 2)
                    ring_job(issued)
                    issued += 1
                pe.wait_ge(s_slo, n + 1)
                for k, w in enumerate((WQ, WK, WV)):
                    if e == 0 and m:
                        if k < 2:
                            pe.wait_ge(s_qk, 2 * (m - 1) + k + 1)
                        else:
                            pe.wait_ge(s_vT, m)
                    sl = slice(e * C, (e + 1) * C)
                    last = three_pass(ps[:, k, :], whi[:, w, sl], wlo[:, w, sl],
                                      shi[:, n % 3, :], slo[:, n % 3, :], e == 0, e == NE - 1)
                    if e == NE - 1 and k < 2:
                        last.then_inc(s_qksum, 1)
                last.then_inc(s_mm, 1)
                if n == CH["out"]:
                    pe.wait_ge(s_head, 2 + NHF * NG)
                    for u in range(2):
                        pe.wait_ge(s_ht[u], 16 * GH * NB * NG)
                    for k in range(NB):
                        out_one(1, k)
                if n == CH["turn"]:
                    for k in range(NB):
                        turn_u(0, 1, k)
                if n == CH["rows"]:
                    pe.wait_ge(s_sq, 1)
                    for k in range(NB):
                        logit_rows(0, 1, k)
                if n == CH["tokens"]:
                    logits(0, 1)
                if n == CH["rw"]:
                    turn_rw(2, 1)
                for T in range(T_IN):
                    if n == ATT[T] + 4 and T % 2:
                        attend(T)
                    if n == ATT[T] + 2:
                        turn_prob(T)
                    if n == ATT[T]:
                        if T == 0:
                            pe.wait_ge(s_rowsc, 4)
                        qk(T)
            turn_v(NB * NHF - 1, 2)

            def oproj(T):
                if T == 0:
                    pe.wait_ge(s_v, NB * NHF)
                    pe.wait_ge(s_qk, 2 * NB * NHF)
                if T == PT:
                    pe.wait_ge(s_pt, len(ptjobs))
                    pe.wait_ge(s_alo, NB * NHF)
                pe.wait_ge(s_alo, T // 4 + 1)
                for k, t in ((0, T), (0, T + 1), (1, T), (1, T + 1)):
                    if k == 0 and t % PT >= 2:
                        pe.wait_ge(s_acc, t - 1)
                    if k == 1 and t < PT and t:
                        pe.wait_ge(s_esc, t)
                    if k == 1 and t >= PT + 2:
                        pe.wait_ge(s_esc, t - 1)
                    t0 = t * P
                    sl = slice(k * 512, (k + 1) * 512)
                    o = ps[:, op_bank(t, k), :]
                    pe.matmul(o, ahi[:, t0:t0 + P], whi[:, WO, sl], start=True, stop=False)
                    pe.matmul(o, ahi[:, t0:t0 + P], wlo[:, WO, sl], start=False, stop=False)
                    pe.matmul(o, alo[:, t0:t0 + P], whi[:, WO, sl], start=False, stop=True)\
                        .then_inc(s_op if k == 0 else s_op2, 1)

            qk(T_IN)
            for T in range(T_IN, NB * NT):
                if T + 1 < NB * NT:
                    qk(T + 1)
                if T == 13:
                    pe.wait_ge(s_acc, PT)
                    pe.wait_ge(s_esc, PT)
                    for b in range(NB):
                        turn_u(1, 0, b)
                if T == 14:
                    pe.wait_ge(s_sq, 2)
                    for b in range(NB):
                        logit_rows(1, 0, b)
                turn_prob(T)
                if T > T_IN and T % 2 == 0:
                    attend(T - 1)
                for t in OPROJ_AT.get(T, ()):
                    oproj(t)
            logits(1, 0)
            attend(NB * NT - 1)
            oproj(8)
            oproj(10)
            turn_rw(3, 0)

            def first_layer(n):
                m, e = divmod(n, NE)
                b, hf = divmod(m, NHF)
                if n >= 2:
                    pe.wait_ge(s_gel, n - 1)
                if e == 0:
                    pe.wait_ge(s_n2lo, b + 1)
                sl = slice(e * C, (e + 1) * C)
                three_pass(ps[:, n % 2, :], whi[:, W1, sl], wlo[:, W1, sl], ahi[:, toks(b, hf)],
                           alo[:, toks(b, hf)], True, True).then_inc(s_int, 1)

            def gate(n):
                m, e = divmod(n, NE)
                b, hf = divmod(m, NHF)
                if n % (NHF * NE) == 0:
                    pe.wait_ge(s_rpt, 3 + b)
                if n >= 2:
                    pe.wait_ge(s_s, NS + n - 1)
                broadcast(NS + n, b, hf, e, 2 + n % 2)

            def second_layer(n):
                m, e = divmod(n, NE)
                pe.wait_ge(s_slo, NS + n + 1)
                if n == 0:
                    pe.wait_ge(s_esc, NB * NT)
                if e == 0 and m:
                    pe.wait_ge(s_moe, 1 if m == 1 else m - 1)
                k = (NS + n) % 3
                sl = slice(e * C, (e + 1) * C)
                three_pass(ps[:, MOE_SUM[m], :], whi[:, W2, sl], wlo[:, W2, sl], shi[:, k, :], slo[:, k, :],
                           e == 0, e == NE - 1).then_inc(s_mm, 1)

            def turn_moe(m):
                pe.wait_ge(s_moe, m + 1)
                if m:
                    pe.wait_ge(s_fin, m)
                for k in range(TPH):
                    last = pe.transpose(ps[:, 7, k * P:(k + 1) * P], moeT[:, m % 2, k * P:(k + 1) * P],
                                        ident[:, :])
                last.then_inc(s_mtr, 1)

            for n in range(NS + LAG):
                if n < NS:
                    first_layer(n)
                    gate(n)
                if n >= LAG:
                    second_layer(n - LAG)
                if n < 2:
                    oproj(12 + 2 * n)
                if n + 1 in MOE_OUT:
                    turn_moe(MOE_OUT.index(n + 1))
                if n == MH["turn"]:
                    for k in range(NB):
                        turn_u(1, 1, k)
                if n == MH["rows"]:
                    pe.wait_ge(s_sq, 3)
                    for k in range(NB):
                        logit_rows(1, 1, k)
                if n == MH["tokens"]:
                    logits(1, 1)
                if n == MH["rw"]:
                    turn_rw(4, 1)
            turn_moe(NB * NHF - 1)


_INS = ['L0_attn_x', 'L0_attn_Wq', 'L0_attn_bq', 'L0_attn_Wk', 'L0_attn_bk', 'L0_attn_Wv', 'L0_attn_bv',
        'L0_attn_Wo', 'L0_attn_bo', 'L0_ffn_ln1_w', 'L0_ffn_ln1_b', 'L0_ffn_ln2_w', 'L0_ffn_ln2_b',
        'L0_ffn_smha_sim', 'L0_ffn_smha_gates', 'L0_ffn_q_proj', 'L0_ffn_k_proj', 'L0_ffn_v_proj',
        'L0_ffn_o_proj', 'L0_ffn_moe_sim', 'L0_ffn_moe_gates', 'L0_ffn_w1', 'L0_ffn_w2']
_OUTS = [((2, 1024, 128), 'float32')]


def kernel(**inputs):
    import numpy as _np
    import concourse.bacc as _bacc
    from concourse import mybir as _mybir
    from concourse.bass_utils import run_bass_kernel_spmd as _run

    nc = _bacc.Bacc("TRN2", target_bir_lowering=False, num_devices=1)
    arrays, args = {}, []
    for name in _INS:
        a = _np.ascontiguousarray(inputs[name])
        arrays[f"in_{name}_dram"] = a
        args.append(nc.dram_tensor(f"in_{name}_dram", a.shape, _mybir.dt.from_np(a.dtype), kind="ExternalInput").ap())
    for i, (shape, dtype) in enumerate(_OUTS):
        dt = _mybir.dt.from_np(_np.dtype(dtype))
        args.append(nc.dram_tensor(f"out_{i}_dram", shape, dt, kind="ExternalOutput").ap())
    preln_layer(nc, *args)
    r = _run(nc, [arrays], core_ids=[0])
    got = tuple(r.results[0][f"out_{i}_dram"] for i in range(len(_OUTS)))
    return got[0]
```

```python
from contextlib import ExitStack

import concourse.bass as bass
from concourse import mybir

ALU = mybir.AluOpType
ACT = mybir.ActivationFunctionType
AX = mybir.AxisListType
F32 = mybir.dt.float32
F32R = mybir.dt.float32r
BF16 = mybir.dt.bfloat16

P = 128
EPS = 1e-5
MASKED = -3.0e38


def preln_layer(nc, x, Wq, bq, Wk, bk, Wv, bv, Wo, bo, ln1_w, ln1_b, ln2_w, ln2_b,
                smha_sim, smha_gates, q_proj, k_proj, v_proj, o_proj, moe_sim, moe_gates, w1, w2, out):
    NB, S, C = x.shape
    NH = 16
    D = C // NH
    NE = q_proj.shape[0]
    NT = S // P
    HALF = 512
    NHF = S // HALF
    TPH = HALF // P
    PT = NB * TPH
    assert C == P and NB == 2 and NE * C == 1024 and NT == 8
    GH = 4
    NG = NH // GH
    R = NB * D
    SMAX_SCALE = float(C) ** -0.5
    Q_, K_ = 0, 1
    PAIRS = [(0, 0), (0, 1), (0, 2), (1, 0), (1, 1), (1, 2), (2, 0), (2, 1)]
    OP_DMAS = 2 * len(PAIRS)
    NW = 6
    WQ, WK, WV, WO, W1, W2 = range(NW)

    JOBS = [("wT", 0, 0, "act"), ("xT", 0, 0, "act"), ("xT", 0, 1, "act")]
    JOBS += [(w, 0, b, "act") for w in "qk" for b in range(NB)]
    JOBS += [("xT", 1, 0, "dve"), ("xT", 1, 1, "dve")]
    JOBS += [(w, 1, b, "act") for w in "kq" for b in range(NB)]
    JOBS += [("v", c, b, "dve") for c in range(NHF) for b in range(NB)]
    JOB = {j[:3]: n for n, j in enumerate(JOBS)}

    def emptied(n):
        e = JOBS[n][3]
        return e, sum(1 for j in JOBS[:n + 1] if j[3] == e)

    SPLITS = [(Q_, 0, 0), (Q_, 0, 1), (K_, 0, 0), (K_, 0, 1), (K_, 1, 0), (K_, 1, 1), (Q_, 1, 0), (Q_, 1, 1)]

    qk_parts = nc.dram_tensor("qk_parts", [2, 3, P, NB, S], BF16, kind="Internal").ap()

    with ExitStack() as ctx:
        def tensor(name, shape, dt, stack=ctx):
            return stack.enter_context(nc.sbuf_tensor(name, shape, dt))

        def sem(name):
            return ctx.enter_context(nc.semaphore(name))

        ps = ctx.enter_context(nc.psum_tensor("ps", [P, 8, 512], F32))
        psf = ps[:, :, :].rearrange("p a b -> p (a b)")

        ident = tensor("ident", [P, P], F32)
        identb = tensor("identb", [P, P], BF16)
        maskb = tensor("maskb", [P, P], BF16)
        spread = tensor("spread", [P, NE, P], BF16)
        before = tensor("before", [P, NE, NE], BF16)
        ones = tensor("ones", [P, P], F32)
        minus_half = tensor("minus_half", [P, 16], F32)
        warm = tensor("warm", [P, 3], F32)
        start = tensor("start", [P, 2], F32)
        bcol = tensor("bcol", [P, 4], F32)
        lncol = tensor("lncol", [P, 4], F32)
        bv_row = tensor("bv_row", [P, P], F32)
        bo_row = tensor("bo_row", [P, P], F32)
        gates = tensor("gates", [P, 2, NE], F32)
        sims = tensor("sims", [P, 4, NE], F32)
        simsq = tensor("simsq", [P, 2 * NE], F32)
        simn2 = tensor("simn2", [P, 2 * NE], F32)
        simrn = tensor("simrn", [P, 2 * NE], F32)
        wnat = tensor("wnat", [P, 4, P], F32)
        wT = tensor("wT", [P, 4, P], F32)
        X = tensor("X", [P, NB * NT, P], F32)
        U = tensor("U", [P, NB * NT, P], F32)
        nT = tensor("nT", [P, NB * S], F32)
        stats = tensor("stats", [P, NB * NT, 6], F32)
        mv = tensor("mv", [P, NB * NT, 2], F32)
        powin = tensor("powin", [P, NB, 2, NT], F32)
        powout = tensor("powout", [P, NB, 2, NT], F32)
        bv_half = tensor("bv_half", [P, 1], F32)
        sumq = tensor("sumq", [P, NB * NHF], F32)
        sumx = tensor("sumx", [P, NB], F32)
        cvec = tensor("cvec", [P, NB], F32)
        cvecb = tensor("cvecb", [P, NB, P], F32)
        row_add = tensor("row_add", [P, NB, P], F32)
        whi = tensor("whi", [P, NW, NE * C], F32R)
        wlo = tensor("wlo", [P, NW, NE * C], F32R)
        HT = tensor("HT", [P, NB * S], F32)
        wraw = tensor("wraw", [P, 2, NE * C], F32)
        SQ = wraw[:, 0, :]
        RP = tensor("RP", [P, NHF, PT, 3 * NE], BF16)
        RPT = tensor("RPT", [P, NHF, S], BF16)
        rw = tensor("rw", [P, NHF, PT, NE], F32)
        gt = tensor("gt", [P, NHF, 3, PT, NE], F32)
        cmp_ = wraw[:, 1, :].bitcast(BF16)[:, 0:2 * PT * NE * NE].rearrange("p (t i j e) -> p t i j e", t=2, i=PT, j=NE)
        g1 = tensor("g1", [P, 6, PT], F32)

        early = ExitStack()
        parts = tensor("parts", [P, 2, 3, NB, S], BF16, early)
        q32 = tensor("q32", [P, 2, HALF], F32, early)
        rest = tensor("rest", [P, 2, HALF], F32, early)
        ops_k = tensor("ops_k", [P, 2, GH, S], BF16, early)
        ops_q = tensor("ops_q", [P, 2, GH, HALF], BF16, early)
        VP = tensor("VP", [P, NT, NH, R], F32, early)
        vst = tensor("vst", [P, 2, NT, GH, 32], F32, early)
        tanhs = tensor("tanhs", [P, 4, 2, HALF], F32, early)
        hout = tensor("hout", [P, 2, HALF], F32, early)
        early.close()
        HS = tensor("HS", [P, NB * NT, P], F32)
        sring = tensor("sring", [P, 3, HALF], F32)
        shi = tensor("shi", [P, 3, HALF], F32R)
        slo = tensor("slo", [P, 3, HALF], F32R)
        qT = tensor("qT", [P, NB * NHF, HALF], F32)
        kT = tensor("kT", [P, NB * NHF, HALF], F32)
        vT = tensor("vT", [P, 2, HALF], F32)
        V = tensor("V", [P, NB * NT, P], F32)
        prob = tensor("prob", [P, 2, S], F32)
        probT = tensor("probT", [P, 2, NT, 2, P], F32)
        mx = tensor("mx", [P, 2, NB * NT], F32)
        rowsum = tensor("rowsum", [P, NB * NT], F32)
        rwn = tensor("rwn", [P, NHF, PT, NE], F32)
        ahi = tensor("ahi", [P, NB * S], F32R)
        alo = tensor("alo", [P, NB * S], F32R)
        gel = tensor("gel", [P, 2, HALF], F32)
        pair_terms = [gel[:, :, :], sring[:, 0:2, :]] * 2 + [qT[:, 0:2, :], qT[:, 2:4, :]] * 2
        pair_terms = [t.rearrange("p t (e c) -> p t e c", c=P) for t in pair_terms]

        def eterm(T):
            return pair_terms[T // 2][:, T % 2]

        moeT = vT
        fin = HS

        s_x = [sem(f"x_loaded{b}") for b in range(NB)]
        s_wnat = sem("wnat_loaded")
        s_small = sem("biases_loaded")
        s_rows_in = sem("small_loaded")
        s_const = sem("consts_made")
        s_id = sem("ident_made")
        s_pool = sem("pool_step")
        s_dve = sem("dve_step")
        s_powin = sem("pow_inputs")
        s_pow = sem("pow_results")
        s_xn = sem("xn_ready")
        s_job = sem("job_products")
        s_jact = sem("job_emptied_by_act")
        s_jdve = sem("job_emptied_by_dve")
        s_rest = sem("qk_rest_taken")
        s_mid = sem("qk_middle_taken")
        s_split = sem("qk_split")
        s_sums = sem("sums_inputs")
        s_cvec = sem("cvec_ready")
        s_gtan = sem("gates_tanh")
        s_kd = sem("k_parts_in_dram")
        s_qd = [sem(f"q_parts{c}_in_dram") for c in range(NHF)]
        s_ops = [sem(f"ops_loaded{u}") for u in range(2)]
        s_vst = sem("v_staged")
        s_score = sem("scores_ready")
        s_tanh = sem("tanh_done")
        s_pair = sem("tanh_pairs_used")
        s_head = sem("heads_emptied")
        s_ht = [sem(f"heads_moved{u}") for u in range(2)]
        s_wraw = [sem(f"wraw_loaded{u}") for u in range(2)]
        s_wsplit = sem("weights_split")
        s_o1 = sem("out_proj_ready")
        s_x1 = sem("x1_ready")
        s_r1 = sem("first_norm_ready")
        s_u = sem("u_ready")
        s_uT = sem("uT_ready")
        s_nT = sem("nT_ready")
        s_sq = sem("sq_ready")
        s_log = sem("logits_ready")
        s_gex = sem("gate_tanh_in")
        s_gexo = sem("gate_tanh_out")
        s_rp = sem("rw_parts")
        s_rpT = sem("rw_partsT")
        s_rpt = sem("rpt_ready")
        s_bc = sem("bcast_ready")
        s_s = sem("scaled_ready")
        s_shi = sem("scaled_hi")
        s_slo = sem("scaled_lo")
        s_mm = sem("steps_done")
        s_qksum = sem("qk_sums")
        s_rptz = sem("rpt_cleared")
        s_added = sem("experts_added")
        s_sumd = sem("batch_sums_ready")
        s_addrow = sem("added_rows_ready")
        s_rowadd = sem("added_rows_taken")
        s_simz = sem("sims_cleared")
        s_nTe = sem("part0_n1_ready")
        s_sqe = sem("part0_sq_ready")
        s_rows = sem("logit_rows_ready")
        s_rowsc = sem("logit_rows_copied")
        s_rwn = sem("gates_over_rowsum")
        s_op2 = sem("oproj_second_ready")
        s_esc = sem("experts_scaled")
        s_pool2 = sem("pool_sums")
        s_qk = sem("qk_copied")
        s_vT = sem("vT_copied")
        s_vtr = sem("v_turned")
        s_v = sem("v_copied")
        s_S = sem("S_ready")
        s_nb = sem("negmax_ready")
        s_exp = sem("exp_done")
        s_ptm = sem("probT_made")
        s_pt = sem("probT_copied")
        s_av = sem("av_done")
        s_ahi = sem("attn_hi")
        s_alo = sem("attn_lo")
        s_op = sem("oproj_ready")
        s_acc = sem("oproj_added")
        s_hs = sem("hs_ready")
        s_xh = sem("xh_ready")
        s_n2hi = sem("n2_hi")
        s_n2lo = sem("n2_lo")
        s_int = sem("inter_ready")
        s_gel = sem("gelu_done")
        s_moe = sem("moe_copied")
        s_mtr = sem("moe_turned")
        s_fin = sem("fin_ready")
        s_out = [sem(f"out_stored{u}") for u in range(2)]

        SCORES = 3 + NHF * NG * NT * 2
        NS = NB * NHF * NE
        LAG = 3
        MOE_SUM = (4, 4, 5, 4)
        MOE_OUT = (19, 24, 30)
        OPROJ_AT = {8: (0,), 9: (2, 4), 10: (6,)}
        SUM_RESIDUALS = (17, 22)
        AH = dict(sums=0, add=3, out=(6, 8), turn=(14, 14), rows=(16, 18), tokens=20, exp=25, rw=29)
        CH = dict(out=2, x1=4, stats=6, power=8, norms=10, turn=9, normed=11, squares=11, rows=12, copy=13,
                  tokens=13, norm=15, direction=14, logits=15, exp=14, ranks=15, weights=15, rw=15, rpt=15)
        MH = dict(stats=2, power=2, norms=3, turn=5, normed=4, squares=5, rows=7, copy=7, tokens=8, norm=8,
                  direction=6, logits=9, exp=9, ranks=10, weights=12, rw=14, rpt=14)
        ring_jobs = []
        for m in range(NB * NHF):
            for e in range(NE):
                ring_jobs.append(("bc", m, e))
                if e == 3 and m:
                    ring_jobs.append(("v", m - 1, 0))
        RING = {j: n for n, j in enumerate(ring_jobs)}
        RING0, SCORE0, HEADS = 3, 5, 7
        OUT1 = ((7, 7), (5, 6))
        TURNED = (((7, 7), (5, 6)), ((0, 1), (5, 6)))
        LOGITS_T = (((7, 7), (5, 6)), ((0, 1), (5, 6)))
        LOGITS = ((7, 7), (2, 7))
        RW_TURNED = (7, 7, 2, 7)

        def op_bank(T, k):
            if T < PT:
                return 2 if k else T % 2
            return (4, 7)[T % 2] if k else 5 + T % 2

        def ring_bank(r):
            return RING0 + r % 2 if r else HEADS

        ATT = {0: 14, 1: 15, 2: 18, 3: 21, 4: 21, 5: 23, 6: 26, 7: 27}
        T_IN = len(ATT)

        def place(T):
            m = T // TPH
            return m % NB, m // NB * TPH + T % TPH

        def tile_of(b, i):
            return (i // TPH * NB + b) * TPH + i % TPH

        def score_bank(T):
            if T < PT:
                return SCORE0 + T % 2
            return RING0 if T % 2 else SCORE0

        ptjobs = []
        for T in range(NB * NT):
            i = place(T)[1]
            for k0 in range(0, i + 1, 4):
                ptjobs.append((T, k0, min(4, i + 1 - k0)))

        def pt_until(T):
            return sum(1 for j in ptjobs if j[0] <= T)

        GR = 4 * NE

        def rows_of(c):
            return U[0:2 * GR, c * PT:(c + 1) * PT, :].rearrange("p i c -> p (i c)")

        def toks(c, b):
            return slice(c * S + b * HALF, c * S + (b + 1) * HALF)

        block = ctx.enter_context(nc.Block())

        @block.sync
        def _(sp):
            xv = x.rearrange("b (i p) c -> b p i c", p=P)
            for c in range(NHF):
                for b in range(NB):
                    m = c * NB + b
                    sp.dma_start(X[:, m * TPH:(m + 1) * TPH, :], xv[b, :, c * TPH:(c + 1) * TPH]).then_inc(s_x[c], 16)
                if c == 0:
                    for n, w in enumerate((Wq, Wk, Wv, Wo)):
                        sp.dma_start(wnat[:, n, :], w).then_inc(s_wnat, 16)

            for n, a in enumerate((ln1_w, ln1_b, ln2_w, ln2_b)):
                sp.dma_start(lncol[:, n:n + 1], a.rearrange("(p a) -> p a", a=1)).then_inc(s_rows_in, 16)
            for t, a in ((bv_row, bv), (bo_row, bo)):
                sp.dma_start(t[:, :], a.rearrange("(a c) -> a c", a=1).to_broadcast([P, P])).then_inc(s_rows_in, 16)
            for n, a in enumerate((smha_gates, moe_gates)):
                sp.dma_start(gates[:, n, :], a.rearrange("(a c) -> a c", a=1).to_broadcast([P, NE]))\
                    .then_inc(s_rows_in, 16)
            for n, a in enumerate((smha_sim, moe_sim)):
                sp.dma_start(sims[:, n, :], a).then_inc(s_rows_in, 16)

            def load_weight(n):
                if n >= 2:
                    sp.wait_ge(s_wsplit, n - 1)
                src = (q_proj, k_proj, v_proj, o_proj, w1, w2)[n]
                sp.dma_start(wraw[:, n % 2, :].rearrange("p (e n) -> p e n", e=NE),
                             src.rearrange("e c n -> c e n")).then_inc(s_wraw[n % 2], 16)

            load_weight(0)
            load_weight(1)
            def write_parts(n):
                t, c, b = SPLITS[n]
                sl = slice(c * HALF, (c + 1) * HALF)
                sp.wait_ge(s_split, n + 1)
                sp.dma_start(qk_parts[t, :, :, b, sl].rearrange("a r s -> r a s"), parts[:, t, :, b, sl])\
                    .then_inc(s_kd if t == K_ else s_qd[c], 16)

            def load_group(G, queries=range(len(PAIRS)), keys=range(len(PAIRS))):
                half, g = divmod(G, NG)
                if G >= 2:
                    sp.wait_ge(s_score, 16 * (G - 1))
                own = qk_parts[:, :, 32 * g:32 * g + 32].rearrange("t a (h d) b s -> t a (d b) h s", d=D)

                def load(ops, t, which, sl):
                    for r in which:
                        sp.dma_start(ops[r * R:(r + 1) * R, G % 2, :, :], own[t, PAIRS[r][t], :, :, sl])\
                            .then_inc(s_ops[G % 2], 16)

                load(ops_q, Q_, queries, slice(half * HALF, (half + 1) * HALF))
                load(ops_k, K_, keys, slice(0, S))

            for n in range(4):
                write_parts(n)
            sp.wait_ge(s_qd[0], 16 * 2)
            load_group(0, queries=range(0, 3), keys=())
            write_parts(4)
            load_group(0, queries=range(3, 6), keys=())
            write_parts(5)
            load_group(0, queries=range(6, 8), keys=())
            sp.wait_ge(s_kd, 16 * 4)
            load_group(0, queries=())
            load_group(1)
            for n in range(2, NW):
                load_weight(n)
            write_parts(6)
            write_parts(7)
            sp.wait_ge(s_qd[1], 16 * 2)
            for G in range(NHF * NG):
                if G + 2 < NHF * NG:
                    load_group(G + 2)
                sp.wait_ge(s_head, 2 + G + 1)
                half, g = divmod(G, NG)
                for j in range(GH):
                    for b in range(NB):
                        h = g * GH + j
                        sp.dma_start(HT[D * h:D * h + D, toks(half, b)],
                                     hout[32 * j + D * b:32 * j + D * b + D, G % 2, :]).then_inc(s_ht[G % 2], 16)
            ov = out.rearrange("b (i p) c -> b p i c", p=P)
            for m in range(NB * NHF):
                c, b = divmod(m, NB)
                sp.wait_ge(s_fin, m + 1)
                sp.dma_start(ov[b, :, c * TPH:(c + 1) * TPH, :],
                             fin[:, m * TPH:(m + 1) * TPH, :]).then_inc(s_out[m % 2], 16)
            for u in range(2):
                sp.wait_ge(s_out[u], 16 * NB * NHF // 2)

        @block.gpsimd
        def _(pool):
            pool.memset(ident[:, :], 0.0).then_inc(s_pool, 1)
            pool.memset(warm[:, :], 0.0).then_inc(s_const, 1)
            pool.memset(minus_half[:, :], -0.5).then_inc(s_pool, 1)
            pool.wait_ge(s_pool, 2)
            pool.affine_select(out=ident[:, :], in_=ident[:, :], compare_op=ALU.not_equal, fill=1.0,
                               base=0, pattern=[[-1, P]], channel_multiplier=1).then_inc(s_id, 1)
            pool.memset(ones[:, :], 1.0).then_inc(s_const, 1)
            pool.memset(start[:, 0:1], 0.0).then_inc(s_pair, 2)
            pool.memset(start[:, 1:2], 0.0).then_inc(s_head, 2)
            pool.memset(sims[:, 2:4, :], 0.0).then_inc(s_simz, 1)
            pool.memset(RPT[:, :, :], 0.0).then_inc(s_rptz, 1)
            pool.memset(before[:, :, :], 1.0).then_inc(s_pool, 1)
            pool.memset(maskb[:, :], 0.0).then_inc(s_pool, 1)
            pool.memset(spread[:, :, :], 0.0).then_inc(s_pool, 1)
            pool.memset(identb[:, :], 0.0).then_inc(s_pool, 1)
            pool.memset(vst[:, 0, :, :, :], 0.0).then_inc(s_const, 1)
            pool.memset(vst[:, 1, :, :, :], 0.0).then_inc(s_const, 1)

            def power(n, o, i):
                pool.wait_ge(s_powin, n)
                pool.tensor_tensor(o, i, minus_half[:, 0:i.shape[1]], ALU.pow).then_inc(s_pow, 1)

            for c in range(NHF):
                power(c + 1, powout[:, c, 0, :], powin[:, c, 0, :])

            def low_part(nq):
                t, c, b = SPLITS[nq]
                dst = parts[:, t, :, b, c * HALF:(c + 1) * HALF]
                pool.wait_ge(s_mid, nq + 1)
                pool.tensor_tensor(dst[:, 2, :], rest[:, nq % 2, :], dst[:, 1, :], ALU.subtract).then_inc(s_split, 1)

            for n in range(len(SPLITS)):
                low_part(n)
            pool.wait_ge(s_pool, 6)
            pool.affine_select(out=identb[:, :], in_=identb[:, :], compare_op=ALU.not_equal, fill=1.0,
                               base=0, pattern=[[-1, P]], channel_multiplier=1).then_inc(s_const, 1)
            pool.affine_select(out=maskb[:, :], in_=maskb[:, :], compare_op=ALU.is_ge, fill=MASKED,
                               base=0, pattern=[[-1, P]], channel_multiplier=1).then_inc(s_const, 1)
            pool.affine_select(out=before[:, :, :], in_=before[:, :, :], compare_op=ALU.is_gt, fill=0.0,
                               base=0, pattern=[[1, NE], [-1, NE]], channel_multiplier=0).then_inc(s_const, 1)
            for a in range(3):
                if a:
                    pool.wait_ge(s_pool, 6 + a)
                pool.affine_select(out=spread[:, :, :], in_=spread[:, :, :], compare_op=ALU.not_equal, fill=1.0,
                                   base=-NE * a, pattern=[[-1, NE], [0, P]], channel_multiplier=1)\
                    .then_inc(s_pool if a < 2 else s_const, 1)
            power(3, simrn[:, :], simn2[:, :])

            def first_scale(c):
                pool.wait_ge(s_powin, 4 + 2 * c)
                pool.tensor_tensor(powout[:, c, 0, :], powin[:, c, 0, :], minus_half[:, 0:PT], ALU.pow)\
                    .then_inc(s_r1, 1)
                pool.wait_ge(s_r1, c + 1)

            def residual(T):
                c, i = divmod(T, PT)
                pool.wait_ge(s_o1, 4)
                pool.tensor_scalar(HS[:, T, :], X[:, T, :], mv[:, T, 0:1], powout[:, c, 0, i:i + 1],
                                   ALU.subtract, ALU.mult).then_inc(s_hs, 1)

            def direction(c, n):
                power(n, g1[:, 2 * c + 1, :], g1[:, 2 * c, :])

            def low(n):
                pool.wait_ge(s_shi, n + 1)
                if n >= 3:
                    pool.wait_ge(s_mm, n - 2)
                pool.tensor_tensor(slo[:, n % 3, :], sring[:, n % 3, :], shi[:, n % 3, :].bitcast(F32),
                                   ALU.subtract).then_inc(s_slo, 1)

            def add_scaled(T):
                pool.wait_ge(s_esc, T + 2)
                t = pair_terms[T // 2]
                pool.tensor_tensor(t[:, :, 0:2, :], t[:, :, 0:2, :], t[:, :, 2:4, :], ALU.add).then_inc(s_pool2, 1)
                pool.wait_ge(s_pool2, T + 1)
                pool.tensor_tensor(t[:, :, 0, :], t[:, :, 0, :], t[:, :, 1, :], ALU.add).then_inc(s_pool2, 1)
                pool.wait_ge(s_pool2, T + 2)
                pool.wait_ge(s_acc, T + 2)
                pool.tensor_tensor(HS[:, T:T + 2, :], HS[:, T:T + 2, :], t[:, :, 0, :], ALU.add).then_inc(s_added, 2)

            def sum_residuals(c):
                pool.wait_ge(s_added, (c + 1) * PT)
                xb = X[:, c * PT:(c + 1) * PT, :]
                pool.tensor_tensor(xb, xb, HS[:, c * PT:(c + 1) * PT, :], ALU.add).then_inc(s_xh, 1)

            def n2_low():
                pool.wait_ge(s_n2hi, 1)
                sl = slice(0, S)
                pool.tensor_tensor(alo[:, sl], nT[:, sl], ahi[:, sl].bitcast(F32), ALU.subtract).then_inc(s_n2lo, 1)

            power(4, powout[:, 0, 1, :], powin[:, 0, 1, :])
            direction(0, 5)
            first_scale(0)
            for n in range(NS):
                low(n)
                if n == CH["power"]:
                    power(6, powout[:, 1, 1, :], powin[:, 1, 1, :])
                if n == CH["direction"]:
                    direction(1, 7)
                if n == NS // 2 + 4:
                    first_scale(1)
                if n >= NS // 2:
                    residual(n - NS // 2)
            for T in range(0, PT, 2):
                add_scaled(T)
            power(8, powout[:, 0, 0, :], powin[:, 0, 0, :])
            n2_low()
            direction(0, 9)
            for T in range(PT, NB * NT - 2, 2):
                add_scaled(T)
            for n in range(NS):
                low(NS + n)
                if n == 0:
                    add_scaled(14)
                if n == MH["power"]:
                    power(10, powout[:, 1, 0, :], powin[:, 1, 0, :])
                if n == MH["direction"]:
                    direction(1, 11)
                if n in SUM_RESIDUALS:
                    sum_residuals(SUM_RESIDUALS.index(n))

        @block.scalar
        def _(act):
            act.dma_start(bcol[:, 0:1], bq.rearrange("(p a) -> p a", a=1)).then_inc(s_small, 16)
            act.dma_start(bcol[:, 1:2], bk.rearrange("(p a) -> p a", a=1)).then_inc(s_small, 16)
            act.dma_start(bcol[:, 2:3], bv.rearrange("(p a) -> p a", a=1)).then_inc(s_small, 16)
            act.wait_ge(s_const, 1)
            act.activation(warm[:, 1:2], warm[:, 0:1], ACT.Tanh).then_inc(s_tanh, 3)

            nq = 0
            for n, (what, b, h, e) in enumerate(JOBS):
                if e != "act":
                    continue
                act.wait_ge(s_job, n + 1)
                src = ps[:, n % 8, :]
                if what == "wT":
                    act.activation(wT[:, :, :].rearrange("p a b -> p (a b)"), src, ACT.Copy).then_inc(s_jact, 1)
                elif what == "xT":
                    act.activation(nT[:, toks(b, h)], src, ACT.Copy).then_inc(s_jact, 1)
                else:
                    t = Q_ if what == "q" else K_
                    c, b = b, h
                    sign = -1.0 if (t == K_ and b == 1) else 1.0
                    bias = bcol[:, 3:4] if sign < 0 else bcol[:, t:t + 1]
                    if nq == 0:
                        act.wait_ge(s_small, 16 * 3)
                    if nq >= 2:
                        act.wait_ge(s_rest, nq - 1)
                    if sign < 0 and c == 0:
                        act.wait_ge(s_sums, 1)
                    act.activation(q32[:, nq % 2, :], src, ACT.Identity, bias=bias, scale=sign)
                    act.activation(parts[:, t, 0, b, c * HALF:(c + 1) * HALF], src, ACT.Identity,
                                   bias=bias, scale=sign).then_inc(s_jact, 1)
                    nq += 1
            act.wait_ge(s_rows_in, 16 * 10)
            act.activation(gates[:, :, :].rearrange("p a b -> p (a b)"),
                           gates[:, :, :].rearrange("p a b -> p (a b)"), ACT.Tanh, scale=0.5).then_inc(s_gtan, 1)

            def tanh(i, scored, free):
                act.wait_ge(s_score, scored)
                if i % 2 == 0:
                    act.wait_ge(s_pair, free)
                act.activation(tanhs[:, i % 4, :, :].rearrange("p a b -> p (a b)"),
                               psf[:, (i % 3) * 1024:(i % 3) * 1024 + 1024],
                               ACT.Tanh, scale=0.5).then_inc(s_tanh, 1)

            def gate_tanh(part, c):
                act.wait_ge(s_gex, 2 * part + c + 1)
                act.activation(gt[:, c, 2, :, :], gt[:, c, 2, :, :], ACT.Tanh, scale=0.5).then_inc(s_gexo, 1)

            with act.Fori(0, NG // 2) as gg:
                for i in range(32):
                    tanh(i, 32 * gg + (i + 1), 16 * gg + (i // 2 + 1))
            for i in range(64):
                tanh(i, 64 + i + 1, 32 + i // 2 + 1)
                if i == 2 * AH["exp"]:
                    gate_tanh(0, 0)

            def normed(part, c):
                act.wait_ge(s_uT, 2 * (2 * part + c) + 2)
                k = TURNED[part][c][0]
                act.activation(nT[:, c * S:(c + 1) * S], psf[:, k * 512:k * 512 + S], ACT.Identity,
                               bias=lncol[:, 2 * part + 1:2 * part + 2],
                               scale=lncol[:, 2 * part:2 * part + 1]).then_inc(s_nT, 1)

            def squares(part, c):
                act.wait_ge(s_nT, 2 * part + c)
                act.activation(SQ[:, 0:S], nT[:, c * S:(c + 1) * S], ACT.Square).then_inc(s_sq, 1)

            def n2_high(c):
                act.activation(ahi[:, c * S:(c + 1) * S], nT[:, c * S:(c + 1) * S], ACT.Copy).then_inc(s_n2hi, 1)

            def high(n):
                act.wait_ge(s_s, n + 1)
                if n >= 3:
                    act.wait_ge(s_mm, n - 2)
                act.activation(shi[:, n % 3, :], sring[:, n % 3, :], ACT.Copy).then_inc(s_shi, 1)

            def exps(T):
                i = place(T)[1]
                act.wait_ge(s_nb, T + 1)
                if T >= 2:
                    act.wait_ge(s_ptm, pt_until(T - 2))
                col = score_bank(T) * 512
                act.activation(prob[:, T % 2, 0:(i + 1) * P], psf[:, col:col + (i + 1) * P],
                               ACT.Exp, bias=mx[:, 1, T:T + 1], scale=SMAX_SCALE,
                               accum_out=rowsum[:, T:T + 1]).then_inc(s_exp, 1)

            def copies(T):
                for n, (T_, k0, nk) in enumerate(ptjobs):
                    if T_ != T:
                        continue
                    act.wait_ge(s_ptm, n + 1)
                    if T >= 4 and k0 == 0:
                        act.wait_ge(s_av, T // 2 - 1)
                    act.activation(probT[:, T // 2 % 2, k0:k0 + nk, T % 2, :],
                                   ps[:, score_bank(T) + k0 // 4, 0:nk * P].rearrange("p (a b) -> p a b", b=P),
                                   ACT.Copy).then_inc(s_pt, 1)

            def attn_hi(q):
                act.wait_ge(s_av, 2 * q + 2)
                act.activation(ahi[:, q * HALF:(q + 1) * HALF], ps[:, HEADS, :], ACT.Copy).then_inc(s_ahi, 1)

            def take_qk(m):
                for k, t in enumerate((qT, kT)):
                    act.wait_ge(s_qksum, 2 * m + k + 1)
                    act.activation(t[:, m, :], ps[:, k, :], ACT.Copy).then_inc(s_qk, 1)

            for n in range(NS):
                m, e = divmod(n, NE)
                high(n)
                if e == 0 and m:
                    take_qk(m - 1)
                if n == CH["normed"]:
                    normed(0, 1)
                if n == CH["squares"]:
                    squares(0, 1)
                if n == CH["exp"]:
                    gate_tanh(0, 1)
                for T in range(T_IN):
                    if n == ATT[T] + 4:
                        copies(T)
                    if n == ATT[T] + 2:
                        exps(T)
                if n == ATT[3] + 6:
                    attn_hi(0)
            take_qk(NB * NHF - 1)

            def scale_experts(T):
                c, i = divmod(T, PT)
                act.wait_ge(s_rwn, c + 1)
                act.wait_ge(s_op2, T + 1)
                if T >= 4:
                    act.wait_ge(s_added, T // 2 * 2 - 2)
                for e in range(NE // 2):
                    ins = act.activation(eterm(T)[:, e, :], ps[:, op_bank(T, 1), e * P:(e + 1) * P], ACT.Copy,
                                         scale=rwn[:, c, i, NE // 2 + e:NE // 2 + e + 1])
                ins.then_inc(s_esc, 1)

            exps(T_IN)
            for T in range(T_IN, NB * NT):
                if T + 1 < NB * NT:
                    exps(T + 1)
                copies(T)
                if T in (PT, PT + 5):
                    attn_hi(1 if T == PT else 2)
                for t in OPROJ_AT.get(T, ()):
                    scale_experts(t)
                    scale_experts(t + 1)
                if T == 13:
                    normed(1, 0)
                    squares(1, 0)
                if T == 14:
                    n2_high(0)
            act.activation(warm[:, 2:3], warm[:, 0:1], ACT.Gelu)
            attn_hi(3)
            scale_experts(8)
            scale_experts(9)
            gate_tanh(1, 0)
            for T in range(10, 14):
                scale_experts(T)

            def gelu(n):
                act.wait_ge(s_int, n + 1)
                if n >= 2:
                    act.wait_ge(s_s, NS + n - 1)
                act.activation(gel[:, n % 2, :], ps[:, n % 2, :], ACT.Gelu).then_inc(s_gel, 1)

            act.wait_ge(s_added, PT)
            gelu(0)
            for n in range(NS):
                if n + 1 < NS:
                    gelu(n + 1)
                high(NS + n)
                if n == 0:
                    scale_experts(14)
                    scale_experts(15)
                if n == MH["normed"]:
                    normed(1, 1)
                if n == MH["squares"]:
                    squares(1, 1)
                    n2_high(1)
                if n == MH["exp"]:
                    gate_tanh(1, 1)

        @block.vector
        def _(dve):
            steps = [0]

            def link(ins):
                steps[0] += 1
                ins.then_inc(s_dve, 1)
                dve.wait_ge(s_dve, steps[0])

            def statistics(src, c):
                for i in range(PT):
                    last = dve.bn_stats(stats[:, c * PT + i, :], src[:, c * PT + i, :])
                link(last)
                for i in range(PT):
                    last = dve.bn_aggr(mv[:, c * PT + i, :], stats[:, c * PT + i, :])
                link(last)
                return mv[:, c * PT:(c + 1) * PT, 0], mv[:, c * PT:(c + 1) * PT, 1]

            def first_statistics(c):
                dve.wait_ge(s_x[c], 32)
                m_, v_ = statistics(X, c)
                dve.tensor_scalar(powin[:, c, 0, :], v_, EPS, None, ALU.add).then_inc(s_powin, 1)

            def normalise(c, r, sem_, only=None):
                for i in range(PT) if only is None else range(only * TPH, (only + 1) * TPH):
                    last = dve.tensor_scalar(U[:, c * PT + i, :], X[:, c * PT + i, :], mv[:, c * PT + i, 0:1],
                                             r[:, i:i + 1], ALU.subtract, ALU.mult)
                last.then_inc(sem_, 1)

            def empty(n, fn):
                dve.wait_ge(s_job, n + 1)
                fn(ps[:, n % 8, :]).then_inc(s_jdve, 1)

            def split_rest(nq):
                t, c, b = SPLITS[nq]
                dst = parts[:, t, :, b, c * HALF:(c + 1) * HALF]
                n = JOB[("qk"[t], c, b)]
                dve.wait_ge(s_jact, emptied(n)[1])
                if nq >= 2:
                    dve.wait_ge(s_split, nq - 1)
                ins = dve.tensor_tensor(rest[:, nq % 2, :], q32[:, nq % 2, :], dst[:, 0, :], ALU.subtract)
                ins.then_inc(s_rest, 1)
                dve.wait_ge(s_rest, nq + 1)
                dve.tensor_copy(dst[:, 1, :], rest[:, nq % 2, :]).then_inc(s_mid, 1)

            first_statistics(0)
            dve.wait_ge(s_pow, 1)
            for b in range(NB):
                normalise(0, powout[:, 0, 0, :], s_xn, b)
            first_statistics(1)
            dve.wait_ge(s_small, 16 * 3)
            dve.tensor_scalar(bcol[:, 3:4], bcol[:, 1:2], -1.0, None, ALU.mult).then_inc(s_sums, 1)
            split_rest(0)
            dve.wait_ge(s_pow, 2)
            for b in range(NB):
                normalise(1, powout[:, 1, 0, :], s_xn, b)
            split_rest(1)
            empty(JOB[("xT", 1, 0)], lambda src: dve.tensor_copy(nT[:, toks(1, 0)], src))
            empty(JOB[("xT", 1, 1)], lambda src: dve.tensor_copy(nT[:, toks(1, 1)], src))
            for n in range(2, 6):
                split_rest(n)

            dve.wait_ge(s_rows_in, 16 * 10)
            link(dve.tensor_scalar(cvecb[:, 0, :], bv_row[:, :], 0.5, None, ALU.mult))
            link(dve.tensor_scalar(cvecb[:, 1, :], bv_row[:, :], -0.5, None, ALU.mult))
            for c in range(NHF):
                for b in range(NB):
                    n = JOB[("v", c, b)]
                    dve.wait_ge(s_job, n + 1)
                    for k in range(TPH):
                        last = dve.scalar_tensor_tensor(
                            out=VP[:, c * TPH + k, :, b * D:(b + 1) * D],
                            in0=ps[:, n % 8, k * P:(k + 1) * P].rearrange("p (h d) -> p h d", d=D),
                            scalar=0.5 if b == 0 else -0.5,
                            in1=cvecb[:, b, :].rearrange("p (h d) -> p h d", d=D), op0=ALU.mult, op1=ALU.add)
                    last.then_inc(s_jdve, 1)
            jd = emptied(JOB[("v", 1, 1)])[1]
            dve.wait_ge(s_jdve, jd)
            dve.wait_ge(s_const, 4)
            def stage_v(G):
                if G >= 2:
                    dve.wait_ge(s_pair, 2 + NT * (G - 1))
                g = G % NG
                dve.tensor_copy(vst[:, G % 2, :, :, 0:R], VP[:, :, g * GH:(g + 1) * GH, :]).then_inc(s_vst, 1)

            stage_v(0)
            stage_v(1)
            split_rest(6)
            split_rest(7)

            link(dve.tensor_tensor(simsq[:, :], sims[:, 0:2, :].rearrange("p a b -> p (a b)"),
                                   sims[:, 0:2, :].rearrange("p a b -> p (a b)"), ALU.mult))
            dve.wait_ge(s_jact, emptied(JOB[("xT", 0, 1)])[1])
            link(dve.tensor_reduce(sumq[:, :], nT[:, :].rearrange("p (m s) -> p m s", s=HALF), AX.X, ALU.add))
            dve.tensor_tensor(sumx[:, :], sumq[:, 0:NB], sumq[:, NB:2 * NB], ALU.add).then_inc(s_sums, 1)
            def batch_sums():
                dve.wait_ge(s_sumd, 1)
                dve.tensor_scalar(simn2[:, :], ps[:, 7, 0:2 * NE], 1e-24, None, ALU.max).then_inc(s_powin, 1)
                link(dve.tensor_scalar(cvec[:, :], ps[:, 7, 2 * NE:2 * NE + NB], 0.5, None, ALU.mult))
                link(dve.tensor_scalar(bv_half[:, :], bcol[:, 2:3], 0.5 * S, None, ALU.mult))
                link(dve.tensor_tensor(cvec[:, :], cvec[:, :], bv_half[:, :].to_broadcast([P, NB]), ALU.add))
                for b in range(NB):
                    last = dve.tensor_scalar(cvecb[:, b, :], ones[:, :], cvec[:, b:b + 1], None, ALU.mult)
                last.then_inc(s_cvec, 1)

            def add_rows():
                dve.wait_ge(s_addrow, 1)
                for b in range(NB):
                    last = dve.tensor_tensor(row_add[:, b, :], ps[:, 7, b * P:(b + 1) * P], bo_row[:, :], ALU.add)
                last.then_inc(s_rowadd, 1)
                dve.wait_ge(s_rowadd, 1)
                for m in range(NB * NHF):
                    b = m % NB
                    xb = X[:, m * TPH:(m + 1) * TPH, :]
                    last = dve.tensor_tensor(xb, xb, row_add[:, b:b + 1, :].to_broadcast([P, TPH, P]), ALU.add)
                link(last)
                dve.wait_ge(s_pow, 3)
                link(dve.tensor_tensor(sims[:, 0:2, :].rearrange("p a b -> p (a b)"),
                                       sims[:, 0:2, :].rearrange("p a b -> p (a b)"), simrn[:, :], ALU.mult))

            dve.wait_ge(s_gtan, 1)
            link(dve.tensor_scalar(gates[:, :, :], gates[:, :, :], 0.5, 0.5, ALU.mult, ALU.add))

            def split_weight(n):
                dve.wait_ge(s_wraw[n % 2], 16 * (n // 2 + 1))
                link(dve.tensor_copy(whi[:, n, :], wraw[:, n % 2, :]))
                dve.tensor_tensor(wlo[:, n, :], wraw[:, n % 2, :], whi[:, n, :].bitcast(F32),
                                  ALU.subtract).then_inc(s_wsplit, 1)

            for n in range(NW):
                split_weight(n)
            def take_heads(G):
                if G >= 2:
                    dve.wait_ge(s_ht[G % 2], 16 * GH * NB * (G // 2))
                dve.wait_ge(s_pair, 2 + NT * (G + 1))
                dve.tensor_copy(hout[:, G % 2, :], ps[:, 6 + (G % 2 if G < NG else 0), :]).then_inc(s_head, 1)
                if G + 2 < NHF * NG:
                    stage_v(G + 2)

            def add_x1(c):
                for b in range(NB):
                    m = c * NB + b
                    dve.wait_ge(s_o1, m + 1)
                    xb = X[:, m * TPH:(m + 1) * TPH, :].rearrange("p a b -> p (a b)")
                    dve.tensor_tensor(xb, ps[:, OUT1[c][b], :], xb, ALU.add).then_inc(s_x1, 1)

            def x1_statistics(c):
                dve.wait_ge(s_x1, NB * (c + 1))
                m_, v_ = statistics(X, c)
                dve.tensor_scalar(powin[:, c, 0, :], v_, EPS, None, ALU.add)
                dve.tensor_scalar(powin[:, c, 1, :], v_, 1.0 + EPS, EPS * EPS, ALU.mult, ALU.add)\
                    .then_inc(s_powin, 1)

            def x1_norms(c):
                dve.wait_ge(s_pow, 4 + 2 * c)
                normalise(c, powout[:, c, 1, :], s_u)

            def normed_early(b):
                dve.wait_ge(s_uT, b + 1)
                dve.tensor_scalar(nT[:, toks(0, b)], ps[:, 7, :], lncol[:, 0:1], lncol[:, 1:2],
                                  ALU.mult, ALU.add).then_inc(s_nTe, 1)
                dve.wait_ge(s_nTe, b + 1)
                sl = toks(0, b)
                dve.tensor_tensor(SQ[:, sl], nT[:, sl], nT[:, sl], ALU.mult).then_inc(s_sqe, 1)

            full = [P, NT, NE]

            def wide(t):
                return t.unsqueeze(2).to_broadcast(full)

            def copy_rows(part, c, b):
                k = 2 * (2 * part + c) + b
                dve.wait_ge(s_rows, k + 1)
                dve.tensor_copy(rows_of(c)[:, b * HALF:(b + 1) * HALF],
                                ps[0:2 * GR, LOGITS_T[part][c][b], :]).then_inc(s_rowsc, 1)

            def gate_norm(part, c):
                dve.wait_ge(s_log, 2 * part + c + 1)
                L = ps[:, LOGITS[part][c], :].rearrange("p (i e) -> p i e", e=2 * GR)
                dve.tensor_scalar(g1[:, 2 * c, :], L[:, :, GR], 1e-24, None, ALU.max).then_inc(s_powin, 1)

            def gate_logits(part, c, npow):
                lg, gr, ex = gt[:, c, 0, :, :], gt[:, c, 1, :, :], gt[:, c, 2, :, :]
                L = ps[:, LOGITS[part][c], :].rearrange("p (i e) -> p i e", e=2 * GR)[:, :, part * NE:(part + 1) * NE]
                dve.wait_ge(s_pow, npow)
                link(dve.tensor_tensor(lg, L, wide(g1[:, 2 * c + 1, :]), ALU.mult))
                link(dve.tensor_tensor(lg, lg, gates[:, part:part + 1, :].to_broadcast(full), ALU.subtract))
                link(dve.tensor_scalar(gr, lg, 0.0, None, ALU.max))
                link(dve.tensor_reduce(g1[:, 4, :], gr, AX.X, ALU.max))
                dve.tensor_tensor(ex, gr, wide(g1[:, 4, :]), ALU.subtract).then_inc(s_gex, 1)
                others = lg.unsqueeze(2).to_broadcast([P, PT, NE, NE])
                own = lg.unsqueeze(3).to_broadcast([P, PT, NE, NE])
                dve.tensor_tensor(cmp_[:, 0], others, own, ALU.is_gt)
                link(dve.tensor_tensor(cmp_[:, 1], others, own, ALU.is_equal))

            def gate_ranks(c):
                lg, gr, ss = gt[:, c, 0, :, :], gt[:, c, 1, :, :], g1[:, 5, :]
                link(dve.tensor_tensor(cmp_[:, 1], cmp_[:, 1],
                                       before[:, :, :].unsqueeze(1).to_broadcast([P, PT, NE, NE]), ALU.mult))
                link(dve.tensor_tensor(cmp_[:, 0], cmp_[:, 0], cmp_[:, 1], ALU.add))
                link(dve.tensor_reduce(lg, cmp_[:, 0], AX.X, ALU.add))
                link(dve.tensor_scalar(ss, g1[:, 4, :], 0.0, None, ALU.is_le))
                link(dve.scalar_tensor_tensor(out=lg, in0=lg, scalar=2.0, in1=wide(ss), op0=ALU.is_lt, op1=ALU.mult))
                link(dve.scalar_tensor_tensor(out=lg, in0=gr, scalar=0.0, in1=lg, op0=ALU.is_gt, op1=ALU.max))

            def gate_weights(part, c):
                lg, ex, ss = gt[:, c, 0, :, :], gt[:, c, 2, :, :], g1[:, 5, :]
                dve.wait_ge(s_gexo, 2 * part + c + 1)
                om = gt[:, c, 1, :, :]
                link(dve.tensor_scalar(om, ex, -1.0, 1.0, ALU.mult, ALU.add))
                link(dve.reciprocal(om, om))
                link(dve.scalar_tensor_tensor(out=ex, in0=ex, scalar=1.0, in1=om, op0=ALU.add, op1=ALU.mult))
                link(dve.tensor_tensor(ex, ex, lg, ALU.mult))
                link(dve.tensor_reduce(ss, ex, AX.X, ALU.add))
                link(dve.reciprocal(ss, ss))
                r = rw[:, c, :, :]
                link(dve.tensor_tensor(r, ex, wide(ss), ALU.mult))
                rp = RP[:, c, :, :]
                link(dve.tensor_copy(rp[:, :, 0:NE], r))
                link(dve.tensor_tensor(lg, r, rp[:, :, 0:NE], ALU.subtract))
                link(dve.tensor_copy(rp[:, :, NE:2 * NE], lg))
                dve.tensor_tensor(rp[:, :, 2 * NE:3 * NE], lg, rp[:, :, NE:2 * NE], ALU.subtract).then_inc(s_rp, 1)

            def rpt_copy(n, c):
                dve.wait_ge(s_rpT, n)
                dve.tensor_copy(RPT[0:3 * NE, c, :], ps[0:3 * NE, RW_TURNED[n - 1], :].bitcast(BF16))\
                    .then_inc(s_rpt, 1)

            for G in range(NG):
                take_heads(G)
            batch_sums()
            add_rows()
            add_x1(0)
            take_heads(4)
            x1_statistics(0)
            x1_norms(0)
            for b in range(NB):
                normed_early(b)
            take_heads(5)
            for b in range(NB):
                copy_rows(0, 0, b)
            gate_norm(0, 0)
            take_heads(6)
            gate_logits(0, 0, 5)
            gate_ranks(0)
            gate_weights(0, 0)
            dve.wait_ge(s_rptz, 1)
            rpt_copy(1, 0)

            def maxima(T):
                i = place(T)[1]
                col = score_bank(T) * 512
                dve.wait_ge(s_S, T + 1)
                link(dve.tensor_reduce(mx[:, 0, T:T + 1], psf[:, col:col + (i + 1) * P], AX.X, ALU.max))
                dve.tensor_scalar(mx[:, 1, T:T + 1], mx[:, 0, T:T + 1], -SMAX_SCALE, None,
                                  ALU.mult).then_inc(s_nb, 1)

            def attn_low(q):
                dve.wait_ge(s_ahi, q + 1)
                sl = slice(q * HALF, (q + 1) * HALF)
                dve.tensor_tensor(alo[:, sl], ps[:, HEADS, :], ahi[:, sl].bitcast(F32),
                                  ALU.subtract).then_inc(s_alo, 1)

            def take_v(m):
                dve.wait_ge(s_mm, (m + 1) * NE)
                if m >= 2:
                    dve.wait_ge(s_vtr, m - 1)
                dve.tensor_copy(vT[:, m % 2, :], ps[:, 2, :]).then_inc(s_vT, 1)

            for r, (kind, m, e) in enumerate(ring_jobs):
                if kind == "v":
                    dve.wait_ge(s_vtr, m + 1)
                    dve.tensor_copy(V[:, m * TPH:(m + 1) * TPH, :].rearrange("p a b -> p (a b)"),
                                    ps[:, ring_bank(r), :]).then_inc(s_v, 1)
                    continue
                n = m * NE + e
                c, b = divmod(m, NB)
                dve.wait_ge(s_bc, n + 1)
                if n >= 3:
                    dve.wait_ge(s_slo, n - 2)
                dve.tensor_tensor(sring[:, n % 3, :], ps[:, ring_bank(r), :], nT[:, toks(c, b)],
                                  ALU.mult).then_inc(s_s, 1)
                if n == 0:
                    take_heads(7)
                if e == 1 and m:
                    take_v(m - 1)
                if n == CH["x1"]:
                    add_x1(1)
                if n == CH["stats"]:
                    x1_statistics(1)
                if n == CH["norms"]:
                    x1_norms(1)
                if n == CH["copy"]:
                    for k in range(NB):
                        copy_rows(0, 1, k)
                if n == CH["norm"]:
                    gate_norm(0, 1)
                if n == CH["logits"]:
                    gate_logits(0, 1, 7)
                if n == CH["ranks"]:
                    gate_ranks(1)
                if n == CH["weights"]:
                    gate_weights(0, 1)
                if n == CH["rpt"]:
                    rpt_copy(2, 1)
                for T in range(T_IN):
                    if n == ATT[T] + 2:
                        maxima(T)
                if n == ATT[3] + 7:
                    attn_low(0)
            m = NB * NHF - 1
            take_v(m)
            dve.wait_ge(s_vtr, m + 1)
            dve.tensor_copy(V[:, m * TPH:(m + 1) * TPH, :].rearrange("p a b -> p (a b)"), ps[:, 2, :]).then_inc(s_v, 1)

            def gates_over_rowsum(c):
                dve.wait_ge(s_exp, (c + 1) * PT)
                own = rowsum[:, c * PT:(c + 1) * PT]
                link(dve.reciprocal(own, own))
                dve.tensor_tensor(rwn[:, c], rw[:, c], own.unsqueeze(2).to_broadcast([P, PT, NE]),
                                  ALU.mult).then_inc(s_rwn, 1)
                dve.wait_ge(s_rwn, c + 1)

            def add_experts(T):
                dve.wait_ge(s_op, T + 2)
                for e in range(NE // 2):
                    for t in (T, T + 1):
                        if e:
                            dve.wait_ge(s_dve, steps[0] - (0 if t > T and e == NE // 2 - 1 else 1))
                        c, i = divmod(t, PT)
                        ins = dve.scalar_tensor_tensor(out=HS[:, t, :], in0=ps[:, op_bank(t, 0), e * P:(e + 1) * P],
                                                       scalar=rwn[:, c, i, e:e + 1], in1=HS[:, t, :],
                                                       op0=ALU.mult, op1=ALU.add)
                        if e < NE // 2 - 1:
                            ins.then_inc(s_dve, 1)
                            steps[0] += 1
                        else:
                            ins.then_inc(s_acc, 1)

            def second_statistics(c):
                dve.wait_ge(s_added, (c + 1) * PT)
                m_, v_ = statistics(HS, c)
                dve.tensor_scalar(powin[:, c, 0, :], v_, EPS, None, ALU.add).then_inc(s_powin, 1)

            def second_norm(c, npow):
                dve.wait_ge(s_pow, npow)
                for i in range(PT):
                    last = dve.tensor_scalar(U[:, c * PT + i, :], HS[:, c * PT + i, :], mv[:, c * PT + i, 0:1],
                                             powout[:, c, 0, i:i + 1], ALU.subtract, ALU.mult)
                last.then_inc(s_u, 1)

            dve.wait_ge(s_hs, NB * NT)
            for T in range(T_IN, NB * NT):
                maxima(T)
                if T == 8:
                    gates_over_rowsum(0)
                if T == 13:
                    second_norm(0, 8)
                if T in (PT + 1, PT + 6):
                    attn_low(1 if T == PT + 1 else 2)
                for t in OPROJ_AT.get(T - 1, ()):
                    add_experts(t)
                if T == 12:
                    second_statistics(0)
                if T == 15:
                    for b in range(NB):
                        copy_rows(1, 0, b)
            gate_norm(1, 0)
            attn_low(3)
            gates_over_rowsum(1)
            gate_logits(1, 0, 9)
            add_experts(8)
            gate_ranks(0)
            add_experts(10)
            gate_weights(1, 0)
            add_experts(12)
            rpt_copy(3, 0)

            def moe_end(m):
                dve.wait_ge(s_mm, NS + (m + 1) * NE)
                dve.tensor_copy(moeT[:, m % 2, :], ps[:, MOE_SUM[m], :]).then_inc(s_moe, 1)

            def moe_out(m):
                dve.wait_ge(s_mtr, m + 1)
                dve.wait_ge(s_xh, m // NHF + 1)
                dve.tensor_tensor(fin[:, m * TPH:(m + 1) * TPH, :].rearrange("p a b -> p (a b)"), ps[:, 7, :],
                                  X[:, m * TPH:(m + 1) * TPH, :].rearrange("p a b -> p (a b)"),
                                  ALU.add).then_inc(s_fin, 1)

            for n in range(NS):
                m, e = divmod(n, NE)
                dve.wait_ge(s_bc, NS + n + 1)
                dve.wait_ge(s_gel, n + 1)
                if n >= 3:
                    dve.wait_ge(s_slo, NS + n - 2)
                dve.tensor_tensor(sring[:, (NS + n) % 3, :], ps[:, 2 + n % 2, :], gel[:, n % 2, :],
                                  ALU.mult).then_inc(s_s, 1)
                if n == 0:
                    add_experts(14)
                if n == MH["stats"]:
                    second_statistics(1)
                if n == MH["norms"]:
                    second_norm(1, 10)
                if n == MH["copy"]:
                    for k in range(NB):
                        copy_rows(1, 1, k)
                if n == MH["norm"]:
                    gate_norm(1, 1)
                    dve.wait_ge(s_n2hi, 2)
                    sl = slice(S, 2 * S)
                    dve.tensor_tensor(alo[:, sl], nT[:, sl], ahi[:, sl].bitcast(F32), ALU.subtract).then_inc(s_n2lo, 1)
                if n == MH["logits"]:
                    gate_logits(1, 1, 11)
                if n == MH["ranks"]:
                    gate_ranks(1)
                if n == MH["weights"]:
                    gate_weights(1, 1)
                if n == MH["rpt"]:
                    rpt_copy(4, 1)
                if e == LAG and m:
                    moe_end(m - 1)
                if n in MOE_OUT:
                    moe_out(MOE_OUT.index(n))
            moe_end(NB * NHF - 1)
            moe_out(NB * NHF - 1)

        @block.tensor
        def _(pe):
            def three_pass(o, wh, wl, xh, xl, start, stop):
                pe.matmul(o, wh, xh, start=start, stop=False)
                pe.matmul(o, wl, xh, start=False, stop=False)
                return pe.matmul(o, wh, xl, start=False, stop=stop)

            pe.wait_ge(s_id, 1)
            for n, (what, b, h, e) in enumerate(JOBS):
                if n >= 8:
                    eng, cnt = emptied(n - 8)
                    pe.wait_ge(s_jact if eng == "act" else s_jdve, cnt)
                bank = ps[:, n % 8, :]
                if what == "wT":
                    pe.wait_ge(s_wnat, 64)
                    for k in range(4):
                        last = pe.transpose(bank[:, k * P:(k + 1) * P], wnat[:, k, :], ident[:, :])
                elif what == "xT":
                    pe.wait_ge(s_xn, 2 * b + h + 1)
                    for k in range(TPH):
                        last = pe.transpose(bank[:, k * P:(k + 1) * P], U[:, b * NT + h * TPH + k, :], ident[:, :])
                elif what in "qk":
                    eng, cnt = emptied(JOB[("xT", b, h)])
                    pe.wait_ge(s_jact if eng == "act" else s_jdve, cnt)
                    last = pe.matmul(bank, wT[:, "qk".index(what), :], nT[:, toks(b, h)], start=True, stop=True)
                elif what == "v":
                    for k in range(TPH):
                        t0 = (b * NB + h) * HALF + k * P
                        last = pe.matmul(bank[:, k * P:(k + 1) * P], nT[:, t0:t0 + P], wT[:, 2, :],
                                         start=True, stop=True)
                last.then_inc(s_job, 1)
            pe.wait_ge(s_jact, sum(1 for j in JOBS if j[3] == "act"))
            pe.wait_ge(s_jdve, sum(1 for j in JOBS if j[3] == "dve"))

            def scores(i, slot, kc, pair):
                for j in range(2):
                    h = 2 * pair + j
                    col = (i % 3) * 1024 + j * 512
                    last = pe.matmul(psf[:, col:col + 512], ops_k[:, slot, h, kc * P:(kc + 1) * P],
                                     ops_q[:, slot, h, :], start=True, stop=True)
                last.then_inc(s_score, 1)

            def heads(k, slot, bank):
                kc = k % NT
                for j in range(GH):
                    last = pe.matmul(ps[32 * j:32 * j + 32, bank, :], vst[:, slot, kc, j, :],
                                     tanhs[:, (2 * k + j // 2) % 4, j % 2, :], start=(kc == 0), stop=(kc == NT - 1))
                last.then_inc(s_pair, 1)

            with pe.Fori(0, NG // 2) as gg:
                def loop_heads(k):
                    u = k // NT
                    if k % NT == 0:
                        pe.wait_ge(s_head, 2 * gg + (u + 1))
                    pe.wait_ge(s_tanh, 32 * gg + (3 + 2 * k + 2))
                    heads(k, u, 6 + u)

                for k in range(2 * NT):
                    u = k // NT
                    if k % NT == 0:
                        pe.wait_ge(s_ops[u], 16 * OP_DMAS * gg + 16 * OP_DMAS)
                    for i in (2 * k, 2 * k + 1):
                        if i == 0:
                            pe.wait_ge(s_tanh, 32 * gg + 3)
                        elif i >= 3:
                            pe.wait_ge(s_tanh, 32 * gg + (i + 1))
                        scores(i, u, k % NT, i % 2)
                    if k % NT == 1:
                        pe.wait_ge(s_vst, 2 * gg + (u + 1))
                    if k:
                        loop_heads(k - 1)
                loop_heads(2 * NT - 1)

            def out_one(c, b):
                for i in range(TPH):
                    t0 = (c * NB + b) * HALF + i * P
                    last = pe.matmul(ps[:, OUT1[c][b], i * P:(i + 1) * P], HT[:, t0:t0 + P], wT[:, 3, :],
                                     start=True, stop=True)
                last.then_inc(s_o1, 1)

            def turn_u(part, c, b):
                pe.wait_ge(s_u, 2 * part + c + 1)
                for i in range(TPH):
                    last = pe.transpose(ps[:, TURNED[part][c][b], i * P:(i + 1) * P],
                                        U[:, c * PT + b * TPH + i, :], ident[:, :])
                last.then_inc(s_uT, 1)

            def logit_rows(part, c, b):
                bank = LOGITS_T[part][c][b]
                pe.matmul(ps[0:GR, bank, :], sims[:, :, :].rearrange("p a b -> p (a b)"), nT[:, toks(c, b)],
                          start=True, stop=True)
                pe.matmul(ps[GR:2 * GR, bank, :], ones[:, 0:GR], SQ[:, b * HALF:(b + 1) * HALF],
                          start=True, stop=True).then_inc(s_rows, 1)

            def logits(part, c):
                pe.wait_ge(s_rowsc, 2 * (2 * part + c) + 2)
                for i in range(PT):
                    last = pe.transpose(ps[:, LOGITS[part][c], i * 2 * GR:(i + 1) * 2 * GR],
                                        rows_of(c)[:, i * P:(i + 1) * P], ident[0:2 * GR, 0:2 * GR])
                last.then_inc(s_log, 1)

            def turn_rw(n, c):
                pe.wait_ge(s_rp, n)
                for i in range(PT):
                    last = pe.transpose(ps[0:3 * NE, RW_TURNED[n - 1], :].bitcast(BF16)[:, i * P:(i + 1) * P],
                                        RP[:, c, i, :], identb[:, :])
                last.then_inc(s_rpT, 1)

            def late_heads(k):
                if k == 0:
                    pe.wait_ge(s_head, 2 + NG - 1)
                elif k % NT == 0:
                    pe.wait_ge(s_head, 2 + NG + k // NT)
                pe.wait_ge(s_tanh, 64 + 3 + 2 * k + 2)
                heads(k, k // NT % 2, 6)

            for k in range(NG * NT):
                G = NG + k // NT
                if k % NT == 0:
                    pe.wait_ge(s_ops[G % 2], 16 * OP_DMAS * (G // 2 + 1))
                for i in (2 * k, 2 * k + 1):
                    if i == 0:
                        pe.wait_ge(s_tanh, 64 + 3)
                    elif i >= 3:
                        pe.wait_ge(s_tanh, 64 + i + 1)
                    scores(i, G % 2, k % NT, i % 2)
                if k % NT == 1:
                    pe.wait_ge(s_vst, G + 1)
                if k:
                    late_heads(k - 1)
                if k == AH["sums"]:
                    pe.wait_ge(s_head, 2 + NG)
                    pe.wait_ge(s_sums, 2)
                    pe.wait_ge(s_const, 2)
                    pe.matmul(ps[:, 7, 0:2 * NE], ones[:, :], simsq[:, :], start=True, stop=True)
                    pe.matmul(ps[:, 7, 2 * NE:2 * NE + NB], wT[:, 2, :], sumx[:, :],
                              start=True, stop=True).then_inc(s_sumd, 1)
                if k == AH["add"]:
                    pe.wait_ge(s_cvec, 1)
                    for b in range(NB):
                        last = pe.matmul(ps[:, 7, b * P:(b + 1) * P], cvecb[:, b, :], wT[:, 3, :],
                                         start=True, stop=True)
                    last.then_inc(s_addrow, 1)
                if k == AH["out"][0]:
                    pe.wait_ge(s_rowadd, 1)
                    for u in range(2):
                        pe.wait_ge(s_ht[u], 16 * GH * NB * 2)
                    out_one(0, 0)
                if k == AH["out"][1]:
                    pe.wait_ge(s_x1, 1)
                    out_one(0, 1)
                if k == AH["turn"][0]:
                    turn_u(0, 0, 0)
                if k == AH["turn"][1]:
                    pe.wait_ge(s_nTe, 1)
                    turn_u(0, 0, 1)
                if k == AH["rows"][0]:
                    pe.wait_ge(s_simz, 1)
                    pe.wait_ge(s_nTe, 2)
                    pe.wait_ge(s_sqe, 2)
                    logit_rows(0, 0, 0)
                if k == AH["rows"][1]:
                    pe.wait_ge(s_rowsc, 1)
                    logit_rows(0, 0, 1)
                if k == AH["tokens"]:
                    logits(0, 0)
                if k == AH["rw"]:
                    pe.wait_ge(s_const, 8)
                    turn_rw(1, 0)
                if k == NG * NT - 1:
                    pe.wait_ge(s_rpt, 1)
                    pe.matmul(ps[:, ring_bank(0), :], spread[:, 0, :], RPT[:, 0, 0:HALF],
                              start=True, stop=True).then_inc(s_bc, 1)
            late_heads(NG * NT - 1)
            pe.wait_ge(s_tanh, SCORES)

            def broadcast(n, c, b, e, bank):
                last = pe.matmul(ps[:, bank, :], spread[:, e, :], RPT[:, c, b * HALF:(b + 1) * HALF],
                                 start=True, stop=True)
                last.then_inc(s_bc, 1)

            def qk(T):
                b, i = place(T)
                pe.wait_ge(s_qk, 2 * (T // 4 + 1))
                if T in (2, 3, 4, 5, 6, 7):
                    pe.wait_ge(s_pt, pt_until(T - 2))
                elif T == PT:
                    pe.wait_ge(s_pt, pt_until(T - 1))
                elif T == PT + 1:
                    pe.wait_ge(s_s, NS)
                elif T > PT:
                    pe.wait_ge(s_pt, pt_until(T - 2))
                base, nk = score_bank(T) * 512, (i + 1) * P
                for k0 in range(0, nk, HALF):
                    w = min(HALF, nk - k0)
                    pe.matmul(psf[:, base + k0:base + k0 + w], qT[:, T // TPH, T % TPH * P:(T % TPH + 1) * P],
                              kT[:, k0 // HALF * NB + b, 0:w],
                              start=True, stop=True)
                pe.matmul(psf[:, base + nk - P:base + nk], identb[:, :], maskb[:, :], start=False, stop=True,
                          skip_group_check=True).then_inc(s_S, 1)

            def turn_prob(T):
                pe.wait_ge(s_exp, T + 1)
                for n, (T_, k0, nk) in enumerate(ptjobs):
                    if T_ != T:
                        continue
                    for k in range(nk):
                        last = pe.transpose(ps[:, score_bank(T) + k0 // 4, k * P:(k + 1) * P],
                                            prob[:, T % 2, (k0 + k) * P:(k0 + k + 1) * P], ident[:, :])
                    last.then_inc(s_ptm, 1)

            def attend(T, half=None):
                b, i = place(T)
                if half != 1:
                    pe.wait_ge(s_pt, pt_until(T))
                    pe.wait_ge(s_v, T // 4 + 1)
                    if T == 1:
                        pe.wait_ge(s_rpt, 2)
                    elif T % 4 == 1:
                        pe.wait_ge(s_alo, T // 4)
                col = (T % 4) * P
                mid = i // 2 + 1
                for j in {None: range(i), 0: range(mid), 1: range(mid, i)}[half]:
                    pe.matmul(ps[:, HEADS, col - P:col + P], V[:, tile_of(b, j), :],
                              probT[:, T // 2 % 2, j, :, :].rearrange("p a b -> p (a b)"),
                              start=(j == 0), stop=(j == i - 1))
                if half != 0:
                    pe.matmul(ps[:, HEADS, col:col + P], V[:, tile_of(b, i), :], probT[:, T // 2 % 2, i, 1, :],
                              start=False, stop=True, skip_group_check=True).then_inc(s_av, 1)

            pe.wait_ge(s_wsplit, NW)

            def turn_v(m, bank):
                pe.wait_ge(s_vT, m + 1)
                for k in range(TPH):
                    last = pe.transpose(ps[:, bank, k * P:(k + 1) * P], vT[:, m % 2, k * P:(k + 1) * P],
                                        ident[:, :])
                last.then_inc(s_vtr, 1)

            def ring_job(r):
                kind, m, e = ring_jobs[r]
                if r >= 2:
                    k, m2, e2 = ring_jobs[r - 2]
                    if k == "bc":
                        pe.wait_ge(s_s, m2 * NE + e2 + 1)
                    else:
                        pe.wait_ge(s_v, m2 + 1)
                if kind == "bc":
                    c, b = divmod(m, NB)
                    broadcast(m * NE + e, c, b, e, ring_bank(r))
                else:
                    turn_v(m, ring_bank(r))

            issued = 1
            for n in range(NS):
                m, e = divmod(n, NE)
                ahead = min(n + 2, NS // 2 - 1 if n < NS // 2 else NS - 1)
                while issued <= RING[("bc", *divmod(ahead, NE))]:
                    if ring_jobs[issued] == ("bc", NHF, 0):
                        pe.wait_ge(s_rpt, 2)
                    ring_job(issued)
                    issued += 1
                pe.wait_ge(s_slo, n + 1)
                for k, w in enumerate((WQ, WK, WV)):
                    if e == 0 and m:
                        if k < 2:
                            pe.wait_ge(s_qk, 2 * (m - 1) + k + 1)
                        else:
                            pe.wait_ge(s_vT, m)
                    sl = slice(e * C, (e + 1) * C)
                    last = three_pass(ps[:, k, :], whi[:, w, sl], wlo[:, w, sl],
                                      shi[:, n % 3, :], slo[:, n % 3, :], e == 0, e == NE - 1)
                    if e == NE - 1 and k < 2:
                        last.then_inc(s_qksum, 1)
                last.then_inc(s_mm, 1)
                if n == CH["out"]:
                    pe.wait_ge(s_head, 2 + NHF * NG)
                    for u in range(2):
                        pe.wait_ge(s_ht[u], 16 * GH * NB * NG)
                    for k in range(NB):
                        out_one(1, k)
                if n == CH["turn"]:
                    for k in range(NB):
                        turn_u(0, 1, k)
                if n == CH["rows"]:
                    pe.wait_ge(s_sq, 1)
                    for k in range(NB):
                        logit_rows(0, 1, k)
                if n == CH["tokens"]:
                    logits(0, 1)
                if n == CH["rw"]:
                    turn_rw(2, 1)
                for T in range(T_IN):
                    if n == ATT[T] + 4 and T % 2:
                        attend(T)
                    if n == ATT[T] + 2:
                        turn_prob(T)
                    if n == ATT[T]:
                        if T == 0:
                            pe.wait_ge(s_rowsc, 4)
                        qk(T)
            turn_v(NB * NHF - 1, 2)

            def oproj(T, last=None):
                jobs = {None: ((0, T), (0, T + 1), (1, T), (1, T + 1)), 0: ((0, T), (0, T + 1), (1, T)),
                        1: ((1, T + 1),)}[last]
                if T == 0:
                    pe.wait_ge(s_v, NB * NHF)
                    pe.wait_ge(s_qk, 2 * NB * NHF)
                if T == PT:
                    pe.wait_ge(s_pt, len(ptjobs))
                    pe.wait_ge(s_alo, NB * NHF)
                pe.wait_ge(s_alo, T // 4 + 1)
                for k, t in jobs:
                    if k == 0 and t % PT >= 2:
                        pe.wait_ge(s_acc, t - 1)
                    if k == 1 and t < PT and t:
                        pe.wait_ge(s_esc, t)
                    if k == 1 and t >= PT + 2:
                        pe.wait_ge(s_esc, t - 1)
                    t0 = t * P
                    sl = slice(k * 512, (k + 1) * 512)
                    o = ps[:, op_bank(t, k), :]
                    pe.matmul(o, ahi[:, t0:t0 + P], whi[:, WO, sl], start=True, stop=False)
                    pe.matmul(o, ahi[:, t0:t0 + P], wlo[:, WO, sl], start=False, stop=False)
                    pe.matmul(o, alo[:, t0:t0 + P], whi[:, WO, sl], start=False, stop=True)\
                        .then_inc(s_op if k == 0 else s_op2, 1)

            qk(T_IN)
            for T in range(T_IN, NB * NT):
                if T + 1 < NB * NT:
                    qk(T + 1)
                if T == 13:
                    pe.wait_ge(s_acc, PT)
                    pe.wait_ge(s_esc, PT)
                    for b in range(NB):
                        turn_u(1, 0, b)
                if T == 14:
                    pe.wait_ge(s_sq, 2)
                    for b in range(NB):
                        logit_rows(1, 0, b)
                for t in OPROJ_AT.get(T - 1, ())[-1:]:
                    oproj(t, 1)
                if T > PT + 1:
                    attend(T - 1 - T % 2, T % 2)
                turn_prob(T)
                for t in OPROJ_AT.get(T, ()):
                    oproj(t, 0 if t == OPROJ_AT[T][-1] else None)
            logits(1, 0)
            attend(NB * NT - 1)
            oproj(8)
            oproj(10)
            oproj(12)
            turn_rw(3, 0)
            oproj(14)

            def first_layer(n):
                m, e = divmod(n, NE)
                c, b = divmod(m, NB)
                if n >= 2:
                    pe.wait_ge(s_gel, n - 1)
                if e == 0:
                    pe.wait_ge(s_n2lo, c + 1)
                sl = slice(e * C, (e + 1) * C)
                three_pass(ps[:, n % 2, :], whi[:, W1, sl], wlo[:, W1, sl], ahi[:, toks(c, b)],
                           alo[:, toks(c, b)], True, True).then_inc(s_int, 1)

            def gate(n):
                m, e = divmod(n, NE)
                c, b = divmod(m, NB)
                if n % (NHF * NE) == 0:
                    pe.wait_ge(s_rpt, 3 + c)
                if n >= 2:
                    pe.wait_ge(s_s, NS + n - 1)
                broadcast(NS + n, c, b, e, 2 + n % 2)

            def second_layer(n):
                m, e = divmod(n, NE)
                pe.wait_ge(s_slo, NS + n + 1)
                if n == 0:
                    pe.wait_ge(s_esc, NB * NT)
                if e == 0 and m:
                    pe.wait_ge(s_moe, 1 if m == 1 else m - 1)
                k = (NS + n) % 3
                sl = slice(e * C, (e + 1) * C)
                three_pass(ps[:, MOE_SUM[m], :], whi[:, W2, sl], wlo[:, W2, sl], shi[:, k, :], slo[:, k, :],
                           e == 0, e == NE - 1).then_inc(s_mm, 1)

            def turn_moe(m):
                pe.wait_ge(s_moe, m + 1)
                if m:
                    pe.wait_ge(s_fin, m)
                for k in range(TPH):
                    last = pe.transpose(ps[:, 7, k * P:(k + 1) * P], moeT[:, m % 2, k * P:(k + 1) * P],
                                        ident[:, :])
                last.then_inc(s_mtr, 1)

            for n in range(NS + LAG):
                if n < NS:
                    first_layer(n)
                    gate(n)
                if n >= LAG:
                    second_layer(n - LAG)
                if n + 1 in MOE_OUT:
                    turn_moe(MOE_OUT.index(n + 1))
                if n == MH["turn"]:
                    for k in range(NB):
                        turn_u(1, 1, k)
                if n == MH["rows"]:
                    pe.wait_ge(s_sq, 3)
                    for k in range(NB):
                        logit_rows(1, 1, k)
                if n == MH["tokens"]:
                    logits(1, 1)
                if n == MH["rw"]:
                    turn_rw(4, 1)
            turn_moe(NB * NHF - 1)


_INS = ['L0_attn_x', 'L0_attn_Wq', 'L0_attn_bq', 'L0_attn_Wk', 'L0_attn_bk', 'L0_attn_Wv', 'L0_attn_bv',
        'L0_attn_Wo', 'L0_attn_bo', 'L0_ffn_ln1_w', 'L0_ffn_ln1_b', 'L0_ffn_ln2_w', 'L0_ffn_ln2_b',
        'L0_ffn_smha_sim', 'L0_ffn_smha_gates', 'L0_ffn_q_proj', 'L0_ffn_k_proj', 'L0_ffn_v_proj',
        'L0_ffn_o_proj', 'L0_ffn_moe_sim', 'L0_ffn_moe_gates', 'L0_ffn_w1', 'L0_ffn_w2']
_OUTS = [((2, 1024, 128), 'float32')]


def kernel(**inputs):
    import numpy as _np
    import concourse.bacc as _bacc
    from concourse import mybir as _mybir
    from concourse.bass_utils import run_bass_kernel_spmd as _run

    nc = _bacc.Bacc("TRN2", target_bir_lowering=False, num_devices=1)
    arrays, args = {}, []
    for name in _INS:
        a = _np.ascontiguousarray(inputs[name])
        arrays[f"in_{name}_dram"] = a
        args.append(nc.dram_tensor(f"in_{name}_dram", a.shape, _mybir.dt.from_np(a.dtype), kind="ExternalInput").ap())
    for i, (shape, dtype) in enumerate(_OUTS):
        dt = _mybir.dt.from_np(_np.dtype(dtype))
        args.append(nc.dram_tensor(f"out_{i}_dram", shape, dt, kind="ExternalOutput").ap())
    preln_layer(nc, *args)
    r = _run(nc, [arrays], core_ids=[0])
    got = tuple(r.results[0][f"out_{i}_dram"] for i in range(len(_OUTS)))
    return got[0]
```
